# Optimizing a Trainium2 kernel written in Bass

```python
import numpy as np
import jax
import jax.numpy as jnp

def _softmax(x, axis=-1):
    return jax.nn.softmax(x, axis=axis)

def _gelu(x):
    return jax.nn.gelu(x, approximate=True)

def _silu(x):
    return jax.nn.silu(x)

def _sigmoid(x):
    return jax.nn.sigmoid(x)

def _layernorm(x, axis=-1, eps=1e-05):
    m = jnp.mean(x, axis=axis, keepdims=True)
    v = jnp.var(x, axis=axis, keepdims=True)
    return (x - m) / jnp.sqrt(v + eps)

def _scatter_add(tgt, idx, src, axis=0):
    return tgt.at[idx].add(src)

def _segment_sum(src, seg, n):
    return jax.ops.segment_sum(src, seg, n)
kernel_name = 'mk_decoder_postln_d4_seqx_r8_72ef2d'

def setup_inputs(seed: int=0):
    np.random.seed(seed)
    _w = jnp.asarray

    def _rec_inputs():
        import jax
        import jax.numpy as jnp
        _rk = jax.random.key(seed)
        x = 7.22e-05 + 1 * jax.random.normal(jax.random.fold_in(_rk, 1), (4, 512, 128), jnp.float32)
        _lenS = 512 - jax.random.randint(jax.random.fold_in(_rk, 7), (4,), 0, max(1, 512 // 4) + 1, jnp.int32)
        _lenS2 = 154 - jax.random.randint(jax.random.fold_in(_rk, 8), (4,), 0, max(1, 154 // 4) + 1, jnp.int32)
        _ctx_1024P = jax.random.normal(jax.random.fold_in(_rk, 11), (4, 16, 128), jnp.float32)
        _ctx_1024c = jax.random.dirichlet(jax.random.fold_in(_rk, 511), 0.3 * jnp.ones((16,), jnp.float32), (4, 154))
        _ctx_1024t = jnp.einsum('bsk,bkd->bsd', _ctx_1024c, _ctx_1024P)
        _ctx_1024t = _ctx_1024t * jax.lax.rsqrt(jnp.mean(jnp.square(_ctx_1024t)) + 1e-12) * 0.953939
        ctx_1024 = 4.13588e-05 + 0.999923 * (_ctx_1024t + 0.3 * jax.random.normal(jax.random.fold_in(_rk, 611), (4, 154, 128), jnp.float32))
        _validS = jnp.arange(512)[None, :] < _lenS[:, None]
        _validS2 = jnp.arange(154)[None, :] < _lenS2[:, None]
        _causal = jnp.tril(jnp.ones((512, 512), dtype=bool))
        mask_BxS_bf1 = jnp.ones((4, 512), dtype=bool)
        mask_BxS2_if1 = jnp.where(jnp.ones((4, 154), dtype=bool), 1, 0).astype(jnp.int32)
        return (x, ctx_1024, mask_BxS_bf1, mask_BxS2_if1)
    x, ctx_1024, mask_BxS_bf1, mask_BxS2_if1 = _rec_inputs()

    def _L0_attn_setup():
        import jax, jax.numpy as jnp
        import numpy as np
        B, N, D = (4, 512, 128)
        H, F = (16, 32)
        HD = D // H
        EPS_ATTN = 1e-08
        EPS_LN = 1e-05

        def _layernorm(x, gamma, beta):
            mu = jnp.mean(x, axis=-1, keepdims=True)
            var = jnp.var(x, axis=-1, keepdims=True)
            return (x - mu) * jax.lax.rsqrt(var + EPS_LN) * gamma + beta
        key = jax.random.key(seed)
        ks = jax.random.split(key, 10)

        def kaiming(k, shape):
            fan_in = shape[1]
            return jax.random.normal(k, shape, jnp.float32) * jnp.sqrt(2.0 / fan_in)
        pm = jax.random.normal(ks[0], (H, HD, F), jnp.float32)
        return {'x': jax.random.normal(ks[1], (B, N, D), jnp.float32), 'proj': pm, 'w_qkv': kaiming(ks[2], (3 * D, D)), 'w_out': kaiming(ks[3], (D, D)), 'b_out': jnp.zeros((D,), jnp.float32), 'gamma': jnp.ones((D,), jnp.float32), 'beta': jnp.zeros((D,), jnp.float32), 'w1': kaiming(ks[4], (4 * D, D)), 'b1': jnp.zeros((4 * D,), jnp.float32), 'w2': kaiming(ks[5], (D, 4 * D)), 'b2': jnp.zeros((D,), jnp.float32)}
    _L0_attn_all = _L0_attn_setup()
    _L0_attn_in = {k: v for k, v in _L0_attn_all.items() if k in ('proj', 'w_qkv', 'w_out', 'b_out', 'gamma', 'beta', 'w1', 'b1', 'w2', 'b2')}
    del _L0_attn_all

    def _L0_xattn_setup():
        import jax, jax.numpy as jnp
        import numpy as np
        import math
        D = 128
        H = 16
        B = 4
        S = 256

        def _split_heads(x):
            b, s, d = x.shape
            return x.reshape(b, s, H, d // H).transpose(0, 2, 1, 3)
        key = jax.random.key(seed)
        ks = jax.random.split(key, 11)
        s = 1.0 / math.sqrt(D)
        inp = {'queries': jax.random.normal(ks[0], (B, S, D), jnp.float32), 'keys': jax.random.normal(ks[1], (B, S, D), jnp.float32), 'values': jax.random.normal(ks[2], (B, S, D), jnp.float32), 'Wq': jax.random.normal(ks[3], (D, D), jnp.float32) * s, 'bq': jnp.zeros((D,), jnp.float32), 'Wk': jax.random.normal(ks[4], (D, D), jnp.float32) * s, 'bk': jnp.zeros((D,), jnp.float32), 'Wv': jax.random.normal(ks[5], (D, D), jnp.float32) * s, 'bv': jnp.zeros((D,), jnp.float32), 'Wo': jax.random.normal(ks[6], (D, D), jnp.float32) * s, 'bo': jnp.zeros((D,), jnp.float32)}
        return inp
    _L0_xattn_all = _L0_xattn_setup()
    _L0_xattn_in = {k: v for k, v in _L0_xattn_all.items() if k in ('Wq', 'bq', 'Wk', 'bk', 'Wv', 'bv', 'Wo', 'bo')}
    del _L0_xattn_all

    def _L0_ffn_setup():
        import jax, jax.numpy as jnp
        import numpy as np
        B, T, DIM = (4, 128, 128)
        H, E, DH, K = (8, 5, 64, 3)

        def _topk_mask(s, k):
            idx = jax.lax.top_k(s, k)[1]
            return jnp.sum(jax.nn.one_hot(idx, s.shape[-1], dtype=s.dtype), axis=-2)
        key = jax.random.key(seed)
        ks = jax.random.split(key, 6)
        w = lambda k, shape: jax.random.normal(k, shape, jnp.float32) * 0.02
        return {'x': jax.random.normal(ks[0], (B, T, DIM), jnp.float32), 'Wq': w(ks[1], (DIM, H * E * DH)), 'Wkv': w(ks[2], (DIM, 2 * H * E * DH)), 'Ws': w(ks[3], (DIM, H * E)), 'Wd': w(ks[4], (DIM, H * E)), 'Wo': w(ks[5], (DH, E * DIM))}
    _L0_ffn_all = _L0_ffn_setup()
    _L0_ffn_in = {k: v for k, v in _L0_ffn_all.items() if k in ('Wq', 'Wkv', 'Ws', 'Wd', 'Wo')}
    del _L0_ffn_all

    def _L1_attn_setup():
        import jax, jax.numpy as jnp
        import numpy as np
        D_MODEL, D_STATE, D_INNER = (128, 16, 256)
        B, S = (2, 512)
        EPS = 1e-05
        key = jax.random.key(seed)
        ks = jax.random.split(key, 8)
        return {'x': jax.random.normal(ks[0], (B, S, D_MODEL), dtype=jnp.float32), 'norm_w': jnp.ones((D_MODEL,), jnp.float32), 'norm_b': jnp.zeros((D_MODEL,), jnp.float32), 'W_in': jax.random.normal(ks[1], (D_INNER, D_MODEL), jnp.float32) * (1.0 / np.sqrt(D_MODEL)), 'b_in': jnp.zeros((D_INNER,), jnp.float32), 'A': jax.random.normal(ks[2], (D_INNER, D_STATE), jnp.float32), 'B_ssm': jax.random.normal(ks[3], (D_INNER, D_STATE), jnp.float32), 'C_ssm': jax.random.normal(ks[4], (D_INNER, D_STATE), jnp.float32), 'W_out': jax.random.normal(ks[5], (D_MODEL, D_INNER), jnp.float32) * (1.0 / np.sqrt(D_INNER)), 'b_out': jnp.zeros((D_MODEL,), jnp.float32)}
    _L1_attn_all = _L1_attn_setup()
    _L1_attn_in = {k: v for k, v in _L1_attn_all.items() if k in ('norm_w', 'norm_b', 'W_in', 'b_in', 'A', 'B_ssm', 'C_ssm', 'W_out', 'b_out')}
    del _L1_attn_all

    def _L1_xattn_setup():
        import jax, jax.numpy as jnp
        import numpy as np
        DIM = 128
        DEPTH = 4
        HEADS = 8
        DH = 64
        INNER = HEADS * DH
        FF = 4 * DIM
        ROT = 32
        B, CHUNK, SEQ = (128, 128, 64)

        def rope_freqs(n, rot_dim):
            inv = 1.0 / 10000.0 ** (jnp.arange(0, rot_dim, 2, dtype=jnp.float32) / rot_dim)
            freqs = jnp.arange(n, dtype=jnp.float32)[:, None] * inv[None, :]
            return jnp.concatenate([freqs, freqs], axis=-1)

        def apply_rope(t, freqs):
            rot = freqs.shape[-1]
            t1, tp = (t[..., :rot], t[..., rot:])
            d2 = rot // 2
            rh = jnp.concatenate([-t1[..., d2:], t1[..., :d2]], axis=-1)
            t1 = t1 * jnp.cos(freqs) + rh * jnp.sin(freqs)
            return jnp.concatenate([t1, tp], axis=-1)

        def rmsnorm(x, gamma, eps=1e-08):
            n = jnp.sqrt(jnp.sum(x * x, axis=-1, keepdims=True)) * x.shape[-1] ** (-0.5)
            return x / jnp.maximum(n, eps) * gamma

        def attn_block(xq, ctx, Wq, Wk, Wv, Wo, bo, pe_q, pe_k, mask):
            b, n, _ = xq.shape
            j = ctx.shape[1]
            q = (xq @ Wq).reshape(b, n, HEADS, DH).transpose(0, 2, 1, 3)
            k = (ctx @ Wk).reshape(b, j, HEADS, DH).transpose(0, 2, 1, 3)
            v = (ctx @ Wv).reshape(b, j, HEADS, DH).transpose(0, 2, 1, 3)
            q = q * DH ** (-0.5)
            q = apply_rope(q, pe_q)
            k = apply_rope(k, pe_k)
            sim = jnp.einsum('bhid,bhjd->bhij', q, k)
            if mask is not None:
                sim = jnp.where(mask[:, None, None, :], sim, -jnp.finfo(sim.dtype).max)
            a = jax.nn.softmax(sim, axis=-1)
            out = jnp.einsum('bhij,bhjd->bhid', a, v)
            out = out.transpose(0, 2, 1, 3).reshape(b, n, INNER)
            return out @ Wo + bo
        key = jax.random.key(seed)
        ks = jax.random.split(key, 16)
        g = lambda k, shape: 0.02 * jax.random.normal(k, shape, dtype=jnp.float32)
        inp = {'x': jax.random.normal(ks[0], (B, CHUNK, DIM), dtype=jnp.float32), 'chunked_seq': jax.random.normal(ks[1], (B, SEQ, DIM), dtype=jnp.float32), 'mask': jnp.ones((B, CHUNK), dtype=bool), 'sWq': g(ks[2], (DEPTH, DIM, INNER)), 'sWk': g(ks[3], (DEPTH, DIM, INNER)), 'sWv': g(ks[4], (DEPTH, DIM, INNER)), 'sWo': g(ks[5], (DEPTH, INNER, DIM)), 'sbo': jnp.zeros((DEPTH, DIM), jnp.float32), 'sg': jnp.ones((DEPTH, DIM), jnp.float32), 'cWq': g(ks[6], (DEPTH, DIM, INNER)), 'cWk': g(ks[7], (DEPTH, DIM, INNER)), 'cWv': g(ks[8], (DEPTH, DIM, INNER)), 'cWo': g(ks[9], (DEPTH, INNER, DIM)), 'cbo': jnp.zeros((DEPTH, DIM), jnp.float32), 'cg': jnp.ones((DEPTH, DIM), jnp.float32), 'fW1': g(ks[10], (DEPTH, DIM, FF)), 'fb1': jnp.zeros((DEPTH, FF), jnp.float32), 'fW2': g(ks[11], (DEPTH, FF, DIM)), 'fb2': jnp.zeros((DEPTH, DIM), jnp.float32), 'fg': jnp.ones((DEPTH, DIM), jnp.float32), 'g_out': jnp.ones((DIM,), jnp.float32)}
        return inp
    _L1_xattn_all = _L1_xattn_setup()
    _L1_xattn_in = {k: v for k, v in _L1_xattn_all.items() if k in ('sWq', 'sWk', 'sWv', 'sWo', 'sbo', 'sg', 'cWq', 'cWk', 'cWv', 'cWo', 'cbo', 'cg', 'fW1', 'fb1', 'fW2', 'fb2', 'fg', 'g_out')}
    del _L1_xattn_all

    def _L1_ffn_setup():
        import jax, jax.numpy as jnp
        import numpy as np
        NUM_EXPERTS = 4
        key = jax.random.key(seed)
        ks = jax.random.split(key, 8)
        B, L, H = (8, 256, 128)
        F = 4 * H
        s = 0.02
        x = jax.random.normal(ks[0], (B, L, H), dtype=jnp.float32)
        Wr = jax.random.normal(ks[1], (H, NUM_EXPERTS), dtype=jnp.float32) * s
        br = jnp.zeros((NUM_EXPERTS,), dtype=jnp.float32)
        We1 = jax.random.normal(ks[2], (NUM_EXPERTS, H, F), dtype=jnp.float32) * s
        be1 = jnp.zeros((NUM_EXPERTS, F), dtype=jnp.float32)
        We2 = jax.random.normal(ks[3], (NUM_EXPERTS, F, H), dtype=jnp.float32) * s
        be2 = jnp.zeros((NUM_EXPERTS, H), dtype=jnp.float32)
        return {'x': x, 'Wr': Wr, 'br': br, 'We1': We1, 'be1': be1, 'We2': We2, 'be2': be2}
    _L1_ffn_all = _L1_ffn_setup()
    _L1_ffn_in = {k: v for k, v in _L1_ffn_all.items() if k in ('Wr', 'br', 'We1', 'be1', 'We2', 'be2')}
    del _L1_ffn_all

    def _L2_attn_setup():
        import jax, jax.numpy as jnp
        import numpy as np
        import math
        HEAD_SIZE = 64

        def rotate_every_two(x):
            x1 = x[..., ::2]
            x2 = x[..., 1::2]
            return jnp.stack((-x2, x1), axis=-1).reshape(x.shape)

        def rope_table(seq_len, dtype=jnp.float32):
            pos = jnp.arange(seq_len, dtype=jnp.float32)
            inv = 10000.0 ** (jnp.arange(0, HEAD_SIZE, 2, dtype=jnp.float32) / HEAD_SIZE)
            radians = pos[:, None] / inv
            sincos = jnp.stack((jnp.sin(radians), jnp.cos(radians)), axis=-1).reshape(seq_len, -1)
            t = jnp.repeat(sincos, 2, axis=-1)
            return t.astype(dtype)
        key = jax.random.key(seed)
        ks = jax.random.split(key, 7)
        B, S, H = (2, 512, 128)
        sd = 1.0 / math.sqrt(H)
        return {'hidden_states': jax.random.normal(ks[0], (B, S, H), dtype=jnp.float32), 'Wq': jax.random.normal(ks[1], (H, H), dtype=jnp.float32) * sd, 'bq': jax.random.normal(ks[2], (H,), dtype=jnp.float32) * sd, 'Wk': jax.random.normal(ks[3], (H, H), dtype=jnp.float32) * sd, 'bk': jax.random.normal(ks[4], (H,), dtype=jnp.float32) * sd, 'Wv': jax.random.normal(ks[5], (H, H), dtype=jnp.float32) * sd, 'bv': jax.random.normal(ks[6], (H,), dtype=jnp.float32) * sd}
    _L2_attn_all = _L2_attn_setup()
    _L2_attn_in = {k: v for k, v in _L2_attn_all.items() if k in ('Wq', 'bq', 'Wk', 'bk', 'Wv', 'bv')}
    del _L2_attn_all

    def _L2_xattn_setup():
        import jax, jax.numpy as jnp
        import numpy as np
        DIM = 128
        SCALE_DIM = 4
        QK_DIM = DIM // SCALE_DIM
        B, S = (4, 512)
        key = jax.random.key(seed)
        ks = jax.random.split(key, 8)
        std = 1.0 / np.sqrt(DIM)
        return {'q': jax.random.normal(ks[0], (B, S, DIM), jnp.float32), 'k': jax.random.normal(ks[1], (B, S, DIM), jnp.float32), 'v': jax.random.normal(ks[2], (B, S, DIM), jnp.float32), 'Wq': jax.random.normal(ks[3], (QK_DIM, DIM), jnp.float32) * std, 'bq': jnp.zeros((QK_DIM,), jnp.float32), 'Wk': jax.random.normal(ks[4], (QK_DIM, DIM), jnp.float32) * std, 'bk': jnp.zeros((QK_DIM,), jnp.float32), 'Wv': jax.random.normal(ks[5], (DIM, DIM), jnp.float32) * std, 'bv': jnp.zeros((DIM,), jnp.float32)}
    _L2_xattn_all = _L2_xattn_setup()
    _L2_xattn_in = {k: v for k, v in _L2_xattn_all.items() if k in ('Wq', 'bq', 'Wk', 'bk', 'Wv', 'bv')}
    del _L2_xattn_all

    def _L2_ffn_setup():
        import jax, jax.numpy as jnp
        import numpy as np
        B, S, D_MODEL, D_FF, E, R, TOP_K = (4, 256, 128, 512, 8, 16, 2)
        key = jax.random.key(seed)
        ks = jax.random.split(key, 9)
        sd = 1.0 / np.sqrt(D_MODEL)
        return {'hidden_states': jax.random.normal(ks[0], (B, S, D_MODEL), jnp.float32), 'wi': jax.random.normal(ks[1], (D_FF, D_MODEL), jnp.float32) * sd, 'bi': jax.random.normal(ks[2], (D_FF,), jnp.float32) * 0.01, 'wo': jax.random.normal(ks[3], (D_MODEL, D_FF), jnp.float32) * (1.0 / np.sqrt(D_FF)), 'bo': jax.random.normal(ks[4], (D_MODEL,), jnp.float32) * 0.01, 'lora_A': jax.random.normal(ks[5], (E, R, D_MODEL), jnp.float32) * sd, 'lora_B': jax.random.normal(ks[6], (E, D_FF, R), jnp.float32) * 0.02, 'gate_w': jax.random.normal(ks[7], (E, D_MODEL), jnp.float32) * sd, 'gate_b': jax.random.normal(ks[8], (E,), jnp.float32) * 0.01}
    _L2_ffn_all = _L2_ffn_setup()
    _L2_ffn_in = {k: v for k, v in _L2_ffn_all.items() if k in ('wi', 'bi', 'wo', 'bo', 'lora_A', 'lora_B', 'gate_w', 'gate_b')}
    del _L2_ffn_all

    def _L3_attn_setup():
        import jax, jax.numpy as jnp
        import numpy as np
        D_MODEL = 128
        N_HEADS = 16
        D_K = D_MODEL // N_HEADS
        MAX_LEN = 256
        B, T = (2, 256)
        key = jax.random.key(seed)
        ks = jax.random.split(key, 10)
        s = 1.0 / np.sqrt(D_MODEL)
        inp = {'x': jax.random.normal(ks[0], (B, T, D_MODEL), dtype=jnp.float32), 'WQ': jax.random.uniform(ks[1], (D_MODEL, D_MODEL), minval=-s, maxval=s, dtype=jnp.float32), 'bQ': jax.random.uniform(ks[2], (D_MODEL,), minval=-s, maxval=s, dtype=jnp.float32), 'WK': jax.random.uniform(ks[3], (D_MODEL, D_MODEL), minval=-s, maxval=s, dtype=jnp.float32), 'bK': jax.random.uniform(ks[4], (D_MODEL,), minval=-s, maxval=s, dtype=jnp.float32), 'WV': jax.random.uniform(ks[5], (D_MODEL, D_MODEL), minval=-s, maxval=s, dtype=jnp.float32), 'bV': jax.random.uniform(ks[6], (D_MODEL,), minval=-s, maxval=s, dtype=jnp.float32), 'WO': jax.random.uniform(ks[7], (D_MODEL, D_MODEL), minval=-s, maxval=s, dtype=jnp.float32), 'bO': jax.random.uniform(ks[8], (D_MODEL,), minval=-s, maxval=s, dtype=jnp.float32), 'rel_pos_table': jax.random.normal(ks[9], (2 * MAX_LEN - 1, N_HEADS), dtype=jnp.float32)}
        return inp
    _L3_attn_all = _L3_attn_setup()
    _L3_attn_in = {k: v for k, v in _L3_attn_all.items() if k in ('WQ', 'bQ', 'WK', 'bK', 'WV', 'bV', 'WO', 'bO', 'rel_pos_table')}
    del _L3_attn_all

    def _L3_xattn_setup():
        import jax, jax.numpy as jnp
        import numpy as np
        import math
        N, T, D_MODEL, H, D = (4, 256, 128, 16, 64)
        key = jax.random.key(seed)
        ks = jax.random.split(key, 12)
        s = 0.02
        return {'xq': jax.random.normal(ks[0], (N, T, D_MODEL), dtype=jnp.float32), 'xk': jax.random.normal(ks[1], (N, T, D_MODEL), dtype=jnp.float32), 'xv': jax.random.normal(ks[2], (N, T, D_MODEL), dtype=jnp.float32), 'padding_mask': jnp.ones((N, T), dtype=jnp.int32), 'Wq': jax.random.normal(ks[3], (D_MODEL, H * D), dtype=jnp.float32) * s, 'bq': jnp.zeros((H * D,), dtype=jnp.float32), 'Wk': jax.random.normal(ks[4], (D_MODEL, H * D), dtype=jnp.float32) * s, 'bk': jnp.zeros((H * D,), dtype=jnp.float32), 'Wv': jax.random.normal(ks[5], (D_MODEL, H * D), dtype=jnp.float32) * s, 'bv': jnp.zeros((H * D,), dtype=jnp.float32), 'Wo': jax.random.normal(ks[6], (H * D, D_MODEL), dtype=jnp.float32) * s, 'bo': jnp.zeros((D_MODEL,), dtype=jnp.float32)}
    _L3_xattn_all = _L3_xattn_setup()
    _L3_xattn_in = {k: v for k, v in _L3_xattn_all.items() if k in ('Wq', 'bq', 'Wk', 'bk', 'Wv', 'bv', 'Wo', 'bo')}
    del _L3_xattn_all

    def _L3_ffn_setup():
        import jax, jax.numpy as jnp
        import numpy as np
        NUM_EXPERTS = 8
        TOP_K = 2
        DIM = 128
        HIDDEN = 512
        B, S = (2, 128)
        key = jax.random.key(seed)
        k_x, k_g, k_1, k_2, k_3 = jax.random.split(key, 5)
        s_d = 1.0 / np.sqrt(DIM)
        s_h = 1.0 / np.sqrt(HIDDEN)
        return {'x': jax.random.normal(k_x, (B, S, DIM), dtype=jnp.float32), 'gate_w': jax.random.normal(k_g, (NUM_EXPERTS, DIM), dtype=jnp.float32) * s_d, 'w1': jax.random.normal(k_1, (NUM_EXPERTS, HIDDEN, DIM), dtype=jnp.float32) * s_d, 'w2': jax.random.normal(k_2, (NUM_EXPERTS, DIM, HIDDEN), dtype=jnp.float32) * s_h, 'w3': jax.random.normal(k_3, (NUM_EXPERTS, HIDDEN, DIM), dtype=jnp.float32) * s_d}
    _L3_ffn_all = _L3_ffn_setup()
    _L3_ffn_in = {k: v for k, v in _L3_ffn_all.items() if k in ('gate_w', 'w1', 'w2', 'w3')}
    del _L3_ffn_all
    return {'x': x, 'ctx_1024': ctx_1024, 'mask_BxS_bf1': mask_BxS_bf1, 'mask_BxS2_if1': mask_BxS2_if1, 'L0_attn_proj': _L0_attn_in['proj'], 'L0_attn_w_qkv': _L0_attn_in['w_qkv'], 'L0_attn_w_out': _L0_attn_in['w_out'], 'L0_attn_b_out': _L0_attn_in['b_out'], 'L0_attn_gamma': _L0_attn_in['gamma'], 'L0_attn_beta': _L0_attn_in['beta'], 'L0_attn_w1': _L0_attn_in['w1'], 'L0_attn_b1': _L0_attn_in['b1'], 'L0_attn_w2': _L0_attn_in['w2'], 'L0_attn_b2': _L0_attn_in['b2'], 'L0_xattn_Wq': _L0_xattn_in['Wq'], 'L0_xattn_bq': _L0_xattn_in['bq'], 'L0_xattn_Wk': _L0_xattn_in['Wk'], 'L0_xattn_bk': _L0_xattn_in['bk'], 'L0_xattn_Wv': _L0_xattn_in['Wv'], 'L0_xattn_bv': _L0_xattn_in['bv'], 'L0_xattn_Wo': _L0_xattn_in['Wo'], 'L0_xattn_bo': _L0_xattn_in['bo'], 'L0_ffn_Wq': _L0_ffn_in['Wq'], 'L0_ffn_Wkv': _L0_ffn_in['Wkv'], 'L0_ffn_Ws': _L0_ffn_in['Ws'], 'L0_ffn_Wd': _L0_ffn_in['Wd'], 'L0_ffn_Wo': _L0_ffn_in['Wo'], 'L1_attn_norm_w': _L1_attn_in['norm_w'], 'L1_attn_norm_b': _L1_attn_in['norm_b'], 'L1_attn_W_in': _L1_attn_in['W_in'], 'L1_attn_b_in': _L1_attn_in['b_in'], 'L1_attn_A': _L1_attn_in['A'], 'L1_attn_B_ssm': _L1_attn_in['B_ssm'], 'L1_attn_C_ssm': _L1_attn_in['C_ssm'], 'L1_attn_W_out': _L1_attn_in['W_out'], 'L1_attn_b_out': _L1_attn_in['b_out'], 'L1_xattn_sWq': _L1_xattn_in['sWq'], 'L1_xattn_sWk': _L1_xattn_in['sWk'], 'L1_xattn_sWv': _L1_xattn_in['sWv'], 'L1_xattn_sWo': _L1_xattn_in['sWo'], 'L1_xattn_sbo': _L1_xattn_in['sbo'], 'L1_xattn_sg': _L1_xattn_in['sg'], 'L1_xattn_cWq': _L1_xattn_in['cWq'], 'L1_xattn_cWk': _L1_xattn_in['cWk'], 'L1_xattn_cWv': _L1_xattn_in['cWv'], 'L1_xattn_cWo': _L1_xattn_in['cWo'], 'L1_xattn_cbo': _L1_xattn_in['cbo'], 'L1_xattn_cg': _L1_xattn_in['cg'], 'L1_xattn_fW1': _L1_xattn_in['fW1'], 'L1_xattn_fb1': _L1_xattn_in['fb1'], 'L1_xattn_fW2': _L1_xattn_in['fW2'], 'L1_xattn_fb2': _L1_xattn_in['fb2'], 'L1_xattn_fg': _L1_xattn_in['fg'], 'L1_xattn_g_out': _L1_xattn_in['g_out'], 'L1_ffn_Wr': _L1_ffn_in['Wr'], 'L1_ffn_br': _L1_ffn_in['br'], 'L1_ffn_We1': _L1_ffn_in['We1'], 'L1_ffn_be1': _L1_ffn_in['be1'], 'L1_ffn_We2': _L1_ffn_in['We2'], 'L1_ffn_be2': _L1_ffn_in['be2'], 'L2_attn_Wq': _L2_attn_in['Wq'], 'L2_attn_bq': _L2_attn_in['bq'], 'L2_attn_Wk': _L2_attn_in['Wk'], 'L2_attn_bk': _L2_attn_in['bk'], 'L2_attn_Wv': _L2_attn_in['Wv'], 'L2_attn_bv': _L2_attn_in['bv'], 'L2_xattn_Wq': _L2_xattn_in['Wq'], 'L2_xattn_bq': _L2_xattn_in['bq'], 'L2_xattn_Wk': _L2_xattn_in['Wk'], 'L2_xattn_bk': _L2_xattn_in['bk'], 'L2_xattn_Wv': _L2_xattn_in['Wv'], 'L2_xattn_bv': _L2_xattn_in['bv'], 'L2_ffn_wi': _L2_ffn_in['wi'], 'L2_ffn_bi': _L2_ffn_in['bi'], 'L2_ffn_wo': _L2_ffn_in['wo'], 'L2_ffn_bo': _L2_ffn_in['bo'], 'L2_ffn_lora_A': _L2_ffn_in['lora_A'], 'L2_ffn_lora_B': _L2_ffn_in['lora_B'], 'L2_ffn_gate_w': _L2_ffn_in['gate_w'], 'L2_ffn_gate_b': _L2_ffn_in['gate_b'], 'L3_attn_WQ': _L3_attn_in['WQ'], 'L3_attn_bQ': _L3_attn_in['bQ'], 'L3_attn_WK': _L3_attn_in['WK'], 'L3_attn_bK': _L3_attn_in['bK'], 'L3_attn_WV': _L3_attn_in['WV'], 'L3_attn_bV': _L3_attn_in['bV'], 'L3_attn_WO': _L3_attn_in['WO'], 'L3_attn_bO': _L3_attn_in['bO'], 'L3_attn_rel_pos_table': _L3_attn_in['rel_pos_table'], 'L3_xattn_Wq': _L3_xattn_in['Wq'], 'L3_xattn_bq': _L3_xattn_in['bq'], 'L3_xattn_Wk': _L3_xattn_in['Wk'], 'L3_xattn_bk': _L3_xattn_in['bk'], 'L3_xattn_Wv': _L3_xattn_in['Wv'], 'L3_xattn_bv': _L3_xattn_in['bv'], 'L3_xattn_Wo': _L3_xattn_in['Wo'], 'L3_xattn_bo': _L3_xattn_in['bo'], 'L3_ffn_gate_w': _L3_ffn_in['gate_w'], 'L3_ffn_w1': _L3_ffn_in['w1'], 'L3_ffn_w2': _L3_ffn_in['w2'], 'L3_ffn_w3': _L3_ffn_in['w3']}

def reference(x, ctx_1024, mask_BxS_bf1, mask_BxS2_if1, L0_attn_proj, L0_attn_w_qkv, L0_attn_w_out, L0_attn_b_out, L0_attn_gamma, L0_attn_beta, L0_attn_w1, L0_attn_b1, L0_attn_w2, L0_attn_b2, L0_xattn_Wq, L0_xattn_bq, L0_xattn_Wk, L0_xattn_bk, L0_xattn_Wv, L0_xattn_bv, L0_xattn_Wo, L0_xattn_bo, L0_ffn_Wq, L0_ffn_Wkv, L0_ffn_Ws, L0_ffn_Wd, L0_ffn_Wo, L1_attn_norm_w, L1_attn_norm_b, L1_attn_W_in, L1_attn_b_in, L1_attn_A, L1_attn_B_ssm, L1_attn_C_ssm, L1_attn_W_out, L1_attn_b_out, L1_xattn_sWq, L1_xattn_sWk, L1_xattn_sWv, L1_xattn_sWo, L1_xattn_sbo, L1_xattn_sg, L1_xattn_cWq, L1_xattn_cWk, L1_xattn_cWv, L1_xattn_cWo, L1_xattn_cbo, L1_xattn_cg, L1_xattn_fW1, L1_xattn_fb1, L1_xattn_fW2, L1_xattn_fb2, L1_xattn_fg, L1_xattn_g_out, L1_ffn_Wr, L1_ffn_br, L1_ffn_We1, L1_ffn_be1, L1_ffn_We2, L1_ffn_be2, L2_attn_Wq, L2_attn_bq, L2_attn_Wk, L2_attn_bk, L2_attn_Wv, L2_attn_bv, L2_xattn_Wq, L2_xattn_bq, L2_xattn_Wk, L2_xattn_bk, L2_xattn_Wv, L2_xattn_bv, L2_ffn_wi, L2_ffn_bi, L2_ffn_wo, L2_ffn_bo, L2_ffn_lora_A, L2_ffn_lora_B, L2_ffn_gate_w, L2_ffn_gate_b, L3_attn_WQ, L3_attn_bQ, L3_attn_WK, L3_attn_bK, L3_attn_WV, L3_attn_bV, L3_attn_WO, L3_attn_bO, L3_attn_rel_pos_table, L3_xattn_Wq, L3_xattn_bq, L3_xattn_Wk, L3_xattn_bk, L3_xattn_Wv, L3_xattn_bv, L3_xattn_Wo, L3_xattn_bo, L3_ffn_gate_w, L3_ffn_w1, L3_ffn_w2, L3_ffn_w3):
    import jax
    import jax.numpy as jnp

    def _L0_attn_ref(x, proj, w_qkv, w_out, b_out, gamma, beta, w1, b1, w2, b2):
        import jax, jax.numpy as jnp
        import numpy as np
        B, N, D = (4, 512, 128)
        H, F = (16, 32)
        HD = D // H
        EPS_ATTN = 1e-08
        EPS_LN = 1e-05

        def _layernorm(x, gamma, beta):
            mu = jnp.mean(x, axis=-1, keepdims=True)
            var = jnp.var(x, axis=-1, keepdims=True)
            return (x - mu) * jax.lax.rsqrt(var + EPS_LN) * gamma + beta
        residual = x
        b, n, d = x.shape
        qkv = x @ w_qkv.T
        q, k, v = jnp.split(qkv, 3, axis=-1)

        def to_heads(t):
            return t.reshape(b, n, H, HD).transpose(0, 2, 1, 3)
        q, k, v = (to_heads(q), to_heads(k), to_heads(v))
        q_f = jax.nn.elu(jnp.einsum('bhnd,hdf->bhnf', q, proj)) + 1.0
        k_f = jax.nn.elu(jnp.einsum('bhnd,hdf->bhnf', k, proj)) + 1.0
        kv = jnp.einsum('bhnf,bhnd->bhfd', k_f, v)
        attn = jnp.einsum('bhnf,bhfd->bhnd', q_f, kv)
        k_sum = jnp.sum(k_f, axis=2)
        z = 1.0 / (jnp.einsum('bhnf,bhf->bhn', q_f, k_sum) + EPS_ATTN)
        attn = attn * z[..., None]
        attn = attn.transpose(0, 2, 1, 3).reshape(b, n, d)
        x = residual + attn @ w_out.T + b_out
        x = _layernorm(x, gamma, beta)
        h = jax.nn.gelu(x @ w1.T + b1, approximate=False)
        x = x + h @ w2.T + b2
        x = _layernorm(x, gamma, beta)
        return x

    def _L0_xattn_ref(queries, keys, values, Wq, bq, Wk, bk, Wv, bv, Wo, bo):
        import jax, jax.numpy as jnp
        import numpy as np
        import math
        D = 128
        H = 16
        B = 4
        S = 256

        def _split_heads(x):
            b, s, d = x.shape
            return x.reshape(b, s, H, d // H).transpose(0, 2, 1, 3)
        q = jax.nn.relu(queries @ Wq + bq)
        k = jax.nn.relu(keys @ Wk + bk)
        v = jax.nn.relu(values @ Wv + bv)
        q, k, v = (_split_heads(q), _split_heads(k), _split_heads(v))
        dk = q.shape[-1]
        scores = jnp.einsum('bhqd,bhkd->bhqk', q, k) / jnp.sqrt(jnp.float32(dk))
        attn = jax.nn.softmax(scores, axis=-1)
        y = jnp.einsum('bhqk,bhkd->bhqd', attn, v)
        y = y.transpose(0, 2, 1, 3).reshape(queries.shape[0], queries.shape[1], -1)
        return jax.nn.relu(y @ Wo + bo)

    def _L0_ffn_ref(x, Wq, Wkv, Ws, Wd, Wo):
        import jax, jax.numpy as jnp
        import numpy as np
        B, T, DIM = (4, 128, 128)
        H, E, DH, K = (8, 5, 64, 3)

        def _topk_mask(s, k):
            idx = jax.lax.top_k(s, k)[1]
            return jnp.sum(jax.nn.one_hot(idx, s.shape[-1], dtype=s.dtype), axis=-2)
        b, t, _ = x.shape
        scale = DH ** (-0.5)
        ss = jax.nn.sigmoid(x @ Ws).reshape(b, t, H, E)
        sd = jax.nn.sigmoid(x @ Wd).reshape(b, t, H, E)
        ms = _topk_mask(ss, K)
        md = _topk_mask(sd, K)
        ss_g = ss * ms
        sd_g = sd * md
        q5 = (x @ Wq).reshape(b, t, H, E, DH)
        kv = (x @ Wkv).reshape(b, t, 2, H, E, DH)
        k5, v5 = (kv[:, :, 0], kv[:, :, 1])
        q = jnp.einsum('bthed,bthe->bhtd', q5, sd_g)
        k = jnp.einsum('bthed,bthe->bhtd', k5, ss_g)
        v = jnp.einsum('bthed,bthe->bhtd', v5, ss_g)
        attn = jax.nn.softmax(jnp.einsum('bhid,bhjd->bhij', q * scale, k), axis=-1)
        out = jnp.einsum('bhij,bhjd->bihd', attn, v)
        o5 = jnp.einsum('bthd,dm->bthm', out, Wo).reshape(b, t, H, E, DIM)
        return jnp.einsum('bthem,bthe->btm', o5, md)

    def _L1_attn_ref(x, norm_w, norm_b, W_in, b_in, A, B_ssm, C_ssm, W_out, b_out):
        import jax, jax.numpy as jnp
        import numpy as np
        D_MODEL, D_STATE, D_INNER = (128, 16, 256)
        B, S = (2, 512)
        EPS = 1e-05
        residual = x
        mu = jnp.mean(x, axis=-1, keepdims=True)
        var = jnp.mean(jnp.square(x - mu), axis=-1, keepdims=True)
        xn = (x - mu) * jax.lax.rsqrt(var + EPS) * norm_w + norm_b
        h = jnp.einsum('bsd,ed->bse', xn, W_in) + b_in
        a = jax.nn.sigmoid(jnp.einsum('bse,en->bsn', h, A))
        u = jnp.einsum('bse,en->bsn', h, B_ssm)

        def step(s, inp):
            a_t, u_t = inp
            s = s * a_t + u_t
            return (s, s)
        s0 = jnp.zeros((x.shape[0], D_STATE), x.dtype)
        _, states = jax.lax.scan(step, s0, (jnp.swapaxes(a, 0, 1), jnp.swapaxes(u, 0, 1)))
        y = jnp.einsum('sbn,en->bse', states, C_ssm)
        out = jnp.einsum('bse,de->bsd', y, W_out) + b_out
        return out + residual

    def _L1_xattn_ref(x, chunked_seq, mask, sWq, sWk, sWv, sWo, sbo, sg, cWq, cWk, cWv, cWo, cbo, cg, fW1, fb1, fW2, fb2, fg, g_out):
        import jax, jax.numpy as jnp
        import numpy as np
        DIM = 128
        DEPTH = 4
        HEADS = 8
        DH = 64
        INNER = HEADS * DH
        FF = 4 * DIM
        ROT = 32
        B, CHUNK, SEQ = (128, 128, 64)

        def rope_freqs(n, rot_dim):
            inv = 1.0 / 10000.0 ** (jnp.arange(0, rot_dim, 2, dtype=jnp.float32) / rot_dim)
            freqs = jnp.arange(n, dtype=jnp.float32)[:, None] * inv[None, :]
            return jnp.concatenate([freqs, freqs], axis=-1)

        def apply_rope(t, freqs):
            rot = freqs.shape[-1]
            t1, tp = (t[..., :rot], t[..., rot:])
            d2 = rot // 2
            rh = jnp.concatenate([-t1[..., d2:], t1[..., :d2]], axis=-1)
            t1 = t1 * jnp.cos(freqs) + rh * jnp.sin(freqs)
            return jnp.concatenate([t1, tp], axis=-1)

        def rmsnorm(x, gamma, eps=1e-08):
            n = jnp.sqrt(jnp.sum(x * x, axis=-1, keepdims=True)) * x.shape[-1] ** (-0.5)
            return x / jnp.maximum(n, eps) * gamma

        def attn_block(xq, ctx, Wq, Wk, Wv, Wo, bo, pe_q, pe_k, mask):
            b, n, _ = xq.shape
            j = ctx.shape[1]
            q = (xq @ Wq).reshape(b, n, HEADS, DH).transpose(0, 2, 1, 3)
            k = (ctx @ Wk).reshape(b, j, HEADS, DH).transpose(0, 2, 1, 3)
            v = (ctx @ Wv).reshape(b, j, HEADS, DH).transpose(0, 2, 1, 3)
            q = q * DH ** (-0.5)
            q = apply_rope(q, pe_q)
            k = apply_rope(k, pe_k)
            sim = jnp.einsum('bhid,bhjd->bhij', q, k)
            if mask is not None:
                sim = jnp.where(mask[:, None, None, :], sim, -jnp.finfo(sim.dtype).max)
            a = jax.nn.softmax(sim, axis=-1)
            out = jnp.einsum('bhij,bhjd->bhid', a, v)
            out = out.transpose(0, 2, 1, 3).reshape(b, n, INNER)
            return out @ Wo + bo
        pe_q = rope_freqs(x.shape[1], ROT)
        pe_k = rope_freqs(chunked_seq.shape[1], ROT)
        for l in range(DEPTH):
            h = rmsnorm(x, sg[l])
            x = attn_block(h, h, sWq[l], sWk[l], sWv[l], sWo[l], sbo[l], pe_q, pe_q, mask) + x
            h = rmsnorm(x, cg[l])
            x = attn_block(h, chunked_seq, cWq[l], cWk[l], cWv[l], cWo[l], cbo[l], pe_q, pe_k, None) + x
            h = rmsnorm(x, fg[l])
            x = jax.nn.gelu(h @ fW1[l] + fb1[l], approximate=False) @ fW2[l] + fb2[l] + x
        return rmsnorm(x, g_out)

    def _L1_ffn_ref(x, Wr, br, We1, be1, We2, be2):
        import jax, jax.numpy as jnp
        import numpy as np
        NUM_EXPERTS = 4
        logits = jnp.einsum('blh,he->ble', x, Wr) + br
        top_expert = jnp.argmax(logits, axis=-1)
        mask = jax.nn.one_hot(top_expert, NUM_EXPERTS, dtype=x.dtype)
        out = jnp.zeros_like(x)
        for e in range(NUM_EXPERTS):
            h1 = jax.nn.relu(jnp.einsum('blh,hf->blf', x, We1[e]) + be1[e])
            oe = jnp.einsum('blf,fh->blh', h1, We2[e]) + be2[e]
            out = out + mask[..., e:e + 1] * oe
        return out

    def _L2_attn_ref(hidden_states, Wq, bq, Wk, bk, Wv, bv):
        import jax, jax.numpy as jnp
        import numpy as np
        import math
        HEAD_SIZE = 64

        def rotate_every_two(x):
            x1 = x[..., ::2]
            x2 = x[..., 1::2]
            return jnp.stack((-x2, x1), axis=-1).reshape(x.shape)

        def rope_table(seq_len, dtype=jnp.float32):
            pos = jnp.arange(seq_len, dtype=jnp.float32)
            inv = 10000.0 ** (jnp.arange(0, HEAD_SIZE, 2, dtype=jnp.float32) / HEAD_SIZE)
            radians = pos[:, None] / inv
            sincos = jnp.stack((jnp.sin(radians), jnp.cos(radians)), axis=-1).reshape(seq_len, -1)
            t = jnp.repeat(sincos, 2, axis=-1)
            return t.astype(dtype)
        B, S, H = hidden_states.shape
        t = rope_table(S, hidden_states.dtype)
        q = hidden_states @ Wq.T + bq
        k = hidden_states @ Wk.T + bk
        v = hidden_states @ Wv.T + bv
        q = q * t + rotate_every_two(q) * t
        k = k * t + rotate_every_two(k) * t
        scale = math.sqrt(HEAD_SIZE)
        scores = jnp.einsum('bsh,bth->bst', q, k) / scale
        probs = jax.nn.softmax(scores, axis=-1)
        out = jnp.einsum('bst,bth->bsh', probs, v)
        return out

    def _L2_xattn_ref(q, k, v, Wq, bq, Wk, bk, Wv, bv):
        import jax, jax.numpy as jnp
        import numpy as np
        DIM = 128
        SCALE_DIM = 4
        QK_DIM = DIM // SCALE_DIM
        B, S = (4, 512)
        scale = jnp.asarray(np.sqrt(QK_DIM), q.dtype)
        qp = jnp.einsum('bsd,ed->bse', q, Wq) + bq
        kp = jnp.einsum('bsd,ed->bse', k, Wk) + bk
        vp = jnp.einsum('bsd,ed->bse', v, Wv) + bv
        z = jnp.einsum('bqe,bke->bqk', qp, kp)
        z = jax.nn.sigmoid(z / scale)
        return jnp.einsum('bqk,bkd->bqd', z, vp)

    def _L2_ffn_ref(hidden_states, wi, bi, wo, bo, lora_A, lora_B, gate_w, gate_b):
        import jax, jax.numpy as jnp
        import numpy as np
        B, S, D_MODEL, D_FF, E, R, TOP_K = (4, 256, 128, 512, 8, 16, 2)
        logits = jnp.einsum('bsd,ed->bse', hidden_states, gate_w) + gate_b
        scores = jax.nn.softmax(logits, axis=-1)
        top_v, top_i = jax.lax.top_k(scores, TOP_K)
        val_sum = top_v.sum(axis=-1)
        out = jnp.zeros_like(hidden_states)
        for e in range(E):
            count = (top_i == e).sum(axis=-1).astype(hidden_states.dtype)
            gate = count * val_sum
            inter = jnp.einsum('bsd,fd->bsf', hidden_states, wi) + bi + jnp.einsum('bsr,fr->bsf', jnp.einsum('bsd,rd->bsr', hidden_states, lora_A[e]), lora_B[e])
            h = jax.nn.relu(inter)
            expert_out = jnp.einsum('bsf,df->bsd', h, wo) + bo
            out = out + gate[..., None] * expert_out
        return out

    def _L3_attn_ref(x, WQ, bQ, WK, bK, WV, bV, WO, bO, rel_pos_table):
        import jax, jax.numpy as jnp
        import numpy as np
        D_MODEL = 128
        N_HEADS = 16
        D_K = D_MODEL // N_HEADS
        MAX_LEN = 256
        B, T = (2, 256)
        b, t, d = x.shape
        q = (x @ WQ.T + bQ).reshape(b, t, N_HEADS, D_K).transpose(0, 2, 1, 3)
        k = (x @ WK.T + bK).reshape(b, t, N_HEADS, D_K).transpose(0, 2, 1, 3)
        v = (x @ WV.T + bV).reshape(b, t, N_HEADS, D_K).transpose(0, 2, 1, 3)
        scores = jnp.einsum('bhqd,bhkd->bhqk', q, k) / jnp.sqrt(jnp.float32(D_K))
        pos = jnp.arange(t)
        rel = pos[:, None] - pos[None, :] + (MAX_LEN - 1)
        rel = jnp.clip(rel, 0, 2 * MAX_LEN - 2)
        rel_bias = rel_pos_table[rel]
        scores = scores + rel_bias.transpose(2, 0, 1)[None]
        causal = pos[None, :] <= pos[:, None]
        scores = jnp.where(causal[None, None], scores, -jnp.inf)
        attn = jax.nn.softmax(scores, axis=-1)
        out = jnp.einsum('bhqk,bhkd->bhqd', attn, v)
        out = out.transpose(0, 2, 1, 3).reshape(b, t, d)
        return out @ WO.T + bO

    def _L3_xattn_ref(xq, xk, xv, padding_mask, Wq, bq, Wk, bk, Wv, bv, Wo, bo):
        import jax, jax.numpy as jnp
        import numpy as np
        import math
        N, T, D_MODEL, H, D = (4, 256, 128, 16, 64)
        n, t_out, _ = xq.shape
        t_in = xk.shape[1]
        Q = (xq @ Wq + bq).reshape(n, t_out, H, D).transpose(0, 2, 1, 3)
        K = (xk @ Wk + bk).reshape(n, t_in, H, D).transpose(0, 2, 1, 3)
        V = (xv @ Wv + bv).reshape(n, t_in, H, D).transpose(0, 2, 1, 3)
        scores = jnp.einsum('bhqd,bhkd->bhqk', Q, K) / math.sqrt(D)
        neg_inf = jnp.float32(-jnp.inf)
        scores = jnp.where(padding_mask[:, None, None, :] == 0, neg_inf, scores)
        q_idx = jnp.arange(t_out)[:, None]
        k_idx = jnp.arange(t_in)[None, :]
        scores = jnp.where((k_idx <= q_idx)[None, None, :, :], scores, neg_inf)
        w = jax.nn.softmax(scores, axis=-1)
        attn = jnp.einsum('bhqk,bhkd->bhqd', w, V)
        attn = attn.transpose(0, 2, 1, 3).reshape(n, t_out, H * D)
        return attn @ Wo + bo

    def _L3_ffn_ref(x, gate_w, w1, w2, w3):
        import jax, jax.numpy as jnp
        import numpy as np
        NUM_EXPERTS = 8
        TOP_K = 2
        DIM = 128
        HIDDEN = 512
        B, S = (2, 128)
        orig_shape = x.shape
        xt = x.reshape(-1, orig_shape[-1])
        scores = xt @ gate_w.T
        top_vals, top_idx = jax.lax.top_k(scores, TOP_K)
        top_w = jax.nn.softmax(top_vals, axis=-1)
        combine = jnp.einsum('tke,tk->te', jax.nn.one_hot(top_idx, NUM_EXPERTS, dtype=xt.dtype), top_w)
        h = jax.nn.silu(jnp.einsum('td,ehd->eth', xt, w1)) * jnp.einsum('td,ehd->eth', xt, w3)
        ye = jnp.einsum('eth,edh->etd', h, w2)
        y = jnp.einsum('te,etd->td', combine, ye)
        return y.reshape(orig_shape)
    x = _layernorm(x + _L0_attn_ref(x, L0_attn_proj, L0_attn_w_qkv, L0_attn_w_out, L0_attn_b_out, L0_attn_gamma, L0_attn_beta, L0_attn_w1, L0_attn_b1, L0_attn_w2, L0_attn_b2), axis=-1)
    x = _layernorm(x + _L0_xattn_ref(x, ctx_1024, ctx_1024, L0_xattn_Wq, L0_xattn_bq, L0_xattn_Wk, L0_xattn_bk, L0_xattn_Wv, L0_xattn_bv, L0_xattn_Wo, L0_xattn_bo), axis=-1)
    x = _layernorm(x + _L0_ffn_ref(x, L0_ffn_Wq, L0_ffn_Wkv, L0_ffn_Ws, L0_ffn_Wd, L0_ffn_Wo), axis=-1)
    x = _layernorm(x + _L1_attn_ref(x, L1_attn_norm_w, L1_attn_norm_b, L1_attn_W_in, L1_attn_b_in, L1_attn_A, L1_attn_B_ssm, L1_attn_C_ssm, L1_attn_W_out, L1_attn_b_out), axis=-1)
    x = _layernorm(x + _L1_xattn_ref(x, ctx_1024, mask_BxS_bf1, L1_xattn_sWq, L1_xattn_sWk, L1_xattn_sWv, L1_xattn_sWo, L1_xattn_sbo, L1_xattn_sg, L1_xattn_cWq, L1_xattn_cWk, L1_xattn_cWv, L1_xattn_cWo, L1_xattn_cbo, L1_xattn_cg, L1_xattn_fW1, L1_xattn_fb1, L1_xattn_fW2, L1_xattn_fb2, L1_xattn_fg, L1_xattn_g_out), axis=-1)
    x = _layernorm(x + _L1_ffn_ref(x, L1_ffn_Wr, L1_ffn_br, L1_ffn_We1, L1_ffn_be1, L1_ffn_We2, L1_ffn_be2), axis=-1)
    x = _layernorm(x + _L2_attn_ref(x, L2_attn_Wq, L2_attn_bq, L2_attn_Wk, L2_attn_bk, L2_attn_Wv, L2_attn_bv), axis=-1)
    x = _layernorm(x + _L2_xattn_ref(x, ctx_1024, ctx_1024, L2_xattn_Wq, L2_xattn_bq, L2_xattn_Wk, L2_xattn_bk, L2_xattn_Wv, L2_xattn_bv), axis=-1)
    x = _layernorm(x + _L2_ffn_ref(x, L2_ffn_wi, L2_ffn_bi, L2_ffn_wo, L2_ffn_bo, L2_ffn_lora_A, L2_ffn_lora_B, L2_ffn_gate_w, L2_ffn_gate_b), axis=-1)
    x = _layernorm(x + _L3_attn_ref(x, L3_attn_WQ, L3_attn_bQ, L3_attn_WK, L3_attn_bK, L3_attn_WV, L3_attn_bV, L3_attn_WO, L3_attn_bO, L3_attn_rel_pos_table), axis=-1)
    x = _layernorm(x + _L3_xattn_ref(x, ctx_1024, ctx_1024, mask_BxS2_if1, L3_xattn_Wq, L3_xattn_bq, L3_xattn_Wk, L3_xattn_bk, L3_xattn_Wv, L3_xattn_bv, L3_xattn_Wo, L3_xattn_bo), axis=-1)
    x = _layernorm(x + _L3_ffn_ref(x, L3_ffn_gate_w, L3_ffn_w1, L3_ffn_w2, L3_ffn_w3), axis=-1)
    return x

_drawn_inputs = setup_inputs


def setup_inputs(seed=0):
    import zlib

    import numpy as np

    out = dict(_drawn_inputs(seed))
    spreads = {'L0_attn_b_out': (0.0, 0.1),
     'L0_attn_gamma': (1.0, 0.2),
     'L0_attn_beta': (0.0, 0.1),
     'L0_attn_b1': (0.0, 0.412),
     'L0_attn_b2': (0.0, 0.458),
     'L0_xattn_bq': (0.0, 0.8),
     'L0_xattn_bk': (0.0, 0.8),
     'L0_xattn_bv': (0.0, 0.394),
     'L0_xattn_bo': (0.0, 0.1),
     'L1_attn_norm_w': (1.0, 0.2),
     'L1_attn_norm_b': (0.0, 0.1),
     'L1_attn_b_in': (0.0, 0.1),
     'L1_attn_b_out': (0.0, 2.0),
     'L1_xattn_sbo': (0.0, 0.274),
     'L1_xattn_sg': (1.0, 0.6),
     'L1_xattn_cbo': (0.0, 0.274),
     'L1_xattn_cg': (1.0, 0.6),
     'L1_xattn_fb1': (0.0, 0.8),
     'L1_xattn_fb2': (0.0, 0.1),
     'L1_xattn_fg': (1.0, 0.6),
     'L1_xattn_g_out': (1.0, 0.591),
     'L1_ffn_br': (0.0, 0.482),
     'L1_ffn_be1': (0.0, 0.591),
     'L1_ffn_be2': (0.0, 0.34),
     'L2_xattn_bq': (0.0, 0.398),
     'L2_xattn_bk': (0.0, 0.533),
     'L2_xattn_bv': (0.0, 0.1),
     'L3_xattn_bq': (0.0, 0.8),
     'L3_xattn_bk': (0.0, 2.0),
     'L3_xattn_bv': (0.0, 0.1),
     'L3_xattn_bo': (0.0, 0.1)}
    factors = {'L0_attn_proj': 3.859,
     'L0_xattn_Wq': 3.517,
     'L0_xattn_Wk': 3.3,
     'L0_ffn_Wq': 8.0,
     'L0_ffn_Wkv': 2.999,
     'L0_ffn_Ws': 8.0,
     'L0_ffn_Wd': 4.176,
     'L1_xattn_sWq': 8.0,
     'L1_xattn_sWk': 8.0,
     'L1_xattn_sWv': 2.932,
     'L1_xattn_sWo': 3.827,
     'L1_xattn_cWq': 8.0,
     'L1_xattn_cWk': 8.0,
     'L1_xattn_cWv': 4.442,
     'L1_xattn_cWo': 3.599,
     'L1_xattn_fW1': 3.422,
     'L1_xattn_fW2': 3.52,
     'L1_ffn_Wr': 2.952,
     'L1_ffn_We1': 3.965,
     'L1_ffn_We2': 2.912,
     'L2_attn_bq': 8.0,
     'L2_attn_bk': 8.0,
     'L2_attn_bv': 3.25,
     'L2_ffn_bi': 5.627,
     'L2_ffn_bo': 4.059,
     'L2_ffn_gate_b': 8.0,
     'L3_attn_WQ': 8.0,
     'L3_attn_bQ': 64.0,
     'L3_attn_WK': 8.0,
     'L3_attn_bK': 64.0,
     'L3_attn_rel_pos_table': 5.668,
     'L3_xattn_Wq': 8.0,
     'L3_xattn_Wk': 8.0}
    for name, (base, spread) in spreads.items():
        noise = np.random.default_rng([zlib.crc32(name.encode()), seed]).standard_normal(out[name].shape)
        drawn = base * np.exp(spread * noise) if base else spread * noise
        out[name] = jnp.asarray(drawn.astype(out[name].dtype))
    for name, factor in factors.items():
        out[name] = (out[name] * factor).astype(out[name].dtype)
    return out
```

```python
from contextlib import ExitStack

import concourse.bass as bass
from concourse import mybir

F32 = mybir.dt.float32
I32 = mybir.dt.int32
U8 = mybir.dt.uint8
ALU = mybir.AluOpType
ACT = mybir.ActivationFunctionType
AX = mybir.AxisListType

P = 128
NBATCH, SEQ, CTX = 4, 512, 154
NT = SEQ // P
CK = CTX // 2
LAYERS = 4
HUGE = 3.0e38
MASKED = 1.0e30
EPS = 1e-5
RSQRT8 = 8.0 ** -0.5

WEIGHTS = {
    0: [("wqkv", 384), ("proj", 512), ("wout", 128)],
    1: [("w1", 512), ("w2", 512)],
    2: [("wq", 512), ("wk", 512), ("wv", 128), ("wo", 128)],
    3: [("wq", 2560), ("wk", 2560), ("wv", 2560), ("wsd", 80), ("wo", 384)],
    4: [("win", 256), ("ab", 64), ("c", 256), ("wout", 256)],
    5: [("wq", 512), ("wk", 512), ("wv", 512), ("wo", 512), ("gain", 128), ("bias", 128)],
    6: [("wq", 512), ("wk", 512), ("wv", 512), ("wo", 512), ("gain", 128), ("bias", 128)],
    7: [("w1", 512), ("w2", 512), ("gain", 128), ("bias", 128)],
    9: [("wr", 4), ("w1", 2048), ("w2", 2048)],
    10: [("wq", 128), ("wk", 128), ("wv", 128)],
    11: [("wq", 32), ("wk", 32), ("wv", 128)],
    12: [("gate", 8), ("wi", 512), ("loraA", 256), ("loraB", 1024), ("wo", 512)],
    13: [("wq", 512), ("wk", 512), ("wv", 128), ("wo", 128)],
    14: [("wq", 1024), ("wk", 1024), ("wv", 1024), ("wo", 1024)],
    15: [("gate", 8), ("w1", 4096), ("w3", 4096), ("w2", 4096)],
}
COLS = [("L0a_b1", 4), ("L0x_bq", 4), ("L0x_bk", 4), ("L1a_bin", 2), ("L1x_fb1", 16), ("L1f_be1", 16),
        ("L2a_bq", 1), ("L2a_bk", 1), ("L2x_bq", 1), ("L2x_bk", 1), ("L2f_one", 1),
        ("L3a_bq", 4), ("L3a_bk", 4), ("L3x_bq", 8), ("L3x_bk", 8), ("block4", 4)]
ROWS = [("L0a_bout", 128), ("L0a_gamma", 128), ("L0a_beta", 128), ("L0a_b2", 128), ("L0x_bv", 128),
        ("L0x_bo", 128), ("L1a_nw", 128), ("L1a_nb", 128), ("L1a_bout", 128),
        ("L1x_gout", 128), ("L1f_be2", 512), ("L1f_br", 4), ("L2a_bv", 128), ("L2x_bv", 128),
        ("L2f_bo", 128), ("L2f_gb", 8), ("L3a_bv", 128), ("L3a_bo", 128), ("L3x_bv", 1024), ("L3x_bo", 128),
        ("tri5", 25), ("tri4", 16), ("tri8", 64)]
CONSTS = [("ident", 128), ("rot", 128), ("pair", 128), ("cos", 512), ("sin", 512), ("sincos", 512)]


def spans(spec):
    at, out = 0, {}
    for name, n in spec:
        out[name] = (at, n)
        at += n
    return out, at


WIDTH = {k: spans(v)[1] for k, v in WEIGHTS.items()}
class Roles:
    def __init__(self, sem):
        self.loaded = sem("loaded")
        self.xT_ps = sem("xT_ps")
        self.xT = sem("xT")
        self.proj = sem("proj")
        self.evac_act = sem("evac_act")
        self.evac_dve = sem("evac_dve")
        self.rot_mul = sem("rot_mul")
        self.ones = sem("ones")
        self.scores = sem("scores")
        self.negmax = sem("negmax")
        self.exped = sem("exped")
        self.probsT = sem("probsT")
        self.probsT_sb = sem("probsT_sb")
        self.unit_av = sem("unit_av")
        self.av = sem("av")
        self.normed = sem("normed")
        self.attnT = sem("attnT")
        self.attnT_sb = sem("attnT_sb")
        self.outproj = sem("outproj")
        self.out = sem("out")
        self.var = sem("var")
        self.rstd = sem("rstd")
        self.hid = sem("hid")
        self.hid_sb = sem("hid_sb")
        self.hid_dve = sem("hid_dve")
        self.part = sem("part")
        self.part_used = sem("part_used")
        self.gate = sem("gate")
        self.ready = sem("ready")
        self.early = sem("early")
        self.dve_step = sem("dve_step")
        self.act_step = sem("act_step")
        self.pool_step = sem("pool_step")


class Chain:

    def __init__(self, eng, sem):
        self.eng, self.sem, self.n = eng, sem, 0

    def inc(self, ins):
        ins.then_inc(self.sem, 1)
        self.n += 1
        return ins

    def join(self):
        if self.n:
            self.eng.wait_ge(self.sem, self.n)

    def link(self, ins):
        self.inc(ins)
        self.join()


class Table:

    def __init__(self, rows, before=None):
        self.rows, self.before = rows, before
        self.j0 = before.j1 if before else 0
        a, d = (before.a, before.d) if before else (0, 0)
        self.count = list(before.count) if before else []
        for r in rows:
            if r[3] == "A":
                a += 1
            else:
                d += 1
            self.count.append((r[3], a if r[3] == "A" else d))
        self.a, self.d, self.j1 = a, d, self.j0 + len(rows)


def build(nc, io):
    ctx = ExitStack()
    with ctx:
        def sb(name, shape, dt=F32):
            return ctx.enter_context(nc.sbuf_tensor(name, shape, dt))

        cols_at, ncols = spans(COLS)
        rows_at, nrows = spans(ROWS)
        consts_at, nconsts = spans(CONSTS)
        arena_w = [max(w for k, w in WIDTH.items() if k % 3 == a) for a in range(3)]
        arenas = [sb(f"weights{a}", [P, arena_w[a]]) for a in range(3)]
        cols = sb("cols", [P, ncols])
        scaled = sb("scaled", [P, 16])
        rows = sb("rows", [P, nrows])
        consts = sb("consts", [P, nconsts])
        relbias = sb("relbias", [P, 16, SEQ])
        X = sb("X", [P, NT, P])
        XN = sb("XN", [P, NT, P])
        XR = sb("XR", [P, NT, P])
        Z = sb("Z", [P, NT, P])
        XT = sb("XT", [P, SEQ])
        CT = sb("CT", [P, CTX])
        QT = sb("QT", [P, 8, SEQ])
        KT = sb("KT", [P, 4, SEQ])
        V = sb("V", [P, 2080])
        A = sb("A", [P, 4096])
        EX = sb("EX", [P, 2, SEQ])
        PT = sb("PT", [P, 2, SEQ])
        NB = sb("NB", [P, 2, SEQ])
        maskb = sb("maskb", [P, SEQ])
        mask_u8 = sb("mask_u8", [P, SEQ], U8)
        padm = sb("padm", [P, CTX], I32)
        padb = sb("padb", [P, 3, CTX])
        neg = sb("neg", [P, 8])
        small = sb("small", [P, 880])
        wide = A
        ps = {n: ctx.enter_context(nc.psum_tensor("ps_" + n, [P, SEQ], F32))
              for n in ("S0", "S1", "P0", "P1", "O0", "O1", "T", "OUT")}
        S = [ps["S0"], ps["S1"]]
        PP = [ps["P0"], ps["P1"]]
        O = [ps["O0"], ps["O1"]]
        TB, OUT = ps["T"], ps["OUT"]
        RING = [ps["P0"], ps["P1"], ps["O0"], ps["O1"]]

        sets = []
        for n in range(3):
            nums = []

            def sem(name):
                s = ctx.enter_context(nc.semaphore(f"{name}_{n}"))
                nums.append(s.num)
                return s

            r = Roles(sem)
            r.nums = range(min(nums), max(nums) + 1)
            assert len(r.nums) == len(nums)
            sets.append(r)
        s_boot = ctx.enter_context(nc.semaphore("boot"))
        s_boot3 = ctx.enter_context(nc.semaphore("boot_gpsimd"))
        s_boot2 = ctx.enter_context(nc.semaphore("boot_steps"))

        def C(name, c=0, n=1, parts=P):
            a = cols_at[name][0] + c
            return cols[0:parts, a:a + n]

        def R_(name, parts=P):
            a, n = rows_at[name]
            return rows[0:parts, a:a + n]

        def K(name):
            a, n = consts_at[name]
            return consts[:, a:a + n]

        ident = K("ident")

        def W(step, name):
            at, n = spans(WEIGHTS[step])[0][name]
            return arenas[step % 3][:, at:at + n]

        def tiles(ap, n=NT):
            return ap.rearrange("p (t d) -> p t d", t=n)

        ATB = [XT[:, :].rearrange("p (c d) -> p c d", c=4), XN[:, :, :]]
        flatX, flatZ, flatXN, flatXR = (t[:, :, :].rearrange("p t d -> p (t d)") for t in (X, Z, XN, XR))

        def row4(ap):
            return ap.unsqueeze(1).broadcast_to([P, NT, P])


        def load_weights(sp, r, step):
            sp.dma_start(arenas[step % 3][:, 0:WIDTH[step]], io[f"w{step}"][:, :]).then_inc(r.loaded, 16)

        def clear_previous(eng, step):
            eng.sem_clear(sets[(step - 1) % 3].nums)

        def pe_xT(pe, r, src, n=1):
            for t in range(NT):
                ins = pe.transpose(TB[:, t * P:(t + 1) * P], src[:, t, :], ident)
            ins.then_inc(r.xT_ps, 1)

        def act_xT(act, r, n=1):
            act.wait_ge(r.xT_ps, n)
            act.activation(XT[:, :], TB[:, :], ACT.Copy).then_inc(r.xT, 1)

        def pe_table(pe, r, tab):
            for j, row in enumerate(tab.rows):
                g = tab.j0 + j
                if g >= len(RING):
                    e, n = tab.count[g - len(RING)]
                    pe.wait_ge(r.evac_act if e == "A" else r.evac_dve, n)
                bank = RING[g % len(RING)]
                mms = row[0]
                for i, (lhsT, rhs) in enumerate(mms):
                    ins = pe.matmul(bank[0:row[1], 0:row[2]], lhsT, rhs, start=(i == 0), stop=(i == len(mms) - 1))
                ins.then_inc(r.proj, 1)

        def evacuate(eng, r, tab, who):
            for j, row in enumerate(tab.rows):
                if row[3] != who:
                    continue
                g = tab.j0 + j
                kind, dst, args = row[4], row[5], row[6]
                src = RING[g % len(RING)][0:row[1], 0:row[2]]
                if len(dst.shape) == 3:
                    src = src.rearrange("p (a b) -> p a b", a=dst.shape[1])
                eng.wait_ge(r.proj, g + 1)
                done = r.evac_act if who == "A" else r.evac_dve
                if kind == "act":
                    eng.activation(dst, src, args[0], bias=args[1], scale=args[2]).then_inc(done, 1)
                elif kind == "copy":
                    if who == "A":
                        eng.activation(dst, src, ACT.Copy).then_inc(done, 1)
                    else:
                        eng.tensor_copy(dst, src).then_inc(done, 1)
                elif kind == "scale":
                    eng.activation(dst, src, ACT.Copy, scale=args[0]).then_inc(done, 1)
                elif kind == "col":
                    eng.tensor_scalar(dst, src, args[0], None, ALU.add).then_inc(done, 1)
                elif kind == "row":
                    eng.tensor_tensor(dst, src, args[0], args[1]).then_inc(done, 1)

        def dve_layer_norm(dve, r, ch, n, src, dst, gain=None, shift=None):
            st, mv, ve = small[:, 0:24], small[:, 24:32], small[:, 32:36]
            for t in range(NT):
                ch.inc(dve.bn_stats(st[:, 6 * t:6 * t + 6], src[:, t, :]))
            ch.join()
            for t in range(NT):
                ch.inc(dve.bn_aggr(mv[:, 2 * t:2 * t + 2], st[:, 6 * t:6 * t + 6]))
            ch.join()
            dve.tensor_scalar(ve, mv.rearrange("p (t k) -> p t k", k=2)[:, :, 1], EPS, None,
                              ALU.add).then_inc(r.var, 1)
            dve.wait_ge(r.rstd, n)
            for t in range(NT):
                ch.inc(dve.tensor_scalar(dst[:, t, :], src[:, t, :], mv[:, 2 * t:2 * t + 1],
                                         small[:, 36 + t:37 + t], ALU.subtract, ALU.mult))
            ch.join()
            if gain is not None:
                ch.link(dve.tensor_tensor(dst[:, :, :], dst[:, :, :], row4(gain), ALU.mult))
                ch.link(dve.tensor_tensor(dst[:, :, :], dst[:, :, :], row4(shift), ALU.add))

        def pool_power(pool, r, n, half=40):
            pool.wait_ge(r.var, n)
            pool.tensor_tensor(small[:, 36:40], small[:, 32:36], small[:, half:half + 4], ALU.pow).then_inc(r.rstd, 1)

        def dve_rms_norm(dve, r, ch, n, src, dst, gain):
            for t in range(NT):
                ch.inc(dve.tensor_tensor_reduce(Z[:, t, :], src[:, t, :], src[:, t, :], 1.0, 0.0, ALU.mult, ALU.add,
                                                small[:, 48 + t:49 + t]))
            ch.join()
            dve.tensor_scalar(small[:, 32:36], small[:, 48:52], 1.0 / P, None, ALU.mult).then_inc(r.var, 1)
            dve.wait_ge(r.rstd, n)
            ch.link(dve.tensor_scalar(small[:, 52:56], small[:, 36:40], 1e-8, None, ALU.max))
            ch.link(dve.reciprocal(small[:, 56:60], small[:, 52:56]))
            for t in range(NT):
                ch.inc(dve.scalar_tensor_tensor(dst[:, t, :], src[:, t, :], small[:, 56 + t:57 + t], gain,
                                                ALU.mult, ALU.mult))
            ch.join()

        def dve_ranks(dve, ch, s, G, E, tri, rank, t1, t2):
            mine = s.unsqueeze(3).broadcast_to([P, G, E, E])
            other = s.unsqueeze(2).broadcast_to([P, G, E, E])
            lower = tri.rearrange("p (a b) -> p a b", a=E).unsqueeze(1).broadcast_to([P, G, E, E])
            a = t1[:, 0:G * E * E].rearrange("p (g e f) -> p g e f", g=G, e=E)
            b = t2[:, 0:G * E * E].rearrange("p (g e f) -> p g e f", g=G, e=E)
            ch.inc(dve.tensor_tensor(a, other, mine, ALU.is_gt))
            ch.link(dve.tensor_tensor(b, other, mine, ALU.is_equal))
            ch.link(dve.tensor_tensor(b, b, lower, ALU.mult))
            ch.link(dve.tensor_tensor(a, a, b, ALU.add))
            ch.link(dve.tensor_reduce(rank, a, AX.X, ALU.add))


        class Attention:
            def __init__(self, heads, dh, nkeys, q, k, per_unit=1, group=4, added=None, causal=False, wo=None,
                         direct=False):
                self.heads, self.dh, self.q, self.k, self.added, self.wo = heads, dh, q, k, added, wo
                self.kc = P if nkeys == SEQ else CK
                self.group, self.direct = group, direct
                self.units = []
                for qt in range(NT):
                    n = P * (qt + 1) if causal else nkeys
                    for hs in self.unit_heads(heads, dh, per_unit):
                        self.units.append((qt, hs, n))
                self.per_unit = per_unit
                self.ngroups = heads // group
                self.nch = nkeys // self.kc
                self.vv = V[0:self.kc, 0:self.nch * heads * (dh + 1)].rearrange(
                    "p (c h d) -> p c h d", c=self.nch, h=heads)
                self.width = heads * dh
                self.chunks = self.width // P
                self.last_of = {}
                for i, u in enumerate(self.units):
                    self.last_of[u[0]] = i
                self.steps = len(self.units) + 9
                self.blocks = [c for c in range(0, self.chunks, 4)]

            @staticmethod
            def unit_heads(heads, dh, per_unit):
                if per_unit == 1:
                    return [[h] for h in range(heads)]
                if dh == 64:
                    return [[h, h + 2] for a in range(0, heads, 4) for h in (a, a + 1)]
                return [[h, h + 4] for a in range(4) for h in (a, a + 8)]

            def gidx(self, i):
                qt, hs, _ = self.units[i]
                return qt * self.ngroups + hs[0] // self.group

            def first_in_group(self, i):
                return self.units[i][1][0] % self.group == 0

            def last_in_group(self, i):
                return self.units[i][1][-1] % self.group == self.group - 1

            def attn(self, qt):
                return A[:, qt * self.width:(qt + 1) * self.width]

            def pieces(self, i):
                qt, hs, n = self.units[i]
                out = []
                for a, h in enumerate(hs):
                    for c in range(n // self.kc):
                        out.append((len(out), h, c, a * n + c * self.kc))
                return out

            def pe(self, pe, r):
                n = len(self.units)
                for i in range(self.steps):
                    if i < n:
                        qt, hs, N = self.units[i]
                        if i >= 2:
                            pe.wait_ge(r.negmax if self.added else r.exped, i - 1)
                        for a, h in enumerate(hs):
                            ins = pe.matmul(S[i % 2][:, a * N:(a + 1) * N], self.q(h, qt), self.k(h)[:, 0:N],
                                            start=True, stop=True)
                        ins.then_inc(r.scores, 1)
                    u = i - 1
                    if 0 <= u < n:
                        pe.wait_ge(r.exped, u + 1)
                        if u >= 2:
                            pe.wait_ge(r.probsT_sb, u - 1)
                        for b, h, c, at in self.pieces(u):
                            ins = pe.transpose(PP[u % 2][0:self.kc, b * P:(b + 1) * P],
                                               EX[:, u % 2, at:at + self.kc], ident)
                        ins.then_inc(r.probsT, 1)
                    u = i - 2
                    if 0 <= u < n:
                        pe.wait_ge(r.probsT_sb, u + 1)
                        g = self.gidx(u)
                        if self.first_in_group(u) and g >= 2:
                            pe.wait_ge(r.normed, g - 1)
                        qt, hs, N = self.units[u]
                        for b, h, c, at in self.pieces(u):
                            hg, w = h % self.group, self.dh + 1
                            ins = pe.matmul(O[g % 2][:, hg * w:(hg + 1) * w], PT[0:self.kc, u % 2, b * P:(b + 1) * P],
                                            self.vv[:, c, h, :], start=(c == 0), stop=(c == N // self.kc - 1))
                        ins.then_inc(r.unit_av, 1)
                    if self.direct:
                        continue
                    for qt, last in self.last_of.items():
                        for m, c0 in enumerate(self.blocks):
                            k = qt * len(self.blocks) + m
                            nc4 = min(4, self.chunks)
                            if i == last + 4 + 2 * m:
                                pe.wait_ge(r.normed, (qt + 1) * self.ngroups)
                                if k >= 1:
                                    pe.wait_ge(r.attnT_sb, k)
                                for c in range(nc4):
                                    ins = pe.transpose(TB[:, c * P:(c + 1) * P],
                                                       self.attn(qt)[:, (c0 + c) * P:(c0 + c + 1) * P], ident)
                                ins.then_inc(r.attnT, 1)
                            if i == last + 5 + 2 * m:
                                pe.wait_ge(r.attnT_sb, k + 1)
                                for c in range(nc4):
                                    ins = pe.matmul(OUT[:, qt * P:(qt + 1) * P], ATB[k % 2][:, c, :],
                                                    self.wo[:, (c0 + c) * P:(c0 + c + 1) * P],
                                                    start=(c0 + c == 0), stop=(c0 + c == self.chunks - 1))
                                ins.then_inc(r.outproj, 1)

            def act(self, act, r):
                n = len(self.units)
                for i in range(self.steps):
                    if i < n:
                        qt, hs, N = self.units[i]
                        act.wait_ge(r.negmax, i + 1)
                        if i >= 2:
                            act.wait_ge(r.probsT, i - 1)
                        for a, h in enumerate(hs):
                            src = NB[:, i % 2, a * N:(a + 1) * N] if self.added else S[i % 2][:, a * N:(a + 1) * N]
                            ins = act.activation(EX[:, i % 2, a * N:(a + 1) * N], src, ACT.Exp,
                                                 bias=neg[:, 2 * (i % 4) + a:2 * (i % 4) + a + 1],
                                                 scale=-1.0 if self.added else 1.0)
                        ins.then_inc(r.exped, 1)
                    if self.direct:
                        continue
                    for qt, last in self.last_of.items():
                        for m, c0 in enumerate(self.blocks):
                            k = qt * len(self.blocks) + m
                            nc4 = min(4, self.chunks)
                            if i == last + 4 + 2 * m:
                                act.wait_ge(r.attnT, k + 1)
                                if k >= 2:
                                    act.wait_ge(r.outproj, k - 1)
                                act.activation(ATB[k % 2][:, 0:nc4, :].rearrange("p c d -> p (c d)"),
                                               TB[:, 0:nc4 * P], ACT.Copy).then_inc(r.attnT_sb, 1)

            def dve(self, dve, r, ch):
                n = len(self.units)
                for i in range(self.steps):
                    if i < n:
                        qt, hs, N = self.units[i]
                        dve.wait_ge(r.scores, i + 1)
                        if self.added and i >= 2:
                            dve.wait_ge(r.exped, i - 1)
                        elif i >= 4:
                            dve.wait_ge(r.exped, i - 3)
                        at = 2 * (i % 4)
                        if self.added:
                            for a, h in enumerate(hs):
                                ins = dve.tensor_tensor_reduce(
                                    NB[:, i % 2, a * N:(a + 1) * N], S[i % 2][:, a * N:(a + 1) * N],
                                    self.added(h, qt), -1.0, HUGE, ALU.add, ALU.min, neg[:, at + a:at + a + 1])
                        else:
                            ins = dve.tensor_reduce(neg[:, at:at + len(hs)],
                                                    S[i % 2][:, 0:len(hs) * N].rearrange("p (a k) -> p a k", k=N),
                                                    AX.X, ALU.max, negate=True)
                        ins.then_inc(r.negmax, 1)
                    u = i - 1
                    if 0 <= u < n:
                        dve.wait_ge(r.probsT, u + 1)
                        if u >= 2:
                            dve.wait_ge(r.unit_av, u - 1)
                        w = len(self.pieces(u)) * P
                        dve.tensor_copy(PT[0:self.kc, u % 2, 0:w], PP[u % 2][0:self.kc, 0:w]).then_inc(r.probsT_sb, 1)
                    u = i - 2
                    if 0 <= u < n and self.last_in_group(u):
                        g = self.gidx(u)
                        qt, hs, N = self.units[u]
                        dve.wait_ge(r.unit_av, u + 1)
                        if g >= 1:
                            dve.wait_ge(r.normed, g)
                        o = O[g % 2][:, 0:self.group * (self.dh + 1)].rearrange("p (h d) -> p h d", h=self.group)
                        rec = small[:, 64:64 + self.group]
                        ch.link(dve.reciprocal(rec, o[:, :, self.dh]))
                        gi = g % self.ngroups
                        dst = self.attn(qt)[:, gi * self.group * self.dh:(gi + 1) * self.group * self.dh]
                        dve.tensor_tensor(dst.rearrange("p (h d) -> p h d", h=self.group), o[:, :, 0:self.dh],
                                          rec.unsqueeze(2).broadcast_to([P, self.group, self.dh]),
                                          ALU.mult).then_inc(r.normed, 1)

            def result_count(self):
                return NT * len(self.blocks)

        def pool_ones(pool, r, kc, nch, heads, dh):
            vv = V[0:kc, 0:nch * heads * (dh + 1)].rearrange("p (c h d) -> p (c h) d", c=nch, h=heads)
            pool.memset(vv[:, :, dh:dh + 1], 1.0).then_inc(r.ones, 1)

        def v_cell(kc, nch, heads, dh, c):
            vv = V[0:kc, 0:nch * heads * (dh + 1)].rearrange("p (c h d) -> p c h d", c=nch, h=heads)
            return vv[:, c, :, 0:dh]

        with nc.Block() as block:
            @block.sync
            def _(sp):
                sp.dma_start(cols[:, :], io["cols"][:, :]).then_inc(s_boot, 16)
                sp.dma_start(rows[:, :], bass.AP(io["rows"].tensor, 0, [[0, P], [1, nrows]])).then_inc(s_boot, 16)
                sp.dma_start(consts[:, :], io["consts"][:, :]).then_inc(s_boot, 16)
                sp.dma_start(relbias[:, :, :].rearrange("p h k -> p (h k)"), io["reltab"][:, :]).then_inc(s_boot, 16)
                sp.dma_start(arenas[0][:, 0:WIDTH[0]], io["w0"][:, :]).then_inc(s_boot, 16)
                sp.wait_ge(s_boot, 80)

            @block.gpsimd
            def _(pool):
                pool.wait_ge(s_boot, 80)
                pool.affine_select(relbias[:, :, :], relbias[:, :, :], [[0, 16], [-1, SEQ]], ALU.is_ge, -HUGE,
                                   base=SEQ - P, channel_multiplier=1).then_inc(s_boot3, 1)
                pool.memset(small[:, 40:44], -0.5).then_inc(s_boot3, 1)
                pool.memset(small[:, 44:48], 0.5).then_inc(s_boot3, 1)
                pool.wait_ge(s_boot3, 3)

            @block.vector
            def _(dve):
                dve.wait_ge(s_boot, 80)
                a = cols_at["L0x_bq"][0]
                dve.tensor_scalar(scaled[:, 0:4], cols[:, a:a + 4], RSQRT8, None, ALU.mult).then_inc(s_boot2, 1)
                a = cols_at["L3a_bq"][0]
                dve.tensor_scalar(scaled[:, 4:8], cols[:, a:a + 4], RSQRT8, None, ALU.mult).then_inc(s_boot2, 1)
                a = cols_at["L3x_bq"][0]
                dve.tensor_scalar(scaled[:, 8:16], cols[:, a:a + 8], 0.125, None, ALU.mult).then_inc(s_boot2, 1)
                dve.wait_ge(s_boot2, 3)


        def step_load(b):
            step = 17
            r = sets[step % 3]
            with nc.Block() as block:
                @block.sync
                def _(sp):
                    clear_previous(sp, step)
                    sp.dma_start(X[:, :, :], io["x"][bass.ds(b, 1)].rearrange("o (t p) d -> p (o t) d", p=P)
                                 ).then_inc(r.loaded, 16)
                    sp.dma_start(CT[:, :], io["ctxT"][bass.ds(b, 1)].rearrange("o p k -> p (o k)")
                                 ).then_inc(r.loaded, 16)
                    sp.dma_start(mask_u8[:, :], io["mask1"][bass.ds(b, 1), :].broadcast_to([P, SEQ])
                                 ).then_inc(r.loaded, 16)
                    sp.dma_start(padm[:, :], io["mask2"][bass.ds(b, 1), :].broadcast_to([P, CTX])
                                 ).then_inc(r.loaded, 16)
                    sp.wait_ge(r.loaded, 64)

                @block.vector
                def _(dve):
                    ch = Chain(dve, r.dve_step)
                    dve.wait_ge(r.loaded, 64)
                    ch.inc(dve.tensor_scalar(maskb[:, :], mask_u8[:, :], MASKED, -MASKED, ALU.mult, ALU.add))
                    for m in range(3):
                        ins = dve.tensor_scalar(padb[:, m, :], padm[:, :], 0.0, -HUGE, ALU.is_equal, ALU.mult)
                        ins.then_inc(r.ready, 1)
                    dve.wait_ge(r.early, 2)

                @block.gpsimd
                def _(pool):
                    pool.wait_ge(r.ready, 3)
                    for m in range(2):
                        pool.affine_select(padb[:, m, :], padb[:, m, :], [[-1, CTX]], ALU.is_ge, -HUGE,
                                           base=P * m, channel_multiplier=1).then_inc(r.early, 1)
                    pool.wait_ge(r.early, 2)

        def tail(dve, r, ch, out_wait, base, n=1):
            dve.wait_ge(*out_wait)
            ch.link(dve.tensor_tensor(flatZ, OUT[:, :], base, ALU.add))
            dve_layer_norm(dve, r, ch, n, Z, X)

        def step_L0_linear_attention():
            step = 0
            r = sets[step % 3]
            w = lambda n: W(step, n)
            qT, kT = KT[:, 0, :], KT[:, 1, :]
            qf = QT[:, 0:4, :]
            kf = QT[:, 4:8, :]
            pos = wide[:, 0:4096].rearrange("p (c t) -> p c t", c=8)
            vv = V[:, 0:NT * 144].rearrange("p (t h d) -> p t h d", t=NT, h=16)
            kvb = small[:, 128:272].rearrange("p (c h d) -> p c h d", c=4, h=4)
            rowsA = [([(w("wqkv")[:, 0:128], XT[:, :])], P, SEQ, "A", "copy", qT, None),
                     ([(w("wqkv")[:, 128:256], XT[:, :])], P, SEQ, "D", "copy", kT, None)]
            rowsA += [([(XT[:, t * P:(t + 1) * P], w("wqkv")[:, 256:384])], P, P, "AD"[t % 2], "copy",
                       vv[:, t, :, 0:8], None) for t in range(NT)]
            tab = Table(rowsA)
            with nc.Block() as block:
                @block.sync
                def _(sp):
                    clear_previous(sp, step)
                    load_weights(sp, r, 1)
                    sp.wait_ge(r.loaded, 16)

                @block.gpsimd
                def _(pool):
                    pool.memset(V[:, 0:NT * 144].rearrange("p (t d) -> p t d", d=9)[:, :, 8:9], 1.0).then_inc(r.ones, 1)
                    for c in range(8):
                        pool.wait_ge(r.hid_sb, c + 1)
                        pool.wait_ge(r.hid_dve, 2 * c + 2)
                        f = qf[:, c, :] if c < 4 else kf[:, c - 4, :]
                        pool.tensor_tensor(f, f, pos[:, c, :], ALU.add).then_inc(r.ready, 1)
                    pool_power(pool, r, 1)

                @block.tensor
                def _(pe):
                    pe_xT(pe, r, X)
                    pe.wait_ge(r.xT, 1)
                    pe_table(pe, r, tab)
                    pe.wait_ge(r.evac_act, tab.a)
                    pe.wait_ge(r.evac_dve, tab.d)
                    for c in range(8):
                        if c >= 4:
                            pe.wait_ge(r.hid_dve, 2 * (c - 4) + 2)
                        if c < 4:
                            ins = pe.matmul(RING[c % 4][:, :], w("proj")[:, c * P:(c + 1) * P], qT, start=True, stop=True)
                        else:
                            t = c - 4
                            ins = pe.matmul(RING[c % 4][:, :], kT[:, t * P:(t + 1) * P], w("proj"), start=True, stop=True)
                        ins.then_inc(r.hid, 1)
                    pe.wait_ge(r.ready, 8)
                    pe.wait_ge(r.ones, 1)
                    for c in range(4):
                        for t in range(NT):
                            ins = pe.matmul(TB[:, c * 36:(c + 1) * 36], kf[:, t, c * P:(c + 1) * P],
                                            vv[:, t, 4 * c:4 * c + 4, :], start=(t == 0), stop=(t == NT - 1))
                    ins.then_inc(r.part, 1)
                    pe.wait_ge(r.part_used, 1)
                    for t in range(NT):
                        for c in range(4):
                            ins = pe.matmul(S[t % 2][:, (t // 2) * 144 + c * 36:(t // 2) * 144 + (c + 1) * 36],
                                            qf[:, c, t * P:(t + 1) * P], kvb[:, c, :, :], start=True, stop=True)
                    ins.then_inc(r.av, 1)
                    pe.wait_ge(r.normed, 4)
                    for t in range(NT):
                        ins = pe.transpose(TB[:, t * P:(t + 1) * P], XN[:, t, :], ident)
                    ins.then_inc(r.attnT, 1)
                    pe.wait_ge(r.attnT_sb, 1)
                    for t in range(NT):
                        ins = pe.matmul(OUT[:, t * P:(t + 1) * P], XT[:, t * P:(t + 1) * P], w("wout"),
                                        start=True, stop=True)
                    ins.then_inc(r.out, 1)

                @block.scalar
                def _(act):
                    act_xT(act, r)
                    evacuate(act, r, tab, "A")
                    for c in range(8):
                        act.wait_ge(r.hid_dve, 2 * c + 2)
                        f = qf[:, c, :] if c < 4 else kf[:, c - 4, :]
                        act.activation(f, f, ACT.Exp).then_inc(r.hid_sb, 1)
                    act.wait_ge(r.attnT, 1)
                    act.activation(XT[:, :], TB[:, :], ACT.Copy).then_inc(r.attnT_sb, 1)

                @block.vector
                def _(dve):
                    ch = Chain(dve, r.dve_step)
                    evacuate(dve, r, tab, "D")
                    for c in range(8):
                        dve.wait_ge(r.hid, c + 1)
                        f = qf[:, c, :] if c < 4 else kf[:, c - 4, :]
                        dve.tensor_scalar(f, RING[c % 4][:, :], 0.0, None, ALU.min).then_inc(r.hid_dve, 1)
                        dve.tensor_scalar(pos[:, c, :], RING[c % 4][:, :], 0.0, None, ALU.max).then_inc(r.hid_dve, 1)
                    dve.wait_ge(r.part, 1)
                    dve.tensor_tensor(kvb, TB[:, 0:144].rearrange("p (c h d) -> p c h d", c=4, h=4),
                                      C("block4", 0, 4).unsqueeze(1).unsqueeze(3).broadcast_to([P, 4, 4, 9]),
                                      ALU.mult).then_inc(r.part_used, 1)
                    dve.wait_ge(r.av, 1)
                    for t in range(NT):
                        o = S[t % 2][:, (t // 2) * 144:(t // 2) * 144 + 144].rearrange("p (h d) -> p h d", h=16)
                        den = small[:, 272 + 16 * t:288 + 16 * t]
                        ch.link(dve.tensor_scalar(den, o[:, :, 8], 1e-8, None, ALU.add))
                        ch.link(dve.reciprocal(den, den))
                        dve.tensor_tensor(XN[:, t, :].rearrange("p (h d) -> p h d", h=16), o[:, :, 0:8],
                                          den.unsqueeze(2).broadcast_to([P, 16, 8]), ALU.mult).then_inc(r.normed, 1)
                    ch.link(dve.tensor_tensor(Z[:, :, :], X[:, :, :], row4(R_("L0a_bout")), ALU.add))
                    dve.wait_ge(r.out, 1)
                    ch.link(dve.tensor_tensor(flatZ, OUT[:, :], flatZ, ALU.add))
                    dve_layer_norm(dve, r, ch, 1, Z, XR, R_("L0a_gamma"), R_("L0a_beta"))

        def mlp_pe(pe, r, w, act_done):
            for c in range(4):
                ins = pe.matmul(RING[c][:, :], w("w1")[:, c * P:(c + 1) * P], XT[:, :], start=True, stop=True)
                ins.then_inc(r.hid, 1)
            pe.wait_ge(act_done, 4)
            for t in range(NT):
                for c in range(4):
                    ins = pe.matmul(OUT[:, t * P:(t + 1) * P], QT[:, c, t * P:(t + 1) * P],
                                    w("w2")[:, c * P:(c + 1) * P], start=(c == 0), stop=(c == 3))
            ins.then_inc(r.out, 1)

        def step_L0_mlp():
            step = 1
            r = sets[step % 3]
            w = lambda n: W(step, n)
            with nc.Block() as block:
                @block.sync
                def _(sp):
                    clear_previous(sp, step)
                    load_weights(sp, r, 2)
                    sp.wait_ge(r.loaded, 16)

                @block.gpsimd
                def _(pool):
                    pool_power(pool, r, 1)
                    pool_power(pool, r, 2)

                @block.tensor
                def _(pe):
                    pe_xT(pe, r, XR)
                    pe.wait_ge(r.xT, 1)
                    mlp_pe(pe, r, w, r.hid_sb)

                @block.scalar
                def _(act):
                    act_xT(act, r)
                    for c in range(4):
                        act.wait_ge(r.hid, c + 1)
                        act.activation(QT[:, c, :], RING[c][:, :], ACT.Gelu, bias=C("L0a_b1", c)).then_inc(r.hid_sb, 1)

                @block.vector
                def _(dve):
                    ch = Chain(dve, r.dve_step)
                    ch.link(dve.tensor_tensor(Z[:, :, :], XR[:, :, :], row4(R_("L0a_b2")), ALU.add))
                    dve.wait_ge(r.out, 1)
                    ch.link(dve.tensor_tensor(flatZ, OUT[:, :], flatZ, ALU.add))
                    dve_layer_norm(dve, r, ch, 1, Z, XN, R_("L0a_gamma"), R_("L0a_beta"))
                    ch.link(dve.tensor_tensor(flatZ, flatX, flatXN, ALU.add))
                    dve_layer_norm(dve, r, ch, 2, Z, X)

        def padded_heads(buf):
            def q(h, qt):
                return buf[32 * (h % 4):32 * (h % 4) + 8, h // 4, qt * P:(qt + 1) * P]

            def k(h):
                return KT[32 * (h % 4):32 * (h % 4) + 8, h // 4, :]
            return q, k

        def step_L0_cross():
            step = 2
            r = sets[step % 3]
            w = lambda n: W(step, n)
            q, k = padded_heads(QT)
            att = Attention(16, 8, CTX, q, k, per_unit=2, group=16, wo=w("wo"))
            rowsA = [([(w("wq")[:, c * P:(c + 1) * P], XT[:, :])], P, SEQ, "A", "act", QT[:, c, :],
                      (ACT.Relu, scaled[:, c:c + 1], RSQRT8)) for c in range(4)]
            rowsA += [([(w("wk")[:, c * P:(c + 1) * P], CT[:, :])], P, CTX, "A", "act", KT[:, c, 0:CTX],
                       (ACT.Relu, C("L0x_bk", c), 1.0)) for c in range(4)]
            vrow = R_("L0x_bv", CK).rearrange("p (h d) -> p h d", h=16)
            rowsA += [([(CT[:, c * CK:(c + 1) * CK], w("wv"))], CK, P, "D", "row", v_cell(CK, 2, 16, 8, c),
                       (vrow, ALU.add)) for c in range(2)]
            tab = Table(rowsA)
            with nc.Block() as block:
                @block.sync
                def _(sp):
                    clear_previous(sp, step)
                    load_weights(sp, r, 3)
                    sp.wait_ge(r.loaded, 16)

                @block.gpsimd
                def _(pool):
                    pool_ones(pool, r, CK, 2, 16, 8)
                    pool_power(pool, r, 1)

                @block.tensor
                def _(pe):
                    pe_xT(pe, r, X)
                    pe.wait_ge(r.xT, 1)
                    pe_table(pe, r, tab)
                    pe.wait_ge(r.evac_act, tab.a)
                    pe.wait_ge(r.ready, 1)
                    pe.wait_ge(r.ones, 1)
                    att.pe(pe, r)

                @block.scalar
                def _(act):
                    act_xT(act, r)
                    evacuate(act, r, tab, "A")
                    att.act(act, r)

                @block.vector
                def _(dve):
                    ch = Chain(dve, r.dve_step)
                    evacuate(dve, r, tab, "D")
                    dve.wait_ge(r.evac_dve, tab.d)
                    dve.wait_ge(r.ones, 1)
                    dve.tensor_scalar(V[0:CK, 0:288], V[0:CK, 0:288], 0.0, None, ALU.max).then_inc(r.ready, 1)
                    att.dve(dve, r, ch)
                    dve.wait_ge(r.outproj, att.result_count())
                    ch.link(dve.tensor_tensor(Z[:, :, :], tiles(OUT[:, :]), row4(R_("L0x_bo")), ALU.add))
                    ch.link(dve.scalar_tensor_tensor(flatZ, flatZ, 0.0, flatX, ALU.max, ALU.add))
                    dve_layer_norm(dve, r, ch, 1, Z, X)

        def step_L0_moe_attention():
            step = 3
            r = sets[step % 3]
            w = lambda n: W(step, n)
            H, E, DH = 8, 5, 64
            order = ["q", "k", "v"]
            sig = wide[:, 0:320].rearrange("p (t n) -> p t n", t=NT)
            rank = wide[:, 320:640]
            sel = wide[:, 640:960].rearrange("p (t n) -> p t n", t=NT)
            gated = wide[:, 960:1280].rearrange("p (t n) -> p t n", t=NT)
            t1, t2 = QT[:, 0:4, :].rearrange("p a b -> p (a b)"), QT[:, 4:8, :].rearrange("p a b -> p (a b)")
            prod = [wide[:, 1280 + 512 * i:1792 + 512 * i] for i in range(5)]
            sums = NB
            q = lambda h, qt: QT[64 * (h % 2):64 * (h % 2) + 64, h // 2, qt * P:(qt + 1) * P]
            k = lambda h: KT[64 * (h % 2):64 * (h % 2) + 64, h // 2, :]
            att = Attention(H, DH, SEQ, q, k, direct=True)
            att.attn = lambda qt: L0F_out[:, qt, :]
            L0F_out = wide[:, 1280:3328].rearrange("p (t n) -> p t n", t=NT)
            wsrc = {"q": w("wq"), "k": w("wk"), "v": w("wv")}
            with nc.Block() as block:
                @block.sync
                def _(sp):
                    clear_previous(sp, step)
                    load_weights(sp, r, 4)
                    sp.wait_ge(r.loaded, 16)

                @block.gpsimd
                def _(pool):
                    pool_ones(pool, r, P, NT, H, DH)
                    for i in range(NT * 3):
                        pool.wait_ge(r.part_used, 5 * (i + 1))
                        for e in range(1, 4):
                            pool.tensor_tensor(prod[0], prod[0], prod[e], ALU.add).then_inc(r.pool_step, 1)
                            pool.wait_ge(r.pool_step, 3 * i + e)
                        dst = v_cell(P, NT, H, DH, i // 3) if i % 3 == 2 else \
                            sums[:, i % 3, :].rearrange("p (h d) -> p h d", h=H)
                        if i % 3 == 0 and i >= 3:
                            pool.wait_ge(r.attnT, 2 * (i // 3) - 1)
                        if i % 3 == 1 and i >= 3:
                            pool.wait_ge(r.attnT, 2 * (i // 3))
                        pool.tensor_tensor(dst, prod[0].rearrange("p (h d) -> p h d", h=H),
                                           prod[4].rearrange("p (h d) -> p h d", h=H), ALU.add).then_inc(r.ready, 1)
                    pool_power(pool, r, 1)

                def _turn(pe, t, m):
                    k_ = 2 * t + m
                    pe.wait_ge(r.ready, 3 * t + m + 1)
                    if k_ >= 1:
                        pe.wait_ge(r.attnT_sb, k_)
                    for c in range(4):
                        ins = pe.transpose(TB[:, c * P:(c + 1) * P], sums[:, m, c * P:(c + 1) * P], ident)
                    ins.then_inc(r.attnT, 1)

                @block.tensor
                def _(pe):
                    pe_xT(pe, r, X)
                    pe.wait_ge(r.xT, 1)
                    for t in range(NT):
                        ins = pe.matmul(OUT[:, t * 80:(t + 1) * 80], XT[:, t * P:(t + 1) * P], w("wsd"),
                                        start=True, stop=True)
                    ins.then_inc(r.gate, 1)
                    n = 0
                    for t in range(NT):
                        for m, name in enumerate(order):
                            ws = wsrc[name].rearrange("p (h e d) -> p h e d", h=H, e=E)
                            for e in range(E):
                                if n >= 4:
                                    pe.wait_ge(r.part_used, n - 3)
                                pe.matmul(RING[n % 4][:, :], XT[:, t * P:(t + 1) * P], ws[:, :, e, :],
                                          start=True, stop=True).then_inc(r.part, 1)
                                n += 1
                            if m >= 1:
                                _turn(pe, t, m - 1)
                    pe.wait_ge(r.ready, NT * 3)
                    pe.wait_ge(r.attnT_sb, 2 * NT)
                    pe.wait_ge(r.ones, 1)
                    att.pe(pe, r)
                    for qt in range(NT):
                        pe.wait_ge(r.hid_dve, qt + 1)
                        if qt >= 1:
                            pe.wait_ge(r.hid_sb, qt)
                        for c in range(3):
                            n = 128 if c < 2 else 64
                            ins = pe.transpose(S[qt % 2][0:n, c * P:(c + 1) * P],
                                               NB[:, qt % 2, c * P:c * P + n], ident)
                        ins.then_inc(r.hid, 1)
                        pe.wait_ge(r.hid_sb, qt + 1)
                        for c in range(3):
                            n = 128 if c < 2 else 64
                            ins = pe.matmul(OUT[:, qt * P:(qt + 1) * P], PT[0:n, qt % 2, c * P:(c + 1) * P],
                                            w("wo")[0:n, c * P:(c + 1) * P], start=(c == 0), stop=(c == 2))
                        ins.then_inc(r.outproj, 1)

                @block.scalar
                def _(act):
                    act_xT(act, r)
                    act.wait_ge(r.gate, 1)
                    act.activation(sig, OUT[:, 0:320].rearrange("p (t n) -> p t n", t=NT), ACT.Sigmoid
                                   ).then_inc(r.act_step, 1)
                    for t in range(NT):
                        for m in range(2):
                            act.wait_ge(r.attnT, 2 * t + m + 1)
                            if t == 0 and m == 0:
                                act.wait_ge(r.gate, 2)
                            dst = (QT if m == 0 else KT)[:, 0:4, t * P:(t + 1) * P]
                            act.activation(dst, TB[:, :].rearrange("p (c d) -> p c d", c=4), ACT.Copy
                                           ).then_inc(r.attnT_sb, 1)
                    att.act(act, r)
                    for qt in range(NT):
                        act.wait_ge(r.hid, qt + 1)
                        if qt >= 2:
                            act.wait_ge(r.outproj, qt - 1)
                        act.activation(PT[:, qt % 2, 0:256], S[qt % 2][:, 0:256], ACT.Copy)
                        act.activation(PT[0:64, qt % 2, 256:384], S[qt % 2][0:64, 256:384], ACT.Copy
                                       ).then_inc(r.hid_sb, 1)

                @block.vector
                def _(dve):
                    ch = Chain(dve, r.dve_step)
                    dve.wait_ge(r.act_step, 1)
                    s3 = sig.rearrange("p t (g e) -> p (t g) e", e=E)
                    r3 = rank.rearrange("p (g e) -> p g e", e=E)
                    for g0 in range(0, 64, 32):
                        dve_ranks(dve, ch, s3[:, g0:g0 + 32, :], 32, E, R_("tri5"), r3[:, g0:g0 + 32, :], t1, t2)
                    ch.link(dve.tensor_scalar(sel.rearrange("p t n -> p (t n)"), rank, 2.5, None, ALU.is_lt))
                    ch.link(dve.tensor_tensor(gated, sig, sel, ALU.mult))
                    dve.tensor_scalar(gated[:, :, 40:80], gated[:, :, 40:80], DH ** -0.5, None, ALU.mult
                                      ).then_inc(r.gate, 1)
                    dve.wait_ge(r.gate, 2)
                    n = 0
                    for t in range(NT):
                        for m, name in enumerate(order):
                            g = gated[:, t, 40:80] if name == "q" else gated[:, t, 0:40]
                            g = g.rearrange("p (h e) -> p h e", e=E)
                            if n >= 5:
                                dve.wait_ge(r.ready, n // 5)
                            for e in range(E):
                                dve.wait_ge(r.part, n + 1)
                                dve.tensor_tensor(prod[e].rearrange("p (h d) -> p h d", h=H),
                                                  RING[n % 4][:, :].rearrange("p (h d) -> p h d", h=H),
                                                  g[:, :, e].unsqueeze(2).broadcast_to([P, H, DH]),
                                                  ALU.mult).then_inc(r.part_used, 1)
                                n += 1
                    dve.wait_ge(r.ready, 3 * NT)
                    att.dve(dve, r, ch)
                    dve.wait_ge(r.normed, NT * 2)
                    md = sel[:, :, 40:80].rearrange("p t (h e) -> p t h e", e=E)
                    for qt in range(NT):
                        o = L0F_out[:, qt, :].rearrange("p (h d) -> p h d", h=H)
                        if qt >= 1:
                            dve.wait_ge(r.hid_dve, qt)
                        if qt >= 2:
                            dve.wait_ge(r.hid, qt - 1)
                        for e in range(E):
                            tmp = EX[:, e % 2, :].rearrange("p (h d) -> p h d", h=H)
                            ch.link(dve.tensor_tensor(tmp, o, md[:, qt, :, e].unsqueeze(2).broadcast_to([P, H, DH]),
                                                      ALU.mult))
                            ins = dve.tensor_reduce(NB[:, qt % 2, e * DH:(e + 1) * DH],
                                                    tmp.rearrange("p h d -> p d h"), AX.X, ALU.add)
                            if e == E - 1:
                                ins.then_inc(r.hid_dve, 1)
                            else:
                                ch.inc(ins)
                    tail(dve, r, ch, (r.outproj, NT), flatX)

        def step_L1_ssm():
            step = 4
            r = sets[step % 3]
            w = lambda n: W(step, n)
            tab = Table([([(w("win")[:, c * P:(c + 1) * P], XT[:, :])], P, SEQ, "AD"[c], "act" if c == 0 else "col",
                          QT[:, c, :], (ACT.Identity, C("L1a_bin", c), 1.0) if c == 0 else (C("L1a_bin", c),))
                         for c in range(2)])
            states = QT[0:16, 5, :]
            with nc.Block() as block:
                @block.sync
                def _(sp):
                    clear_previous(sp, step)
                    load_weights(sp, r, 5)
                    sp.wait_ge(r.loaded, 16)

                @block.gpsimd
                def _(pool):
                    pool_power(pool, r, 1)
                    pool_power(pool, r, 2)

                @block.tensor
                def _(pe):
                    pe.wait_ge(r.ready, 1)
                    pe_xT(pe, r, XN)
                    pe.wait_ge(r.xT, 1)
                    pe_table(pe, r, tab)
                    pe.wait_ge(r.evac_act, 1)
                    pe.wait_ge(r.evac_dve, 1)
                    for m in range(2):
                        for c in range(2):
                            ins = pe.matmul(S[m][0:16, :], w("ab")[:, 32 * c + 16 * m:32 * c + 16 * m + 16],
                                            QT[:, c, :], start=(c == 0), stop=(c == 1))
                    ins.then_inc(r.hid, 1)
                    pe.wait_ge(r.hid_dve, 1)
                    for c in range(2):
                        ins = pe.matmul(PP[c][:, :], w("c")[0:16, c * P:(c + 1) * P], states, start=True, stop=True)
                    ins.then_inc(r.part, 1)
                    pe.wait_ge(r.part_used, 2)
                    for t in range(NT):
                        for c in range(2):
                            ins = pe.matmul(OUT[:, t * P:(t + 1) * P], QT[:, 2 + c, t * P:(t + 1) * P],
                                            w("wout")[:, c * P:(c + 1) * P], start=(c == 0), stop=(c == 1))
                    ins.then_inc(r.out, 1)

                @block.scalar
                def _(act):
                    act_xT(act, r)
                    evacuate(act, r, tab, "A")
                    act.wait_ge(r.hid, 1)
                    act.activation(QT[0:16, 4, :], S[0][0:16, :], ACT.Sigmoid).then_inc(r.hid_sb, 1)
                    act.wait_ge(r.part, 1)
                    for c in range(2):
                        act.activation(QT[:, 2 + c, :], PP[c][:, :], ACT.Copy).then_inc(r.part_used, 1)

                @block.vector
                def _(dve):
                    ch = Chain(dve, r.dve_step)
                    dve_layer_norm(dve, r, ch, 1, X, XN, R_("L1a_nw"), R_("L1a_nb"))
                    dve.sem_inc(r.ready, 1)
                    evacuate(dve, r, tab, "D")
                    dve.wait_ge(r.hid_sb, 1)
                    dve.wait_ge(r.hid, 1)
                    dve.tensor_tensor_scan(states, QT[0:16, 4, :], S[1][0:16, :], 0.0, ALU.mult, ALU.add
                                           ).then_inc(r.hid_dve, 1)
                    ch.link(dve.scalar_tensor_tensor(Z[:, :, :], X[:, :, :], 2.0, row4(R_("L1a_bout")),
                                                     ALU.mult, ALU.add))
                    tail(dve, r, ch, (r.out, 1), flatZ, 2)
                    ch.link(dve.tensor_copy(flatXR, flatX))

        def heads64(h, qt):
            return QT[64 * (h % 2):64 * (h % 2) + 64, h // 2, qt * P:(qt + 1) * P]

        def keys64(h):
            return KT[64 * (h % 2):64 * (h % 2) + 64, h // 2, :]

        def step_L1_attention(l, cross):
            step = 6 if cross else 5
            r = sets[step % 3]
            w = lambda n: W(step, n)
            NK = CTX if cross else SEQ
            src = CT if cross else XT
            kc, nch = (CK, 2) if cross else (P, NT)
            raw = wide[:, 0:4096].rearrange("p (c t) -> p c t", c=8)
            gain, bias = w("gain"), w("bias")
            added = None if cross else (lambda h, qt: maskb[:, :])
            att = Attention(8, 64, NK, heads64, keys64, per_unit=2 if cross else 1, added=added, wo=w("wo"))
            rowsA = [([(w("wq")[:, c * P:(c + 1) * P], XT[:, :])], P, SEQ, "A", "scale", raw[:, c, :], (0.125,))
                     for c in range(4)]
            rowsA += [([(w("wk")[:, c * P:(c + 1) * P], src[:, :])], P, NK, "A", "copy", raw[:, 4 + c, 0:NK], None)
                      for c in range(4)]
            tab = Table(rowsA)
            tab2 = Table([([(K("rot"), raw[:, c, 0:(SEQ if c < 4 else NK)])], P, SEQ if c < 4 else NK, "D", "row",
                           (QT[:, c, :] if c < 4 else KT[:, c - 4, 0:NK]),
                           (K("sin")[:, 0:(SEQ if c < 4 else NK)], ALU.mult)) for c in range(8)], tab)
            tab3 = Table([([(src[:, c * kc:(c + 1) * kc], w("wv"))], kc, SEQ, "A", "copy",
                           v_cell(kc, nch, 8, 64, c), None) for c in range(nch)], tab2)
            with nc.Block() as block:
                @block.sync
                def _(sp):
                    clear_previous(sp, step)
                    nxt = step + 1
                    sp.dma_start(arenas[nxt % 3][:, 0:WIDTH[nxt]],
                                 io[f"w{nxt}"][bass.ds(l, 1)].rearrange("o p n -> p (o n)")).then_inc(r.loaded, 16)
                    sp.wait_ge(r.loaded, 16)

                @block.gpsimd
                def _(pool):
                    pool_ones(pool, r, kc, nch, 8, 64)
                    pool_power(pool, r, 1, 44)
                    for c in range(8):
                        n = SEQ if c < 4 else NK
                        pool.wait_ge(r.evac_act, c + 1)
                        pool.wait_ge(r.proj, 9 + c)
                        pool.tensor_tensor(raw[:, c, 0:n], raw[:, c, 0:n], K("cos")[:, 0:n], ALU.mult
                                           ).then_inc(r.rot_mul, 1)

                @block.tensor
                def _(pe):
                    pe.wait_ge(r.early, 1)
                    pe_xT(pe, r, XN)
                    pe.wait_ge(r.xT, 1)
                    pe_table(pe, r, tab)
                    pe.wait_ge(r.evac_act, tab.a)
                    pe_table(pe, r, tab2)
                    pe_table(pe, r, tab3)
                    pe.wait_ge(r.ready, 8)
                    pe.wait_ge(r.evac_act, tab3.a)
                    pe.wait_ge(r.ones, 1)
                    att.pe(pe, r)

                @block.scalar
                def _(act):
                    act_xT(act, r)
                    evacuate(act, r, tab, "A")
                    evacuate(act, r, tab3, "A")
                    att.act(act, r)

                @block.vector
                def _(dve):
                    ch = Chain(dve, r.dve_step)
                    dve_rms_norm(dve, r, ch, 1, X, XN, gain)
                    dve.sem_inc(r.early, 1)
                    evacuate(dve, r, tab2, "D")
                    for c in range(8):
                        n = SEQ if c < 4 else NK
                        dst = QT[:, c, :] if c < 4 else KT[:, c - 4, 0:NK]
                        dve.wait_ge(r.evac_dve, c + 1)
                        dve.wait_ge(r.rot_mul, c + 1)
                        dve.tensor_tensor(dst, dst, raw[:, c, 0:n], ALU.add).then_inc(r.ready, 1)
                    att.dve(dve, r, ch)
                    ch.link(dve.tensor_tensor(X[:, :, :], X[:, :, :], row4(bias), ALU.add))
                    dve.wait_ge(r.outproj, att.result_count())
                    ch.link(dve.tensor_tensor(flatX, OUT[:, :], flatX, ALU.add))

        def step_L1_mlp(l):
            step = 7
            r = sets[step % 3]
            w = lambda n: W(step, n)
            gain, bias = w("gain"), w("bias")
            with nc.Block() as block:
                @block.sync
                def _(sp):
                    clear_previous(sp, step)
                    sp.dma_start(arenas[2][:, 0:WIDTH[5]],
                                 io["w5next"][bass.ds(l, 1)].rearrange("o p n -> p (o n)")).then_inc(r.loaded, 16)
                    sp.wait_ge(r.loaded, 16)

                @block.gpsimd
                def _(pool):
                    pool_power(pool, r, 1, 44)

                @block.tensor
                def _(pe):
                    pe.wait_ge(r.early, 1)
                    pe_xT(pe, r, XN)
                    pe.wait_ge(r.xT, 1)
                    mlp_pe(pe, r, w, r.hid_sb)

                @block.scalar
                def _(act):
                    act_xT(act, r)
                    for c in range(4):
                        act.wait_ge(r.hid, c + 1)
                        act.activation(QT[:, c, :], RING[c][:, :], ACT.Gelu,
                                       bias=cols[:, bass.ds(cols_at["L1x_fb1"][0] + c + 4 * l, 1)]
                                       ).then_inc(r.hid_sb, 1)

                @block.vector
                def _(dve):
                    ch = Chain(dve, r.dve_step)
                    dve_rms_norm(dve, r, ch, 1, X, XN, gain)
                    dve.sem_inc(r.early, 1)
                    ch.link(dve.tensor_tensor(X[:, :, :], X[:, :, :], row4(bias), ALU.add))
                    dve.wait_ge(r.out, 1)
                    ch.link(dve.tensor_tensor(flatX, OUT[:, :], flatX, ALU.add))

        def step_L1_final():
            step = 8
            r = sets[step % 3]
            with nc.Block() as block:
                @block.sync
                def _(sp):
                    clear_previous(sp, step)
                    load_weights(sp, r, 9)
                    sp.wait_ge(r.loaded, 16)

                @block.gpsimd
                def _(pool):
                    pool_power(pool, r, 1, 44)
                    pool_power(pool, r, 2)

                @block.vector
                def _(dve):
                    ch = Chain(dve, r.dve_step)
                    dve_rms_norm(dve, r, ch, 1, X, XN, R_("L1x_gout"))
                    ch.link(dve.tensor_tensor(flatXN, flatXN, flatXR, ALU.add))
                    dve_layer_norm(dve, r, ch, 2, XN, X)

        def step_experts(step, E, swiglu):
            r = sets[step % 3]
            w = lambda n: W(step, n)
            gname = "gate" if swiglu else "wr"
            gates = small[:, 512:512 + NT * E]
            g3 = gates.rearrange("p (t e) -> p t e", e=E)
            acc = XN
            per = 8 if swiglu else 4
            hid = lambda e: QT[:, 4 * (e % 2):4 * (e % 2) + 4, :]
            with nc.Block() as block:
                @block.sync
                def _(sp):
                    clear_previous(sp, step)
                    if step == 9:
                        load_weights(sp, r, 10)
                        sp.wait_ge(r.loaded, 16)

                @block.gpsimd
                def _(pool):
                    pool_power(pool, r, 1)

                @block.tensor
                def _(pe):
                    pe_xT(pe, r, X)
                    pe.wait_ge(r.xT, 1)
                    for t in range(NT):
                        ins = pe.matmul(TB[:, t * E:(t + 1) * E], XT[:, t * P:(t + 1) * P], w(gname),
                                        start=True, stop=True)
                    ins.then_inc(r.gate, 1)
                    n = 0
                    for e in range(E + 1):
                        if e < E:
                            for c in range(4):
                                for m in range(2 if swiglu else 1):
                                    src = w("w3") if m else w("w1")
                                    if n >= 4:
                                        pe.wait_ge(r.part_used, n - 3)
                                    pe.matmul(RING[n % 4][:, :], src[:, e * 512 + c * P:e * 512 + (c + 1) * P],
                                              XT[:, :], start=True, stop=True).then_inc(r.part, 1)
                                    n += 1
                        if e >= 1:
                            f = e - 1
                            pe.wait_ge(r.hid_sb, 4 * e)
                            if f >= 2:
                                pe.wait_ge(r.hid_dve, f - 1)
                            for t in range(NT):
                                for c in range(4):
                                    ins = pe.matmul(S[f % 2][:, t * P:(t + 1) * P],
                                                    hid(f)[:, c, t * P:(t + 1) * P],
                                                    w("w2")[:, f * 512 + c * P:f * 512 + (c + 1) * P],
                                                    start=(c == 0), stop=(c == 3))
                            ins.then_inc(r.out, 1)

                if swiglu:
                    @block.scalar
                    def _(act):
                        act_xT(act, r)
                        act.wait_ge(r.gate, 2)
                        act.activation(small[:, 640:648], small[:, 600:608], ACT.Sigmoid).then_inc(r.act_step, 1)
                        for e in range(E):
                            for c in range(4):
                                n = 8 * e + 2 * c
                                act.wait_ge(r.part, n + 1)
                                if n >= 4:
                                    act.wait_ge(r.hid_sb, n // 2 - 1)
                                act.activation(NB[:, (n // 2) % 2, :], RING[n % 4][:, :], ACT.Silu
                                               ).then_inc(r.ready, 1)
                else:
                    @block.scalar
                    def _(act):
                        act_xT(act, r)
                        for e in range(E):
                            for c in range(4):
                                n = 4 * e + c
                                act.wait_ge(r.part, n + 1)
                                if e >= 2 and c == 0:
                                    act.wait_ge(r.out, e - 1)
                                act.activation(hid(e)[:, c, :], RING[n % 4][:, :], ACT.Relu,
                                               bias=C("L1f_be1", n)).then_inc(r.part_used, 1)
                                act.wait_ge(r.part_used, n + 1)
                                act.sem_inc(r.hid_sb, 1)

                @block.vector
                def _(dve):
                    ch = Chain(dve, r.dve_step)
                    lg, rank = small[:, 544:544 + NT * E], small[:, 608:608 + 32]
                    l3, r3 = lg.rearrange("p (t e) -> p t e", e=E), rank[:, 0:NT * E].rearrange("p (t e) -> p t e", e=E)
                    if swiglu:
                        lg = small[:, 704:704 + NT * E]
                        l3 = lg.rearrange("p (t e) -> p t e", e=E)
                        rank = small[:, 740:740 + NT * E]
                        r3 = rank.rearrange("p (t e) -> p t e", e=E)
                    t1, t2 = wide[:, 0:512], wide[:, 512:1024]
                    dve.wait_ge(r.gate, 1)
                    if swiglu:
                        ch.link(dve.tensor_copy(lg, TB[:, 0:NT * E]))
                    else:
                        ch.link(dve.tensor_tensor(l3, TB[:, 0:NT * E].rearrange("p (t e) -> p t e", e=E),
                                                  R_("L1f_br").unsqueeze(1).broadcast_to([P, NT, E]), ALU.add))
                    dve_ranks(dve, ch, l3, NT, E, R_("tri8" if swiglu else "tri4"), r3, t1, t2)
                    if swiglu:
                        first, second = small[:, 780:812], small[:, 820:852]
                        ch.inc(dve.tensor_scalar(first, rank, 0.0, None, ALU.is_equal))
                        ch.link(dve.tensor_scalar(second, rank, 1.0, None, ALU.is_equal))
                        fl, sl = wide[:, 1024:1056], wide[:, 1056:1088]
                        ch.inc(dve.tensor_tensor(fl, first, lg, ALU.mult))
                        ch.link(dve.tensor_tensor(sl, second, lg, ALU.mult))
                        v12 = wide[:, 1088:1096]
                        ch.inc(dve.tensor_reduce(v12[:, 0:4], fl.rearrange("p (t e) -> p t e", e=E), AX.X, ALU.add))
                        ch.link(dve.tensor_reduce(v12[:, 4:8], sl.rearrange("p (t e) -> p t e", e=E), AX.X, ALU.add))
                        ch.inc(dve.tensor_tensor(small[:, 600:604], v12[:, 0:4], v12[:, 4:8], ALU.subtract))
                        dve.tensor_tensor(small[:, 604:608], v12[:, 4:8], v12[:, 0:4], ALU.subtract).then_inc(r.gate, 1)
                        dve.wait_ge(r.act_step, 1)
                        ch.inc(dve.tensor_tensor(first.rearrange("p (t e) -> p t e", e=E),
                                                 first.rearrange("p (t e) -> p t e", e=E),
                                                 small[:, 640:644].unsqueeze(2).broadcast_to([P, NT, E]), ALU.mult))
                        ch.link(dve.tensor_tensor(second.rearrange("p (t e) -> p t e", e=E),
                                                  second.rearrange("p (t e) -> p t e", e=E),
                                                  small[:, 644:648].unsqueeze(2).broadcast_to([P, NT, E]), ALU.mult))
                        ch.link(dve.tensor_tensor(gates, first, second, ALU.add))
                    else:
                        ch.link(dve.tensor_scalar(gates, rank[:, 0:NT * E], 0.0, None, ALU.is_equal))
                    ch.link(dve.tensor_copy(flatZ, flatX))
                    for e in range(E + 1):
                        if swiglu and e < E:
                            for c in range(4):
                                n = 8 * e + 2 * c
                                if e >= 2 and c == 0:
                                    dve.wait_ge(r.out, e - 1)
                                dve.wait_ge(r.ready, n // 2 + 1)
                                dve.wait_ge(r.part, n + 2)
                                dve.tensor_tensor(hid(e)[:, c, :], RING[(n + 1) % 4][:, :], NB[:, (n // 2) % 2, :],
                                                  ALU.mult).then_inc(r.hid_sb, 1)
                                dve.wait_ge(r.hid_sb, n // 2 + 1)
                                dve.sem_inc(r.part_used, 2)
                        if e < 1:
                            continue
                        f = e - 1
                        dve.wait_ge(r.out, e)
                        src = S[f % 2]
                        if not swiglu:
                            tmp = wide[:, 2048:2560]
                            ch.link(dve.tensor_tensor(tiles(tmp), tiles(src[:, :]),
                                                      row4(R_("L1f_be2")[:, f * P:(f + 1) * P]), ALU.add))
                            src = tmp
                        for t in range(NT):
                            ins = dve.scalar_tensor_tensor(Z[:, t, :], src[:, t * P:(t + 1) * P],
                                                           g3[:, t, f:f + 1], Z[:, t, :], ALU.mult, ALU.add)
                            ch.inc(ins)
                        ch.join()
                        dve.sem_inc(r.hid_dve, 1)
                    dve_layer_norm(dve, r, ch, 1, Z, X)

        def step_L2_attention():
            step = 10
            r = sets[step % 3]
            w = lambda n: W(step, n)
            att = Attention(1, P, SEQ, lambda h, qt: QT[:, 0, qt * P:(qt + 1) * P], lambda h: KT[:, 0, :], group=1,
                            direct=True)
            tab = Table([([(w("wq"), XT[:, :])], P, SEQ, "A", "act", QT[:, 1, :], (ACT.Identity, C("L2a_bq"), 1.0)),
                         ([(w("wk"), XT[:, :])], P, SEQ, "D", "col", KT[:, 1, :], (C("L2a_bk"),))]
                        + [([(XT[:, t * P:(t + 1) * P], w("wv"))], P, P, "D", "row", v_cell(P, NT, 1, P, t)[:, 0, :],
                            (R_("L2a_bv"), ALU.add)) for t in range(NT)])
            tab2 = Table([([(K("pair"), QT[:, 1, :])], P, SEQ, "D", "row", QT[:, 2, :], (K("sincos"), ALU.mult)),
                          ([(K("pair"), KT[:, 1, :])], P, SEQ, "D", "row", KT[:, 0, :], (K("sincos"), ALU.mult))], tab)
            with nc.Block() as block:
                @block.sync
                def _(sp):
                    clear_previous(sp, step)
                    load_weights(sp, r, 11)
                    sp.wait_ge(r.loaded, 16)

                @block.gpsimd
                def _(pool):
                    pool_ones(pool, r, P, NT, 1, P)
                    pool.wait_ge(r.evac_dve, tab2.d)
                    pool.tensor_scalar(QT[:, 0, :], QT[:, 2, :], 0.125, None, ALU.mult).then_inc(r.ready, 1)
                    pool_power(pool, r, 1)

                @block.tensor
                def _(pe):
                    pe_xT(pe, r, X)
                    pe.wait_ge(r.xT, 1)
                    pe_table(pe, r, tab)
                    pe.wait_ge(r.evac_act, tab.a)
                    pe.wait_ge(r.evac_dve, tab.d)
                    pe_table(pe, r, tab2)
                    pe.wait_ge(r.evac_dve, tab2.d)
                    pe.wait_ge(r.ready, 1)
                    pe.wait_ge(r.ones, 1)
                    att.pe(pe, r)

                @block.scalar
                def _(act):
                    act_xT(act, r)
                    evacuate(act, r, tab, "A")
                    att.act(act, r)

                @block.vector
                def _(dve):
                    ch = Chain(dve, r.dve_step)
                    evacuate(dve, r, tab, "D")
                    evacuate(dve, r, tab2, "D")
                    att.dve(dve, r, ch)
                    dve.wait_ge(r.normed, NT)
                    ch.link(dve.tensor_tensor(flatZ, A[:, 0:SEQ], flatX, ALU.add))
                    dve_layer_norm(dve, r, ch, 1, Z, X)

        def step_L2_sigmoid_attention():
            step = 11
            r = sets[step % 3]
            w = lambda n: W(step, n)
            tab = Table([([(w("wq"), XT[:, :])], 32, SEQ, "A", "act", QT[0:32, 0, :],
                          (ACT.Identity, C("L2x_bq", parts=32), 1.0)),
                         ([(w("wk"), CT[:, :])], 32, CTX, "D", "col", KT[0:32, 0, 0:CTX], (C("L2x_bk", parts=32),))]
                        + [([(CT[:, c * CK:(c + 1) * CK], w("wv"))], CK, P, "D", "row", V[0:CK, c * P:(c + 1) * P],
                            (R_("L2x_bv", CK), ALU.add)) for c in range(2)])
            with nc.Block() as block:
                @block.sync
                def _(sp):
                    clear_previous(sp, step)
                    load_weights(sp, r, 12)
                    sp.wait_ge(r.loaded, 16)

                @block.gpsimd
                def _(pool):
                    pool_power(pool, r, 1)

                @block.tensor
                def _(pe):
                    pe_xT(pe, r, X)
                    pe.wait_ge(r.xT, 1)
                    pe_table(pe, r, tab)
                    pe.wait_ge(r.evac_act, tab.a)
                    pe.wait_ge(r.evac_dve, tab.d)
                    for c in range(2):
                        ins = pe.matmul(S[c][0:CK, :], KT[0:32, 0, c * CK:(c + 1) * CK], QT[0:32, 0, :],
                                        start=True, stop=True)
                        ins.then_inc(r.scores, 1)
                    pe.wait_ge(r.exped, 2)
                    for t in range(NT):
                        for c in range(2):
                            ins = pe.matmul(OUT[:, t * P:(t + 1) * P], EX[0:CK, c, t * P:(t + 1) * P],
                                            V[0:CK, c * P:(c + 1) * P], start=(c == 0), stop=(c == 1))
                    ins.then_inc(r.out, 1)

                @block.scalar
                def _(act):
                    act_xT(act, r)
                    evacuate(act, r, tab, "A")
                    for c in range(2):
                        act.wait_ge(r.scores, c + 1)
                        act.activation(EX[0:CK, c, :], S[c][0:CK, :], ACT.Sigmoid, scale=32.0 ** -0.5).then_inc(r.exped, 1)

                @block.vector
                def _(dve):
                    ch = Chain(dve, r.dve_step)
                    evacuate(dve, r, tab, "D")
                    tail(dve, r, ch, (r.out, 1), flatX)

        def step_L2_lora_experts():
            step = 12
            r = sets[step % 3]
            w = lambda n: W(step, n)
            E = 8
            hsum = wide[:, 0:2048].rearrange("p (t f) -> p t f", t=NT)
            part = [wide[:, 2048 + 512 * i:2560 + 512 * i] for i in range(2)]
            gates = small[:, 512:544]
            g3 = gates.rearrange("p (t e) -> p t e", e=E)
            tab = Table([([(w("loraA")[:, c * P:(c + 1) * P], XT[:, :])], P, SEQ, "D", "col", QT[:, c, :],
                          (C("L2f_one"),)) for c in range(2)])
            with nc.Block() as block:
                @block.sync
                def _(sp):
                    clear_previous(sp, step)
                    load_weights(sp, r, 13)
                    sp.wait_ge(r.loaded, 16)

                @block.gpsimd
                def _(pool):
                    for n in range(NT * E):
                        t, e = n % NT, n // NT
                        pool.wait_ge(r.hid_sb, n + 1)
                        if e == 0:
                            pool.tensor_copy(hsum[:, t, :], part[n % 2]).then_inc(r.ready, 1)
                        else:
                            pool.wait_ge(r.ready, n - NT + 1)
                            pool.tensor_tensor(hsum[:, t, :], hsum[:, t, :], part[n % 2], ALU.add).then_inc(r.ready, 1)
                    pool_power(pool, r, 1)

                @block.tensor
                def _(pe):
                    pe_xT(pe, r, X)
                    pe.wait_ge(r.xT, 1)
                    for t in range(NT):
                        ins = pe.matmul(TB[:, t * E:(t + 1) * E], XT[:, t * P:(t + 1) * P], w("gate"),
                                        start=True, stop=True)
                    ins.then_inc(r.gate, 1)
                    pe_table(pe, r, tab)
                    pe.wait_ge(r.evac_dve, tab.d)
                    for n in range(NT * E):
                        t, e = n % NT, n // NT
                        if n >= 4:
                            pe.wait_ge(r.hid_sb, n - 3)
                        j, c = e % 4, e // 4
                        pe.matmul(RING[n % 4][:, :], XT[:, t * P:(t + 1) * P], w("wi"), start=True, stop=False)
                        pe.matmul(RING[n % 4][:, :], QT[32 * j:32 * j + 17, c, t * P:(t + 1) * P],
                                  w("loraB")[32 * j:32 * j + 17, c * 512:(c + 1) * 512],
                                  start=False, stop=True).then_inc(r.hid, 1)
                    pe.wait_ge(r.gate, 3)
                    for t in range(NT):
                        pe.wait_ge(r.ready, NT * (E - 1) + t + 1)
                        if t >= 2:
                            pe.wait_ge(r.attnT_sb, t - 1)
                        for c in range(4):
                            ins = pe.transpose(S[t % 2][:, c * P:(c + 1) * P], hsum[:, t, c * P:(c + 1) * P], ident)
                        ins.then_inc(r.attnT, 1)
                        pe.wait_ge(r.attnT_sb, t + 1)
                        for c in range(4):
                            ins = pe.matmul(OUT[:, t * P:(t + 1) * P], KT[:, t, c * P:(c + 1) * P],
                                            w("wo")[:, c * P:(c + 1) * P], start=(c == 0), stop=(c == 3))
                    ins.then_inc(r.out, 1)

                @block.scalar
                def _(act):
                    act_xT(act, r)
                    act.wait_ge(r.gate, 2)
                    act.activation(small[:, 576:608], small[:, 544:576], ACT.Exp).then_inc(r.act_step, 1)
                    act.wait_ge(r.gate, 3)
                    for n in range(NT * E):
                        t, e = n % NT, n // NT
                        act.wait_ge(r.hid, n + 1)
                        if n >= 2:
                            act.wait_ge(r.ready, n - 1)
                        act.activation(part[n % 2], RING[n % 4][:, :], ACT.Relu, scale=g3[:, t, e:e + 1]
                                       ).then_inc(r.hid_sb, 1)
                    for t in range(NT):
                        act.wait_ge(r.attnT, t + 1)
                        act.activation(KT[:, t, :], S[t % 2][:, :], ACT.Copy).then_inc(r.attnT_sb, 1)

                @block.vector
                def _(dve):
                    ch = Chain(dve, r.dve_step)
                    lg = small[:, 544:576]
                    l3 = lg.rearrange("p (t e) -> p t e", e=E)
                    mx, ex, rank, sel = small[:, 608:612], small[:, 576:608], small[:, 640:672], small[:, 672:704]
                    e3, r3 = (z.rearrange("p (t e) -> p t e", e=E) for z in (ex, rank))
                    s3 = sel.rearrange("p (t e) -> p t e", e=E)
                    dve.wait_ge(r.gate, 1)
                    ch.link(dve.tensor_tensor(l3, TB[:, 0:32].rearrange("p (t e) -> p t e", e=E),
                                              R_("L2f_gb").unsqueeze(1).broadcast_to([P, NT, E]), ALU.add))
                    ch.link(dve.tensor_reduce(mx, l3, AX.X, ALU.max))
                    dve.tensor_tensor(l3, l3, mx.unsqueeze(2).broadcast_to([P, NT, E]), ALU.subtract).then_inc(r.gate, 1)
                    evacuate(dve, r, tab, "D")
                    dve.wait_ge(r.act_step, 1)
                    ch.link(dve.tensor_reduce(small[:, 612:616], e3, AX.X, ALU.add))
                    ch.link(dve.reciprocal(small[:, 616:620], small[:, 612:616]))
                    ch.link(dve.tensor_tensor(e3, e3, small[:, 616:620].unsqueeze(2).broadcast_to([P, NT, E]), ALU.mult))
                    dve_ranks(dve, ch, e3, NT, E, R_("tri8"), r3, NB[:, 0, :], NB[:, 1, :])
                    ch.link(dve.tensor_scalar(sel, rank, 1.5, None, ALU.is_lt))
                    ch.link(dve.tensor_tensor(ex, ex, sel, ALU.mult))
                    ch.link(dve.tensor_reduce(small[:, 620:624], e3, AX.X, ALU.add))
                    dve.tensor_tensor(g3, s3, small[:, 620:624].unsqueeze(2).broadcast_to([P, NT, E]), ALU.mult
                                      ).then_inc(r.gate, 1)
                    dve.wait_ge(r.gate, 3)
                    ch.link(dve.tensor_reduce(small[:, 624:628], g3, AX.X, ALU.add))
                    for t in range(NT):
                        ch.inc(dve.scalar_tensor_tensor(Z[:, t, :], R_("L2f_bo"), small[:, 624 + t:625 + t],
                                                        X[:, t, :], ALU.mult, ALU.add))
                    ch.join()
                    tail(dve, r, ch, (r.out, 1), flatZ)

        def step_L3_attention():
            step = 13
            r = sets[step % 3]
            w = lambda n: W(step, n)
            q, k = padded_heads(QT)
            att = Attention(16, 8, SEQ, q, k, group=16, causal=True, wo=w("wo"),
                            added=lambda h, qt: relbias[:, h, SEQ - P * (qt + 1):SEQ])
            rowsA = [([(w("wq")[:, c * P:(c + 1) * P], XT[:, :])], P, SEQ, "A", "act", QT[:, c, :],
                      (ACT.Identity, scaled[:, 4 + c:5 + c], RSQRT8)) for c in range(4)]
            rowsA += [([(w("wk")[:, c * P:(c + 1) * P], XT[:, :])], P, SEQ, "D", "col", KT[:, c, :],
                       (C("L3a_bk", c),)) for c in range(4)]
            vrow = R_("L3a_bv").rearrange("p (h d) -> p h d", h=16)
            rowsA += [([(XT[:, t * P:(t + 1) * P], w("wv"))], P, P, "D", "row", v_cell(P, NT, 16, 8, t),
                       (vrow, ALU.add)) for t in range(NT)]
            tab = Table(rowsA)
            with nc.Block() as block:
                @block.sync
                def _(sp):
                    clear_previous(sp, step)
                    load_weights(sp, r, 14)
                    sp.wait_ge(r.loaded, 16)

                @block.gpsimd
                def _(pool):
                    pool_ones(pool, r, P, NT, 16, 8)
                    pool_power(pool, r, 1)

                @block.tensor
                def _(pe):
                    pe_xT(pe, r, X)
                    pe.wait_ge(r.xT, 1)
                    pe_table(pe, r, tab)
                    pe.wait_ge(r.evac_act, tab.a)
                    pe.wait_ge(r.evac_dve, tab.d)
                    pe.wait_ge(r.ones, 1)
                    att.pe(pe, r)

                @block.scalar
                def _(act):
                    act_xT(act, r)
                    evacuate(act, r, tab, "A")
                    att.act(act, r)

                @block.vector
                def _(dve):
                    ch = Chain(dve, r.dve_step)
                    evacuate(dve, r, tab, "D")
                    att.dve(dve, r, ch)
                    ch.link(dve.tensor_tensor(Z[:, :, :], X[:, :, :], row4(R_("L3a_bo")), ALU.add))
                    tail(dve, r, ch, (r.outproj, att.result_count()), flatZ)

        def step_L3_cross():
            step = 14
            r = sets[step % 3]
            w = lambda n: W(step, n)
            keys = KT[:, :, :].rearrange("p c t -> p (c t)")[:, 0:8 * CTX].rearrange("p (c t) -> p c t", c=8)
            att = Attention(16, 64, CTX, heads64,
                            lambda h: keys[64 * (h % 2):64 * (h % 2) + 64, h // 2, :], per_unit=2, wo=w("wo"),
                            added=lambda h, qt: padb[:, min(qt, 2), :])
            rowsA = [([(w("wq")[:, c * P:(c + 1) * P], XT[:, :])], P, SEQ, "A", "act", QT[:, c, :],
                      (ACT.Identity, scaled[:, 8 + c:9 + c], 0.125)) for c in range(8)]
            rowsA += [([(w("wk")[:, c * P:(c + 1) * P], CT[:, :])], P, CTX, "D", "col", keys[:, c, :],
                       (C("L3x_bk", c),)) for c in range(8)]
            for c in range(2):
                for m in range(2):
                    rowsA.append(([(CT[:, c * CK:(c + 1) * CK], w("wv")[:, m * 512:(m + 1) * 512])], CK, SEQ, "D", "row",
                                  v_cell(CK, 2, 16, 64, c)[:, 8 * m:8 * m + 8, :],
                                  (R_("L3x_bv", CK)[:, m * 512:(m + 1) * 512].rearrange("p (h d) -> p h d", h=8),
                                   ALU.add)))
            tab = Table(rowsA)
            with nc.Block() as block:
                @block.sync
                def _(sp):
                    clear_previous(sp, step)
                    load_weights(sp, r, 15)
                    sp.wait_ge(r.loaded, 16)

                @block.gpsimd
                def _(pool):
                    pool_ones(pool, r, CK, 2, 16, 64)
                    pool_power(pool, r, 1)

                @block.tensor
                def _(pe):
                    pe_xT(pe, r, X)
                    pe.wait_ge(r.xT, 1)
                    pe_table(pe, r, tab)
                    pe.wait_ge(r.evac_act, tab.a)
                    pe.wait_ge(r.evac_dve, tab.d)
                    pe.wait_ge(r.ones, 1)
                    att.pe(pe, r)

                @block.scalar
                def _(act):
                    act_xT(act, r)
                    evacuate(act, r, tab, "A")
                    att.act(act, r)

                @block.vector
                def _(dve):
                    ch = Chain(dve, r.dve_step)
                    evacuate(dve, r, tab, "D")
                    att.dve(dve, r, ch)
                    ch.link(dve.tensor_tensor(Z[:, :, :], X[:, :, :], row4(R_("L3x_bo")), ALU.add))
                    tail(dve, r, ch, (r.outproj, att.result_count()), flatZ)

        def step_store(b):
            step = 16
            r = sets[step % 3]
            with nc.Block() as block:
                @block.sync
                def _(sp):
                    clear_previous(sp, step)
                    sp.dma_start(io["out"][bass.ds(b, 1)].rearrange("o (t p) d -> p (o t) d", p=P), X[:, :, :]
                                 ).then_inc(r.loaded, 16)
                    load_weights(sp, r, 0)
                    sp.wait_ge(r.loaded, 32)

        with nc.Fori(0, NBATCH) as b:
            step_load(b)
            step_L0_linear_attention()
            step_L0_mlp()
            step_L0_cross()
            step_L0_moe_attention()
            step_L1_ssm()
            with nc.Fori(0, LAYERS) as l:
                step_L1_attention(l, False)
                step_L1_attention(l, True)
                step_L1_mlp(l)
            step_L1_final()
            step_experts(9, 4, False)
            step_L2_attention()
            step_L2_sigmoid_attention()
            step_L2_lora_experts()
            step_L3_attention()
            step_L3_cross()
            step_experts(15, 8, True)
            step_store(b)



def pack(np, parts, widths):
    out = np.zeros((P, sum(widths)), np.float32)
    at = 0
    for a, n in zip(parts, widths):
        assert a.shape[1] == n, (a.shape, n)
        out[:a.shape[0], at:at + n] = a
        at += n
    return out


def chunked(np, a):
    n = -(-a.shape[0] // P)
    full = np.zeros((n * P, a.shape[1]), a.dtype)
    full[:a.shape[0]] = a
    return full.reshape(n, P, -1).transpose(1, 0, 2).reshape(P, -1)


def pad_heads(np, a, real, padded):
    lead = a.shape[:-1]
    out = np.zeros(lead + (a.shape[-1] // real, padded), a.dtype)
    out[..., :real] = a.reshape(lead + (-1, real))
    return out.reshape(lead + (-1,))


def columns(np, v):
    return chunked(np, v.reshape(-1, 1))


def layout(np, i):
    out = {"x": i["x"], "ctxT": i["ctx_1024"].transpose(0, 2, 1), "mask1": i["mask_BxS_bf1"],
           "mask2": i["mask_BxS2_if1"]}
    proj = np.zeros((P, 512), np.float32)
    for h in range(16):
        proj[8 * h:8 * h + 8, 32 * h:32 * h + 32] = i["L0_attn_proj"][h]
    lb = np.zeros((P, 1024), np.float32)
    for e in range(8):
        at = 32 * (e % 4)
        lb[at:at + 16, 512 * (e // 4):512 * (e // 4) + 512] = i["L2_ffn_lora_B"][e].T
        lb[at + 16, 512 * (e // 4):512 * (e // 4) + 512] = i["L2_ffn_bi"]
    kv = i["L0_ffn_Wkv"]
    experts = lambda a: a.transpose(1, 0, 2).reshape(P, -1)
    second = lambda a: np.concatenate([chunked(np, m) for m in a], 1)
    w = {
        0: [i["L0_attn_w_qkv"].T, proj, i["L0_attn_w_out"].T],
        1: [i["L0_attn_w1"].T, chunked(np, i["L0_attn_w2"].T)],
        2: [pad_heads(np, i["L0_xattn_Wq"], 8, 32), pad_heads(np, i["L0_xattn_Wk"], 8, 32), i["L0_xattn_Wv"],
            i["L0_xattn_Wo"]],
        3: [i["L0_ffn_Wq"], kv[:, :2560], kv[:, 2560:], np.concatenate([i["L0_ffn_Ws"], i["L0_ffn_Wd"]], 1),
            chunked(np, i["L0_ffn_Wo"].reshape(64, 5, P).transpose(1, 0, 2).reshape(320, P))],
        4: [i["L1_attn_W_in"].T, chunked(np, np.concatenate([i["L1_attn_A"], i["L1_attn_B_ssm"]], 1)),
            i["L1_attn_C_ssm"].T, chunked(np, i["L1_attn_W_out"].T)],
        9: [i["L1_ffn_Wr"], experts(i["L1_ffn_We1"]), second(i["L1_ffn_We2"])],
        10: [i["L2_attn_Wq"].T, i["L2_attn_Wk"].T, i["L2_attn_Wv"].T],
        11: [i["L2_xattn_Wq"].T, i["L2_xattn_Wk"].T, i["L2_xattn_Wv"].T],
        12: [i["L2_ffn_gate_w"].T, i["L2_ffn_wi"].T,
             pad_heads(np, i["L2_ffn_lora_A"].reshape(P, P).T, 16, 32), lb, chunked(np, i["L2_ffn_wo"].T)],
        13: [pad_heads(np, i["L3_attn_WQ"].T, 8, 32), pad_heads(np, i["L3_attn_WK"].T, 8, 32), i["L3_attn_WV"].T,
             i["L3_attn_WO"].T],
        14: [i["L3_xattn_Wq"], i["L3_xattn_Wk"], i["L3_xattn_Wv"], chunked(np, i["L3_xattn_Wo"])],
        15: [i["L3_ffn_gate_w"].T, experts(i["L3_ffn_w1"].transpose(0, 2, 1)),
             experts(i["L3_ffn_w3"].transpose(0, 2, 1)), second(i["L3_ffn_w2"].transpose(0, 2, 1))],
    }
    for k, parts in w.items():
        out[f"w{k}"] = pack(np, parts, [n for _, n in WEIGHTS[k]])
    for k, c in ((5, "s"), (6, "c")):
        spread = lambda v: np.broadcast_to(v, (P, P))
        layers = [pack(np, [i[f"L1_xattn_{c}Wq"][l], i[f"L1_xattn_{c}Wk"][l], i[f"L1_xattn_{c}Wv"][l],
                            chunked(np, i[f"L1_xattn_{c}Wo"][l]),
                            spread(i[f"L1_xattn_{c}g"][l]), spread(i[f"L1_xattn_{c}bo"][l])], [n for _, n in WEIGHTS[k]]) for l in range(LAYERS)]
        out[f"w{k}"] = np.stack(layers)
    out["w7"] = np.stack([pack(np, [i["L1_xattn_fW1"][l], chunked(np, i["L1_xattn_fW2"][l]),
                                    spread(i["L1_xattn_fg"][l]), spread(i["L1_xattn_fb2"][l])], [512, 512, 128, 128])
                          for l in range(LAYERS)])
    out["w5next"] = out["w5"][[1, 2, 3, 0]]
    out["w5"] = out["w5"][0]
    one = np.zeros((P, 1), np.float32)
    one[16::32] = 1
    block4 = np.zeros((P, 4), np.float32)
    for h in range(4):
        block4[32 * h:32 * h + 32, h] = 1
    padcols = lambda v: columns(np, pad_heads(np, v, 8, 32))
    c = {"L0a_b1": columns(np, i["L0_attn_b1"]), "L0x_bq": padcols(i["L0_xattn_bq"]),
         "L0x_bk": padcols(i["L0_xattn_bk"]), "L1a_bin": columns(np, i["L1_attn_b_in"]),
         "L1x_fb1": columns(np, i["L1_xattn_fb1"].reshape(-1)), "L1f_be1": columns(np, i["L1_ffn_be1"].reshape(-1)),
         "L2a_bq": columns(np, i["L2_attn_bq"]), "L2a_bk": columns(np, i["L2_attn_bk"]),
         "L2x_bq": columns(np, i["L2_xattn_bq"]), "L2x_bk": columns(np, i["L2_xattn_bk"]), "L2f_one": one,
         "L3a_bq": padcols(i["L3_attn_bQ"]), "L3a_bk": padcols(i["L3_attn_bK"]),
         "L3x_bq": columns(np, i["L3_xattn_bq"]), "L3x_bk": columns(np, i["L3_xattn_bk"]), "block4": block4}
    out["cols"] = pack(np, [c[n] for n, _ in COLS], [m for _, m in COLS])
    tri = lambda n: np.tril(np.ones((n, n), np.float32), -1)
    rw = {"L0a_bout": i["L0_attn_b_out"], "L0a_gamma": i["L0_attn_gamma"], "L0a_beta": i["L0_attn_beta"],
          "L0a_b2": i["L0_attn_b2"], "L0x_bv": i["L0_xattn_bv"], "L0x_bo": i["L0_xattn_bo"],
          "L1a_nw": i["L1_attn_norm_w"], "L1a_nb": i["L1_attn_norm_b"], "L1a_bout": i["L1_attn_b_out"],
          "L1x_gout": i["L1_xattn_g_out"], "L1f_be2": i["L1_ffn_be2"], "L1f_br": i["L1_ffn_br"],
          "L2a_bv": i["L2_attn_bv"], "L2x_bv": i["L2_xattn_bv"], "L2f_bo": i["L2_ffn_bo"],
          "L2f_gb": i["L2_ffn_gate_b"], "L3a_bv": i["L3_attn_bV"], "L3a_bo": i["L3_attn_bO"],
          "L3x_bv": i["L3_xattn_bv"], "L3x_bo": i["L3_xattn_bo"], "tri5": tri(5), "tri4": tri(4), "tri8": tri(8)}
    out["rows"] = np.concatenate([rw[n].reshape(1, -1) for n, _ in ROWS], 1)
    ident = np.eye(P, dtype=np.float32)
    rot = np.zeros((P, P), np.float32)
    for h in (0, 64):
        for m in range(16):
            rot[h + m + 16, h + m] = -1
            rot[h + m, h + m + 16] = 1
    pair = np.eye(P, dtype=np.float32)
    for m in range(0, P, 2):
        pair[m + 1, m] = -1
        pair[m, m + 1] = 1
    pos = np.arange(SEQ, dtype=np.float32)
    inv = (1.0 / 10000.0 ** (np.arange(0, 32, 2, dtype=np.float32) / np.float32(32))).astype(np.float32)
    fr = np.concatenate([inv, inv])[:, None] * pos[None, :]
    cos, sin = np.ones((P, SEQ), np.float32), np.zeros((P, SEQ), np.float32)
    for h in (0, 64):
        cos[h:h + 32], sin[h:h + 32] = np.cos(fr), np.sin(fr)
    inv2 = (10000.0 ** (np.arange(0, 64, 2, dtype=np.float32) / np.float32(64))).astype(np.float32)
    rad = pos[None, :] / inv2[:, None]
    sc = np.stack([np.sin(rad), np.cos(rad)], 1).reshape(64, SEQ)
    out["consts"] = pack(np, [ident, rot, pair, cos, sin, np.repeat(sc, 2, 0)], [m for _, m in CONSTS])
    table = i["L3_attn_rel_pos_table"]
    at = np.arange(P)[:, None] - np.arange(SEQ)[None, :] + (SEQ - P) + len(table) // 2
    out["reltab"] = table[np.clip(at, 0, len(table) - 1)].transpose(0, 2, 1).reshape(P, -1)
    return {k: np.ascontiguousarray(v) for k, v in out.items()}


def kernel(**inputs):
    import numpy as np
    import concourse.bacc as bacc
    from concourse.bass_utils import run_bass_kernel_spmd

    nc = bacc.Bacc("TRN2", target_bir_lowering=False, num_devices=1)
    arrays, io = {}, {}
    for name, a in layout(np, {k: np.asarray(v) for k, v in inputs.items()}).items():
        arrays[f"in_{name}_dram"] = a
        io[name] = nc.dram_tensor(f"in_{name}_dram", a.shape, mybir.dt.from_np(a.dtype), kind="ExternalInput").ap()
    io["out"] = nc.dram_tensor("out_0_dram", (NBATCH, SEQ, P), F32, kind="ExternalOutput").ap()
    build(nc, io)
    r = run_bass_kernel_spmd(nc, [arrays], core_ids=[0])
    return r.results[0]["out_0_dram"]
```

```python
from contextlib import ExitStack

import concourse.bass as bass
from concourse import mybir

F32 = mybir.dt.float32
I32 = mybir.dt.int32
U8 = mybir.dt.uint8
ALU = mybir.AluOpType
ACT = mybir.ActivationFunctionType
AX = mybir.AxisListType

P = 128
NBATCH, SEQ, CTX = 4, 512, 154
NT = SEQ // P
CK = CTX // 2
LAYERS = 4
HUGE = 3.0e38
MASKED = 1.0e30
EPS = 1e-5
RSQRT8 = 8.0 ** -0.5

WEIGHTS = {
    0: [("wqkv", 384), ("proj", 512), ("wout", 128)],
    1: [("w1", 512), ("w2", 512)],
    2: [("wq", 512), ("wk", 512), ("wv", 128), ("wo", 512)],
    3: [("wq", 2560), ("wk", 2560), ("wv", 2560), ("wsd", 80), ("wo", 384)],
    4: [("win", 256), ("ab", 64), ("c", 256), ("wout", 256)],
    5: [("wq", 512), ("wk", 512), ("wv", 512), ("wo", 512), ("gain", 128), ("bias", 128)],
    6: [("wq", 512), ("wk", 512), ("wv", 512), ("wo", 512), ("gain", 128), ("bias", 128)],
    7: [("w1", 512), ("w2", 512), ("gain", 128), ("bias", 128)],
    9: [("wr", 4), ("w1", 2048), ("w2", 2048)],
    10: [("wq", 128), ("wk", 128), ("wv", 128), ("sincos", 512)],
    11: [("wq", 32), ("wk", 32), ("wv", 128)],
    12: [("gate", 8), ("wi", 512), ("loraA", 256), ("loraB", 4096), ("wo", 512)],
    13: [("wq", 512), ("wk", 512), ("wv", 128), ("wo", 512)],
    14: [("wq", 1024), ("wk", 1024), ("wv", 1024), ("wo", 1024)],
    15: [("gate", 8), ("w1", 4096), ("w3", 4096), ("w2", 4096)],
}
COLS = [("L0a_b1", 4), ("L0x_bq", 4), ("L0x_bk", 4), ("L1a_bin", 2), ("L1x_fb1", 16), ("L1f_be1", 16),
        ("L2a_bq", 1), ("L2a_bk", 1), ("L2x_bq", 1), ("L2x_bk", 1), ("L2f_one", 1),
        ("L3a_bq", 4), ("L3a_bk", 4), ("L3x_bq", 8), ("L3x_bk", 8), ("block4", 4)]
ROWS = [("L0a_bout", 128), ("L0a_gamma", 128), ("L0a_beta", 128), ("L0a_b2", 128), ("L0x_bv", 128),
        ("L0x_bo", 128), ("L1a_nw", 128), ("L1a_nb", 128), ("L1a_bout", 128),
        ("L1x_gout", 128), ("L1f_be2", 512), ("L1f_br", 4), ("L2a_bv", 128), ("L2x_bv", 128),
        ("L2f_bo", 128), ("L2f_gb", 8), ("L3a_bv", 128), ("L3a_bo", 128), ("L3x_bo", 128),
        ("tri5", 25), ("tri4", 16), ("tri8", 64)]
CONSTS = [("ident", 128), ("rot", 128), ("pair", 128), ("cos", 512), ("sin", 512)]


def spans(spec):
    at, out = 0, {}
    for name, n in spec:
        out[name] = (at, n)
        at += n
    return out, at


WIDTH = {k: spans(v)[1] for k, v in WEIGHTS.items()}
class Roles:
    def __init__(self, sem):
        self.loaded = sem("loaded")
        self.xT_ps = sem("xT_ps")
        self.xT = sem("xT")
        self.proj = sem("proj")
        self.evac_act = sem("evac_act")
        self.evac_dve = sem("evac_dve")
        self.rot_mul = sem("rot_mul")
        self.recip = sem("recip")
        self.probs = sem("probs")
        self.headkeys = sem("headkeys")
        self.av_sb = sem("av_sb")
        self.ones = sem("ones")
        self.scores = sem("scores")
        self.negmax = sem("negmax")
        self.exped = sem("exped")
        self.probsT = sem("probsT")
        self.probsT_sb = sem("probsT_sb")
        self.unit_av = sem("unit_av")
        self.av = sem("av")
        self.normed = sem("normed")
        self.attnT = sem("attnT")
        self.attnT_sb = sem("attnT_sb")
        self.outproj = sem("outproj")
        self.out = sem("out")
        self.var = sem("var")
        self.rstd = sem("rstd")
        self.hid = sem("hid")
        self.hid_sb = sem("hid_sb")
        self.hid_dve = sem("hid_dve")
        self.part = sem("part")
        self.part_used = sem("part_used")
        self.gate = sem("gate")
        self.ready = sem("ready")
        self.early = sem("early")
        self.dve_step = sem("dve_step")
        self.act_step = sem("act_step")
        self.sum_step = sem("sum_step")
        self.pool_step = sem("pool_step")


class Chain:

    def __init__(self, eng, sem):
        self.eng, self.sem, self.n = eng, sem, 0

    def inc(self, ins):
        ins.then_inc(self.sem, 1)
        self.n += 1
        return ins

    def join(self):
        if self.n:
            self.eng.wait_ge(self.sem, self.n)

    def link(self, ins):
        self.inc(ins)
        self.join()


class Table:

    def __init__(self, rows, before=None):
        self.rows, self.before = rows, before
        self.j0 = before.j1 if before else 0
        a, d = (before.a, before.d) if before else (0, 0)
        self.count = list(before.count) if before else []
        for r in rows:
            if r[3] == "A":
                a += 1
            else:
                d += 1
            self.count.append((r[3], a if r[3] == "A" else d))
        self.a, self.d, self.j1 = a, d, self.j0 + len(rows)


def build(nc, io):
    ctx = ExitStack()
    with ctx:
        def sb(name, shape, dt=F32):
            return ctx.enter_context(nc.sbuf_tensor(name, shape, dt))

        cols_at, ncols = spans(COLS)
        rows_at, nrows = spans(ROWS)
        consts_at, nconsts = spans(CONSTS)
        arena_w = [max(w for k, w in WIDTH.items() if k % 3 == a) for a in range(3)]
        arenas = [sb(f"weights{a}", [P, arena_w[a]]) for a in range(3)]
        cols = sb("cols", [P, ncols])
        scaled = sb("scaled", [P, 16])
        rows = sb("rows", [P, nrows])
        consts = sb("consts", [P, nconsts])
        relbias = sb("relbias", [P, 16, SEQ])
        X = sb("X", [P, NT, P])
        XN = sb("XN", [P, NT, P])
        XR = sb("XR", [P, NT, P])
        Z = sb("Z", [P, NT, P])
        XT = sb("XT", [P, SEQ])
        CT = sb("CT", [P, CTX])
        QT = sb("QT", [P, 8, SEQ])
        KT = sb("KT", [P, 4, SEQ])
        V = sb("V", [P, 2080])
        wide = sb("wide", [P, 4096])
        KZ = sb("KZ", [P, 4, SEQ])
        EX = sb("EX", [P, 4, SEQ])
        NB = sb("NB", [P, 2, SEQ])
        maskb = sb("maskb", [P, SEQ])
        mask_u8 = sb("mask_u8", [P, SEQ], U8)
        padm = sb("padm", [P, CTX], I32)
        padb = sb("padb", [P, 3, CTX])
        neg, sums, recips = sb("neg", [P, 8]), sb("sums", [P, 8]), sb("recips", [P, 8])
        small = sb("small", [P, 880])
        ps = {n: ctx.enter_context(nc.psum_tensor("ps_" + n, [P, SEQ], F32))
              for n in ("S0", "S1", "P0", "P1", "O0", "O1", "T", "OUT")}
        S = [ps["S0"], ps["S1"]]
        PP = [ps["P0"], ps["P1"]]
        O = [ps["O0"], ps["O1"]]
        TB, OUT = ps["T"], ps["OUT"]
        RING = [ps["P0"], ps["P1"], ps["O0"], ps["O1"]]

        sets = []
        for n in range(3):
            nums = []

            def sem(name):
                s = ctx.enter_context(nc.semaphore(f"{name}_{n}"))
                nums.append(s.num)
                return s

            r = Roles(sem)
            r.nums = range(min(nums), max(nums) + 1)
            assert len(r.nums) == len(nums)
            sets.append(r)
        s_boot = ctx.enter_context(nc.semaphore("boot"))
        s_boot3 = ctx.enter_context(nc.semaphore("boot_gpsimd"))
        s_boot2 = ctx.enter_context(nc.semaphore("boot_steps"))

        def C(name, c=0, n=1, parts=P):
            a = cols_at[name][0] + c
            return cols[0:parts, a:a + n]

        def R_(name, parts=P):
            a, n = rows_at[name]
            return rows[0:parts, a:a + n]

        def K(name):
            a, n = consts_at[name]
            return consts[:, a:a + n]

        ident = K("ident")

        def W(step, name):
            at, n = spans(WEIGHTS[step])[0][name]
            return arenas[step % 3][:, at:at + n]

        def tiles(ap, n=NT):
            return ap.rearrange("p (t d) -> p t d", t=n)

        flatX, flatZ, flatXN, flatXR = (t[:, :, :].rearrange("p t d -> p (t d)") for t in (X, Z, XN, XR))

        def row4(ap):
            return ap.unsqueeze(1).broadcast_to([P, NT, P])


        def load_weights(sp, r, step):
            sp.dma_start(arenas[step % 3][:, 0:WIDTH[step]], io[f"w{step}"][:, :]).then_inc(r.loaded, 16)

        def clear_previous(eng, step):
            eng.sem_clear(sets[(step - 1) % 3].nums)

        def pe_xT(pe, r, src, n=1):
            for t in range(NT):
                ins = pe.transpose(TB[:, t * P:(t + 1) * P], src[:, t, :], ident)
            ins.then_inc(r.xT_ps, 1)

        def act_xT(act, r, n=1):
            act.wait_ge(r.xT_ps, n)
            act.activation(XT[:, :], TB[:, :], ACT.Copy).then_inc(r.xT, 1)

        def pe_table(pe, r, tab):
            for j, row in enumerate(tab.rows):
                g = tab.j0 + j
                if g >= len(RING):
                    e, n = tab.count[g - len(RING)]
                    pe.wait_ge(r.evac_act if e == "A" else r.evac_dve, n)
                bank = RING[g % len(RING)]
                mms = row[0]
                for i, (lhsT, rhs) in enumerate(mms):
                    ins = pe.matmul(bank[0:row[1], 0:row[2]], lhsT, rhs, start=(i == 0), stop=(i == len(mms) - 1))
                ins.then_inc(r.proj, 1)

        def evacuate(eng, r, tab, who):
            for j, row in enumerate(tab.rows):
                if row[3] != who:
                    continue
                g = tab.j0 + j
                kind, dst, args = row[4], row[5], row[6]
                src = RING[g % len(RING)][0:row[1], 0:row[2]]
                if len(dst.shape) == 3:
                    src = src.rearrange("p (a b) -> p a b", a=dst.shape[1])
                eng.wait_ge(r.proj, g + 1)
                done = r.evac_act if who == "A" else r.evac_dve
                if kind == "act":
                    eng.activation(dst, src, args[0], bias=args[1], scale=args[2]).then_inc(done, 1)
                elif kind == "copy":
                    if who == "A":
                        eng.activation(dst, src, ACT.Copy).then_inc(done, 1)
                    else:
                        eng.tensor_copy(dst, src).then_inc(done, 1)
                elif kind == "scale":
                    eng.activation(dst, src, ACT.Copy, scale=args[0]).then_inc(done, 1)
                elif kind == "col":
                    eng.tensor_scalar(dst, src, args[0], None, ALU.add).then_inc(done, 1)
                elif kind == "row":
                    eng.tensor_tensor(dst, src, args[0], args[1]).then_inc(done, 1)

        def dve_layer_norm(dve, r, ch, n, src, dst, gain=None, shift=None):
            st, mv, ve = small[:, 0:24], small[:, 24:32], small[:, 32:36]
            for t in range(NT):
                ch.inc(dve.bn_stats(st[:, 6 * t:6 * t + 6], src[:, t, :]))
            ch.join()
            for t in range(NT):
                ch.inc(dve.bn_aggr(mv[:, 2 * t:2 * t + 2], st[:, 6 * t:6 * t + 6]))
            ch.join()
            dve.tensor_scalar(ve, mv.rearrange("p (t k) -> p t k", k=2)[:, :, 1], EPS, None,
                              ALU.add).then_inc(r.var, 1)
            dve.wait_ge(r.rstd, n)
            for t in range(NT):
                ch.inc(dve.tensor_scalar(dst[:, t, :], src[:, t, :], mv[:, 2 * t:2 * t + 1],
                                         small[:, 36 + t:37 + t], ALU.subtract, ALU.mult))
            ch.join()
            if gain is not None:
                ch.link(dve.tensor_tensor(dst[:, :, :], dst[:, :, :], row4(gain), ALU.mult))
                ch.link(dve.tensor_tensor(dst[:, :, :], dst[:, :, :], row4(shift), ALU.add))

        def pool_power(pool, r, n, half=40):
            pool.wait_ge(r.var, n)
            pool.tensor_tensor(small[:, 36:40], small[:, 32:36], small[:, half:half + 4], ALU.pow).then_inc(r.rstd, 1)

        def dve_rms_norm(dve, r, ch, n, src, dst, gain):
            for t in range(NT):
                ch.inc(dve.tensor_tensor_reduce(Z[:, t, :], src[:, t, :], src[:, t, :], 1.0, 0.0, ALU.mult, ALU.add,
                                                small[:, 48 + t:49 + t]))
            ch.join()
            dve.tensor_scalar(small[:, 32:36], small[:, 48:52], 1.0 / P, None, ALU.mult).then_inc(r.var, 1)
            dve.wait_ge(r.rstd, n)
            ch.link(dve.tensor_scalar(small[:, 52:56], small[:, 36:40], 1e-8, None, ALU.max))
            ch.link(dve.reciprocal(small[:, 56:60], small[:, 52:56]))
            for t in range(NT):
                ch.inc(dve.scalar_tensor_tensor(dst[:, t, :], src[:, t, :], small[:, 56 + t:57 + t], gain,
                                                ALU.mult, ALU.mult))
            ch.join()

        def dve_ranks(dve, ch, s, G, E, tri, rank, t1, t2):
            mine = s.unsqueeze(3).broadcast_to([P, G, E, E])
            other = s.unsqueeze(2).broadcast_to([P, G, E, E])
            lower = tri.rearrange("p (a b) -> p a b", a=E).unsqueeze(1).broadcast_to([P, G, E, E])
            a = t1[:, 0:G * E * E].rearrange("p (g e f) -> p g e f", g=G, e=E)
            b = t2[:, 0:G * E * E].rearrange("p (g e f) -> p g e f", g=G, e=E)
            ch.inc(dve.tensor_tensor(a, other, mine, ALU.is_gt))
            ch.link(dve.tensor_tensor(b, other, mine, ALU.is_equal))
            ch.link(dve.tensor_tensor(b, b, lower, ALU.mult))
            ch.link(dve.tensor_tensor(a, a, b, ALU.add))
            ch.link(dve.tensor_reduce(rank, a, AX.X, ALU.add))


        class Attention:
            LAG = 3

            def __init__(self, heads, dh, nkeys, added=None, causal=False, keys=None):
                self.heads, self.dh, self.nkeys, self.added, self.causal = heads, dh, nkeys, added, causal
                self.keys = keys
                self.ctx = nkeys == CTX
                self.kc = CK if self.ctx else P
                self.nch = nkeys // self.kc
                self.U = self.nch
                self.slot = {8: 32, 64: 64, P: P}[dh]
                self.hpc = P // self.slot
                self.chunks = heads // self.hpc
                self.units = [(h, [2 * u, 2 * u + 1] if self.ctx else [u],
                               P * (u + 1) if causal else nkeys) for h in range(heads) for u in range(self.U)]
                self.steps = len(self.units) + self.LAG + self.U + 1

            def probs(self, h):
                n = self.nch * SEQ
                return wide[:, (h % 2) * n:(h % 2 + 1) * n].rearrange("p (c q) -> p c q", c=self.nch)

            def value(self, h, c):
                w = self.heads * self.slot
                return V[:, c * w + h * self.slot:c * w + (h + 1) * self.slot]

            def out_chunk(self, c):
                return QT[:, c, :]

            def av_at(self, i):
                k = i - self.LAG - self.U
                return (k // self.U, k % self.U) if 0 <= k < self.heads * self.U else None

            def pool(self, pool, r, waits):
                if self.hpc == 1:
                    return
                for c in range(self.hpc):
                    pool.memset(KZ[:, c, 0:self.nkeys], 0.0).then_inc(r.pool_step, 1)
                pool.wait_ge(r.pool_step, self.hpc)
                for sem, n in waits:
                    pool.wait_ge(sem, n)
                for h in range(self.heads):
                    j = h % self.hpc
                    if h >= self.hpc:
                        pool.wait_ge(r.scores, self.U * (h - self.hpc + 1))
                    rows_of = slice(self.slot * j, self.slot * (j + 1))
                    pool.tensor_copy(KZ[rows_of, j, 0:self.nkeys], self.keys(h // self.hpc)[rows_of, :]
                                     ).then_inc(r.headkeys, 1)

            def pe(self, pe, r):
                n = len(self.units)
                for i in range(self.steps):
                    if i < n:
                        h, qts, N = self.units[i]
                        c = h // self.hpc
                        if i % self.U == 0 and self.hpc > 1:
                            pe.wait_ge(r.headkeys, h + 1)
                        if i >= 2:
                            pe.wait_ge(r.negmax if self.added else r.exped, i - 1)
                        k = KZ[:, h % self.hpc, 0:N] if self.hpc > 1 else self.keys(c)[:, 0:N]
                        for a, qt in enumerate(qts):
                            ins = pe.matmul(S[i % 2][:, a * N:(a + 1) * N], QT[:, c, qt * P:(qt + 1) * P], k,
                                            start=True, stop=True)
                        ins.then_inc(r.scores, 1)
                    u = i - self.LAG
                    if 0 <= u < n:
                        h, qts, N = self.units[u]
                        pe.wait_ge(r.probs, u + 1)
                        if u >= 2:
                            pe.wait_ge(r.probsT_sb, u - 1)
                        for c in range(N // self.kc):
                            for a, qt in enumerate(qts):
                                b = c * len(qts) + a
                                ins = pe.transpose(PP[u % 2][0:self.kc, b * P:(b + 1) * P],
                                                   EX[:, u % 4, a * N + c * self.kc:a * N + (c + 1) * self.kc],
                                                   ident)
                        ins.then_inc(r.probsT, 1)
                    hc = self.av_at(i)
                    if hc:
                        h, c = hc
                        m = h // self.hpc
                        if c == 0:
                            pe.wait_ge(r.probsT_sb, self.U * (h + 1))
                            if h % self.hpc == 0 and m >= 2:
                                pe.wait_ge(r.av_sb, m - 1)
                        q0 = c * P if self.causal else 0
                        j = h % self.hpc
                        ins = pe.matmul(O[m % 2][self.slot * j:self.slot * (j + 1), q0:SEQ], self.value(h, c),
                                        self.probs(h)[:, c, q0:SEQ], start=(c == 0), stop=(c == self.nch - 1),
                                        skip_group_check=self.causal)
                        if c == self.nch - 1:
                            ins.then_inc(r.av, 1)

            def act(self, act, r):
                n = len(self.units)
                for i in range(self.steps):
                    if i < n:
                        h, qts, N = self.units[i]
                        act.wait_ge(r.negmax, i + 1)
                        if i >= 4:
                            act.wait_ge(r.probsT, i - 3)
                        for a in range(len(qts)):
                            src = NB[:, i % 2, a * N:(a + 1) * N] if self.added else S[i % 2][:, a * N:(a + 1) * N]
                            at = 2 * (i % 4) + a
                            ins = act.activation(EX[:, i % 4, a * N:(a + 1) * N], src, ACT.Exp,
                                                 bias=neg[:, at:at + 1], scale=-1.0 if self.added else 1.0,
                                                 accum_out=sums[:, at:at + 1])
                        ins.then_inc(r.exped, 1)
                    u = i - 1
                    if 0 <= u < n and not self.ctx:
                        h, qts, N = self.units[u]
                        act.wait_ge(r.recip, u + 1)
                        at = 2 * (u % 4)
                        act.activation(EX[:, u % 4, 0:N], EX[:, u % 4, 0:N], ACT.Copy, scale=recips[:, at:at + 1]
                                       ).then_inc(r.probs, 1)
                    hc = self.av_at(i)
                    if hc and hc[1] == self.nch - 1 and hc[0] % self.hpc == self.hpc - 1:
                        h = hc[0]
                        act.wait_ge(r.av, h + 1)
                        act.activation(self.out_chunk(h // self.hpc), O[(h // self.hpc) % 2][:, :], ACT.Copy
                                       ).then_inc(r.av_sb, 1)

            def dve(self, dve, r):
                n = len(self.units)
                for i in range(self.steps):
                    if i < n:
                        h, qts, N = self.units[i]
                        dve.wait_ge(r.scores, i + 1)
                        if self.added and i >= 2:
                            dve.wait_ge(r.exped, i - 1)
                        elif i >= 4:
                            dve.wait_ge(r.exped, i - 3)
                        at = 2 * (i % 4)
                        if self.added:
                            for a, qt in enumerate(qts):
                                ins = dve.tensor_tensor_reduce(
                                    NB[:, i % 2, a * N:(a + 1) * N], S[i % 2][:, a * N:(a + 1) * N],
                                    self.added(h, qt), -1.0, HUGE, ALU.add, ALU.min, neg[:, at + a:at + a + 1])
                        else:
                            w = len(qts)
                            ins = dve.tensor_reduce(neg[:, at:at + w],
                                                    S[i % 2][:, 0:w * N].rearrange("p (a k) -> p a k", k=N),
                                                    AX.X, ALU.max, negate=True)
                        ins.then_inc(r.negmax, 1)
                    u = i - 1
                    if 0 <= u < n:
                        h, qts, N = self.units[u]
                        at, w = 2 * (u % 4), len(qts)
                        dve.wait_ge(r.exped, u + 1)
                        if u >= 4 and not self.ctx:
                            dve.wait_ge(r.probs, u - 3)
                        dve.reciprocal(recips[:, at:at + w], sums[:, at:at + w]).then_inc(r.recip, 1)
                        if self.ctx:
                            e = EX[:, u % 4, 0:w * N].rearrange("p (a k) -> p a k", k=N)
                            dve.wait_ge(r.recip, u + 1)
                            dve.tensor_tensor(e, e, recips[:, at:at + w].unsqueeze(2).broadcast_to([P, w, N]),
                                              ALU.mult).then_inc(r.probs, 1)
                    u = i - self.LAG
                    if 0 <= u < n:
                        h, qts, N = self.units[u]
                        dve.wait_ge(r.probsT, u + 1)
                        if u % self.U == 0 and h >= 2:
                            dve.wait_ge(r.av, h - 1)
                        nc_ = N // self.kc
                        w = len(qts) * P
                        dve.tensor_copy(self.probs(h)[0:self.kc, 0:nc_, qts[0] * P:qts[0] * P + w],
                                        PP[u % 2][0:self.kc, 0:nc_ * w].rearrange("p (c q) -> p c q", c=nc_)
                                        ).then_inc(r.probsT_sb, 1)

            def project(self, pe, r, wo):
                pe.wait_ge(r.av_sb, self.chunks)
                for t in range(NT):
                    for c in range(self.chunks):
                        ins = pe.matmul(OUT[:, t * P:(t + 1) * P], self.out_chunk(c)[:, t * P:(t + 1) * P],
                                        wo[:, c * P:(c + 1) * P], start=(c == 0), stop=(c == self.chunks - 1))
                ins.then_inc(r.out, 1)

        def pool_clear_context(pool, r, n):
            pool.memset(V[:, 0:n], 0.0).then_inc(r.ones, 1)
            pool.memset(wide[:, 0:4 * SEQ], 0.0).then_inc(r.ones, 1)

        def v_rows(kc, heads, slot, dh, c):
            w = heads * slot
            return V[0:kc, c * w:(c + 1) * w].rearrange("p (h d) -> p h d", h=heads)[:, :, 0:dh]

        with nc.Block() as block:
            @block.sync
            def _(sp):
                sp.dma_start(cols[:, :], io["cols"][:, :]).then_inc(s_boot, 16)
                sp.dma_start(rows[:, :], bass.AP(io["rows"].tensor, 0, [[0, P], [1, nrows]])).then_inc(s_boot, 16)
                sp.dma_start(consts[:, :], io["consts"][:, :]).then_inc(s_boot, 16)
                sp.dma_start(relbias[:, :, :].rearrange("p h k -> p (h k)"), io["reltab"][:, :]).then_inc(s_boot, 16)
                sp.dma_start(arenas[0][:, 0:WIDTH[0]], io["w0"][:, :]).then_inc(s_boot, 16)
                sp.wait_ge(s_boot, 80)

            @block.gpsimd
            def _(pool):
                pool.wait_ge(s_boot, 80)
                pool.affine_select(relbias[:, :, :], relbias[:, :, :], [[0, 16], [-1, SEQ]], ALU.is_ge, -HUGE,
                                   base=SEQ - P, channel_multiplier=1).then_inc(s_boot3, 1)
                pool.memset(small[:, 40:44], -0.5).then_inc(s_boot3, 1)
                pool.memset(small[:, 44:48], 0.5).then_inc(s_boot3, 1)
                pool.wait_ge(s_boot3, 3)

            @block.vector
            def _(dve):
                dve.wait_ge(s_boot, 80)
                a = cols_at["L0x_bq"][0]
                dve.tensor_scalar(scaled[:, 0:4], cols[:, a:a + 4], RSQRT8, None, ALU.mult).then_inc(s_boot2, 1)
                a = cols_at["L3a_bq"][0]
                dve.tensor_scalar(scaled[:, 4:8], cols[:, a:a + 4], RSQRT8, None, ALU.mult).then_inc(s_boot2, 1)
                a = cols_at["L3x_bq"][0]
                dve.tensor_scalar(scaled[:, 8:16], cols[:, a:a + 8], 0.125, None, ALU.mult).then_inc(s_boot2, 1)
                dve.wait_ge(s_boot2, 3)


        def step_load(b):
            step = 17
            r = sets[step % 3]
            with nc.Block() as block:
                @block.sync
                def _(sp):
                    clear_previous(sp, step)
                    sp.dma_start(X[:, :, :], io["x"][bass.ds(b, 1)].rearrange("o (t p) d -> p (o t) d", p=P)
                                 ).then_inc(r.loaded, 16)
                    sp.dma_start(CT[:, :], io["ctxT"][bass.ds(b, 1)].rearrange("o p k -> p (o k)")
                                 ).then_inc(r.loaded, 16)
                    sp.dma_start(mask_u8[:, :], io["mask1"][bass.ds(b, 1), :].broadcast_to([P, SEQ])
                                 ).then_inc(r.loaded, 16)
                    sp.dma_start(padm[:, :], io["mask2"][bass.ds(b, 1), :].broadcast_to([P, CTX])
                                 ).then_inc(r.loaded, 16)
                    sp.wait_ge(r.loaded, 64)

                @block.vector
                def _(dve):
                    ch = Chain(dve, r.dve_step)
                    dve.wait_ge(r.loaded, 64)
                    ch.inc(dve.tensor_scalar(maskb[:, :], mask_u8[:, :], MASKED, -MASKED, ALU.mult, ALU.add))
                    for m in range(3):
                        ins = dve.tensor_scalar(padb[:, m, :], padm[:, :], 0.0, -HUGE, ALU.is_equal, ALU.mult)
                        ins.then_inc(r.ready, 1)
                    dve.wait_ge(r.early, 2)

                @block.gpsimd
                def _(pool):
                    pool.wait_ge(r.ready, 3)
                    for m in range(2):
                        pool.affine_select(padb[:, m, :], padb[:, m, :], [[-1, CTX]], ALU.is_ge, -HUGE,
                                           base=P * m, channel_multiplier=1).then_inc(r.early, 1)
                    pool.wait_ge(r.early, 2)

        def tail(dve, r, ch, out_wait, base, n=1):
            dve.wait_ge(*out_wait)
            ch.link(dve.tensor_tensor(flatZ, OUT[:, :], base, ALU.add))
            dve_layer_norm(dve, r, ch, n, Z, X)

        def step_L0_linear_attention():
            step = 0
            r = sets[step % 3]
            w = lambda n: W(step, n)
            qT, kT = KT[:, 0, :], KT[:, 1, :]
            qf = QT[:, 0:4, :]
            kf = QT[:, 4:8, :]
            pos = wide[:, 0:4096].rearrange("p (c t) -> p c t", c=8)
            vv = V[:, 0:NT * 144].rearrange("p (t h d) -> p t h d", t=NT, h=16)
            kvb = small[:, 128:272].rearrange("p (c h d) -> p c h d", c=4, h=4)
            rowsA = [([(w("wqkv")[:, 0:128], XT[:, :])], P, SEQ, "A", "copy", qT, None),
                     ([(w("wqkv")[:, 128:256], XT[:, :])], P, SEQ, "D", "copy", kT, None)]
            rowsA += [([(XT[:, t * P:(t + 1) * P], w("wqkv")[:, 256:384])], P, P, "AD"[t % 2], "copy",
                       vv[:, t, :, 0:8], None) for t in range(NT)]
            tab = Table(rowsA)
            with nc.Block() as block:
                @block.sync
                def _(sp):
                    clear_previous(sp, step)
                    load_weights(sp, r, 1)
                    sp.wait_ge(r.loaded, 16)

                @block.gpsimd
                def _(pool):
                    pool.memset(V[:, 0:NT * 144].rearrange("p (t d) -> p t d", d=9)[:, :, 8:9], 1.0).then_inc(r.ones, 1)
                    for c in range(8):
                        pool.wait_ge(r.hid_sb, c + 1)
                        pool.wait_ge(r.hid_dve, 2 * c + 2)
                        f = qf[:, c, :] if c < 4 else kf[:, c - 4, :]
                        pool.tensor_tensor(f, f, pos[:, c, :], ALU.add).then_inc(r.ready, 1)
                    pool_power(pool, r, 1)

                @block.tensor
                def _(pe):
                    pe_xT(pe, r, X)
                    pe.wait_ge(r.xT, 1)
                    pe_table(pe, r, tab)
                    pe.wait_ge(r.evac_act, tab.a)
                    pe.wait_ge(r.evac_dve, tab.d)
                    for c in range(8):
                        if c >= 4:
                            pe.wait_ge(r.hid_dve, 2 * (c - 4) + 2)
                        if c < 4:
                            ins = pe.matmul(RING[c % 4][:, :], w("proj")[:, c * P:(c + 1) * P], qT, start=True, stop=True)
                        else:
                            t = c - 4
                            ins = pe.matmul(RING[c % 4][:, :], kT[:, t * P:(t + 1) * P], w("proj"), start=True, stop=True)
                        ins.then_inc(r.hid, 1)
                    pe.wait_ge(r.ready, 8)
                    pe.wait_ge(r.ones, 1)
                    for c in range(4):
                        for t in range(NT):
                            ins = pe.matmul(TB[:, c * 36:(c + 1) * 36], kf[:, t, c * P:(c + 1) * P],
                                            vv[:, t, 4 * c:4 * c + 4, :], start=(t == 0), stop=(t == NT - 1))
                    ins.then_inc(r.part, 1)
                    pe.wait_ge(r.part_used, 1)
                    for t in range(NT):
                        for c in range(4):
                            ins = pe.matmul(S[t % 2][:, (t // 2) * 144 + c * 36:(t // 2) * 144 + (c + 1) * 36],
                                            qf[:, c, t * P:(t + 1) * P], kvb[:, c, :, :], start=True, stop=True)
                    ins.then_inc(r.av, 1)
                    pe.wait_ge(r.normed, 4)
                    for t in range(NT):
                        ins = pe.transpose(TB[:, t * P:(t + 1) * P], XN[:, t, :], ident)
                    ins.then_inc(r.attnT, 1)
                    pe.wait_ge(r.attnT_sb, 1)
                    for t in range(NT):
                        ins = pe.matmul(OUT[:, t * P:(t + 1) * P], XT[:, t * P:(t + 1) * P], w("wout"),
                                        start=True, stop=True)
                    ins.then_inc(r.out, 1)

                @block.scalar
                def _(act):
                    act_xT(act, r)
                    evacuate(act, r, tab, "A")
                    for c in range(8):
                        act.wait_ge(r.hid_dve, 2 * c + 2)
                        f = qf[:, c, :] if c < 4 else kf[:, c - 4, :]
                        act.activation(f, f, ACT.Exp).then_inc(r.hid_sb, 1)
                    act.wait_ge(r.attnT, 1)
                    act.activation(XT[:, :], TB[:, :], ACT.Copy).then_inc(r.attnT_sb, 1)

                @block.vector
                def _(dve):
                    ch = Chain(dve, r.dve_step)
                    evacuate(dve, r, tab, "D")
                    for c in range(8):
                        dve.wait_ge(r.hid, c + 1)
                        f = qf[:, c, :] if c < 4 else kf[:, c - 4, :]
                        dve.tensor_scalar(f, RING[c % 4][:, :], 0.0, None, ALU.min).then_inc(r.hid_dve, 1)
                        dve.tensor_scalar(pos[:, c, :], RING[c % 4][:, :], 0.0, None, ALU.max).then_inc(r.hid_dve, 1)
                    dve.wait_ge(r.part, 1)
                    dve.tensor_tensor(kvb, TB[:, 0:144].rearrange("p (c h d) -> p c h d", c=4, h=4),
                                      C("block4", 0, 4).unsqueeze(1).unsqueeze(3).broadcast_to([P, 4, 4, 9]),
                                      ALU.mult).then_inc(r.part_used, 1)
                    dve.wait_ge(r.av, 1)
                    for t in range(NT):
                        o = S[t % 2][:, (t // 2) * 144:(t // 2) * 144 + 144].rearrange("p (h d) -> p h d", h=16)
                        den = small[:, 272 + 16 * t:288 + 16 * t]
                        ch.link(dve.tensor_scalar(den, o[:, :, 8], 1e-8, None, ALU.add))
                        ch.link(dve.reciprocal(den, den))
                        dve.tensor_tensor(XN[:, t, :].rearrange("p (h d) -> p h d", h=16), o[:, :, 0:8],
                                          den.unsqueeze(2).broadcast_to([P, 16, 8]), ALU.mult).then_inc(r.normed, 1)
                    ch.link(dve.tensor_tensor(Z[:, :, :], X[:, :, :], row4(R_("L0a_bout")), ALU.add))
                    dve.wait_ge(r.out, 1)
                    ch.link(dve.tensor_tensor(flatZ, OUT[:, :], flatZ, ALU.add))
                    dve_layer_norm(dve, r, ch, 1, Z, XR, R_("L0a_gamma"), R_("L0a_beta"))

        def mlp_pe(pe, r, w, act_done):
            for c in range(4):
                ins = pe.matmul(RING[c][:, :], w("w1")[:, c * P:(c + 1) * P], XT[:, :], start=True, stop=True)
                ins.then_inc(r.hid, 1)
            pe.wait_ge(act_done, 4)
            for t in range(NT):
                for c in range(4):
                    ins = pe.matmul(OUT[:, t * P:(t + 1) * P], QT[:, c, t * P:(t + 1) * P],
                                    w("w2")[:, c * P:(c + 1) * P], start=(c == 0), stop=(c == 3))
            ins.then_inc(r.out, 1)

        def step_L0_mlp():
            step = 1
            r = sets[step % 3]
            w = lambda n: W(step, n)
            with nc.Block() as block:
                @block.sync
                def _(sp):
                    clear_previous(sp, step)
                    load_weights(sp, r, 2)
                    sp.wait_ge(r.loaded, 16)

                @block.gpsimd
                def _(pool):
                    pool_power(pool, r, 1)
                    pool_power(pool, r, 2)

                @block.tensor
                def _(pe):
                    pe_xT(pe, r, XR)
                    pe.wait_ge(r.xT, 1)
                    mlp_pe(pe, r, w, r.hid_sb)

                @block.scalar
                def _(act):
                    act_xT(act, r)
                    for c in range(4):
                        act.wait_ge(r.hid, c + 1)
                        act.activation(QT[:, c, :], RING[c][:, :], ACT.Gelu, bias=C("L0a_b1", c)).then_inc(r.hid_sb, 1)

                @block.vector
                def _(dve):
                    ch = Chain(dve, r.dve_step)
                    ch.link(dve.tensor_tensor(Z[:, :, :], XR[:, :, :], row4(R_("L0a_b2")), ALU.add))
                    dve.wait_ge(r.out, 1)
                    ch.link(dve.tensor_tensor(flatZ, OUT[:, :], flatZ, ALU.add))
                    dve_layer_norm(dve, r, ch, 1, Z, XN, R_("L0a_gamma"), R_("L0a_beta"))
                    ch.link(dve.tensor_tensor(flatZ, flatX, flatXN, ALU.add))
                    dve_layer_norm(dve, r, ch, 2, Z, X)

        def step_L0_cross():
            step = 2
            r = sets[step % 3]
            w = lambda n: W(step, n)
            att = Attention(16, 8, CTX, keys=lambda c: KT[:, c, 0:CTX])
            rowsA = [([(w("wq")[:, c * P:(c + 1) * P], XT[:, :])], P, SEQ, "A", "act", QT[:, c, :],
                      (ACT.Relu, scaled[:, c:c + 1], RSQRT8)) for c in range(4)]
            rowsA += [([(w("wk")[:, c * P:(c + 1) * P], CT[:, :])], P, CTX, "A", "act", KT[:, c, 0:CTX],
                       (ACT.Relu, C("L0x_bk", c), 1.0)) for c in range(4)]
            vrow = R_("L0x_bv", CK).rearrange("p (h d) -> p h d", h=16)
            rowsA += [([(CT[:, c * CK:(c + 1) * CK], w("wv"))], CK, P, "D", "row", v_rows(CK, 16, 32, 8, c),
                       (vrow, ALU.add)) for c in range(2)]
            tab = Table(rowsA)
            with nc.Block() as block:
                @block.sync
                def _(sp):
                    clear_previous(sp, step)
                    load_weights(sp, r, 3)
                    sp.wait_ge(r.loaded, 16)

                @block.gpsimd
                def _(pool):
                    pool_clear_context(pool, r, 1024)
                    att.pool(pool, r, [(r.evac_act, tab.a)])
                    pool_power(pool, r, 1)

                @block.tensor
                def _(pe):
                    pe_xT(pe, r, X)
                    pe.wait_ge(r.xT, 1)
                    pe_table(pe, r, tab)
                    pe.wait_ge(r.evac_act, tab.a)
                    pe.wait_ge(r.ready, 1)
                    att.pe(pe, r)
                    att.project(pe, r, w("wo"))

                @block.scalar
                def _(act):
                    act_xT(act, r)
                    evacuate(act, r, tab, "A")
                    att.act(act, r)

                @block.vector
                def _(dve):
                    ch = Chain(dve, r.dve_step)
                    dve.wait_ge(r.ones, 2)
                    evacuate(dve, r, tab, "D")
                    dve.wait_ge(r.evac_dve, tab.d)
                    dve.tensor_scalar(V[0:CK, 0:1024], V[0:CK, 0:1024], 0.0, None, ALU.max).then_inc(r.ready, 1)
                    att.dve(dve, r)
                    dve.wait_ge(r.out, 1)
                    ch.link(dve.tensor_tensor(Z[:, :, :], tiles(OUT[:, :]), row4(R_("L0x_bo")), ALU.add))
                    ch.link(dve.scalar_tensor_tensor(flatZ, flatZ, 0.0, flatX, ALU.max, ALU.add))
                    dve_layer_norm(dve, r, ch, 1, Z, X)

        def step_L0_moe_attention():
            step = 3
            r = sets[step % 3]
            w = lambda n: W(step, n)
            H, E, DH = 8, 5, 64
            order = ["q", "k", "v"]
            sig = wide[:, 0:320].rearrange("p (t n) -> p t n", t=NT)
            rank = wide[:, 320:640]
            sel = wide[:, 640:960].rearrange("p (t n) -> p t n", t=NT)
            gated = wide[:, 960:1280].rearrange("p (t n) -> p t n", t=NT)
            t1, t2 = QT[:, 0:4, :].rearrange("p a b -> p (a b)"), QT[:, 4:8, :].rearrange("p a b -> p (a b)")
            prod = [wide[:, 1280 + 512 * i:1792 + 512 * i] for i in range(5)]
            sums = NB
            att = Attention(H, DH, SEQ, keys=lambda c: KT[:, c, :])
            tokens = wide[:, 0:2048].rearrange("p (t n) -> p t n", t=NT)
            gsel = small[:, 128:448]
            wsrc = {"q": w("wq"), "k": w("wk"), "v": w("wv")}
            with nc.Block() as block:
                @block.sync
                def _(sp):
                    clear_previous(sp, step)
                    load_weights(sp, r, 4)
                    sp.wait_ge(r.loaded, 16)

                @block.gpsimd
                def _(pool):
                    for i in range(NT * 3):
                        pool.wait_ge(r.part_used, 5 * (i + 1))
                        for e in range(1, 4):
                            pool.tensor_tensor(prod[0], prod[0], prod[e], ALU.add).then_inc(r.sum_step, 1)
                            pool.wait_ge(r.sum_step, 3 * i + e)
                        dst = v_rows(P, H, DH, DH, i // 3) if i % 3 == 2 else \
                            sums[:, i % 3, :].rearrange("p (h d) -> p h d", h=H)
                        if i % 3 == 0 and i >= 3:
                            pool.wait_ge(r.attnT, 2 * (i // 3) - 1)
                        if i % 3 == 1 and i >= 3:
                            pool.wait_ge(r.attnT, 2 * (i // 3))
                        pool.tensor_tensor(dst, prod[0].rearrange("p (h d) -> p h d", h=H),
                                           prod[4].rearrange("p (h d) -> p h d", h=H), ALU.add).then_inc(r.ready, 1)
                    pool.wait_ge(r.gate, 2)
                    att.pool(pool, r, [(r.attnT_sb, 2 * NT)])
                    pool_power(pool, r, 1)

                def _turn(pe, t, m):
                    k_ = 2 * t + m
                    pe.wait_ge(r.ready, 3 * t + m + 1)
                    if k_ >= 1:
                        pe.wait_ge(r.attnT_sb, k_)
                    for c in range(4):
                        ins = pe.transpose(TB[:, c * P:(c + 1) * P], sums[:, m, c * P:(c + 1) * P], ident)
                    ins.then_inc(r.attnT, 1)

                @block.tensor
                def _(pe):
                    pe_xT(pe, r, X)
                    pe.wait_ge(r.xT, 1)
                    for t in range(NT):
                        ins = pe.matmul(OUT[:, t * 80:(t + 1) * 80], XT[:, t * P:(t + 1) * P], w("wsd"),
                                        start=True, stop=True)
                    ins.then_inc(r.gate, 1)
                    n = 0
                    for t in range(NT):
                        for m, name in enumerate(order):
                            ws = wsrc[name].rearrange("p (h e d) -> p h e d", h=H, e=E)
                            for e in range(E):
                                if n >= 4:
                                    pe.wait_ge(r.part_used, n - 3)
                                pe.matmul(RING[n % 4][:, :], XT[:, t * P:(t + 1) * P], ws[:, :, e, :],
                                          start=True, stop=True).then_inc(r.part, 1)
                                n += 1
                            if m >= 1:
                                _turn(pe, t, m - 1)
                    pe.wait_ge(r.ready, NT * 3)
                    pe.wait_ge(r.attnT_sb, 2 * NT)
                    att.pe(pe, r)
                    pe.wait_ge(r.av_sb, att.chunks)
                    for qt in range(NT):
                        if qt >= 2:
                            pe.wait_ge(r.xT, qt)
                        for c in range(4):
                            ins = pe.transpose(PP[qt % 2][:, c * P:(c + 1) * P], QT[:, c, qt * P:(qt + 1) * P], ident)
                        ins.then_inc(r.part, 1)
                    for qt in range(NT):
                        pe.wait_ge(r.hid_dve, qt + 1)
                        if qt >= 1:
                            pe.wait_ge(r.hid_sb, qt)
                        for c in range(3):
                            n = 128 if c < 2 else 64
                            ins = pe.transpose(S[qt % 2][0:n, c * P:(c + 1) * P],
                                               NB[:, qt % 2, c * P:c * P + n], ident)
                        ins.then_inc(r.hid, 1)
                        pe.wait_ge(r.hid_sb, qt + 1)
                        for c in range(3):
                            n = 128 if c < 2 else 64
                            ins = pe.matmul(OUT[:, qt * P:(qt + 1) * P], KZ[0:n, qt % 2, c * P:(c + 1) * P],
                                            w("wo")[0:n, c * P:(c + 1) * P], start=(c == 0), stop=(c == 2))
                        ins.then_inc(r.outproj, 1)

                @block.scalar
                def _(act):
                    act_xT(act, r)
                    act.wait_ge(r.gate, 1)
                    act.activation(sig, OUT[:, 0:320].rearrange("p (t n) -> p t n", t=NT), ACT.Sigmoid
                                   ).then_inc(r.act_step, 1)
                    for t in range(NT):
                        for m in range(2):
                            act.wait_ge(r.attnT, 2 * t + m + 1)
                            if t == 0 and m == 0:
                                act.wait_ge(r.gate, 2)
                            dst = (QT if m == 0 else KT)[:, 0:4, t * P:(t + 1) * P]
                            act.activation(dst, TB[:, :].rearrange("p (c d) -> p c d", c=4), ACT.Copy
                                           ).then_inc(r.attnT_sb, 1)
                    att.act(act, r)
                    for qt in range(NT):
                        act.wait_ge(r.part, 5 * 3 * NT + qt + 1)
                        act.activation(tokens[:, qt, :], PP[qt % 2][:, :], ACT.Copy).then_inc(r.xT, 1)
                    for qt in range(NT):
                        act.wait_ge(r.hid, qt + 1)
                        if qt >= 2:
                            act.wait_ge(r.outproj, qt - 1)
                        act.activation(KZ[:, qt % 2, 0:256], S[qt % 2][:, 0:256], ACT.Copy)
                        act.activation(KZ[0:64, qt % 2, 256:384], S[qt % 2][0:64, 256:384], ACT.Copy
                                       ).then_inc(r.hid_sb, 1)

                @block.vector
                def _(dve):
                    ch = Chain(dve, r.dve_step)
                    dve.wait_ge(r.act_step, 1)
                    s3 = sig.rearrange("p t (g e) -> p (t g) e", e=E)
                    r3 = rank.rearrange("p (g e) -> p g e", e=E)
                    for g0 in range(0, 64, 32):
                        dve_ranks(dve, ch, s3[:, g0:g0 + 32, :], 32, E, R_("tri5"), r3[:, g0:g0 + 32, :], t1, t2)
                    ch.link(dve.tensor_scalar(sel.rearrange("p t n -> p (t n)"), rank, 2.5, None, ALU.is_lt))
                    ch.link(dve.tensor_tensor(gated, sig, sel, ALU.mult))
                    dve.tensor_scalar(gated[:, :, 40:80], gated[:, :, 40:80], DH ** -0.5, None, ALU.mult
                                      ).then_inc(r.gate, 1)
                    dve.wait_ge(r.gate, 2)
                    n = 0
                    for t in range(NT):
                        for m, name in enumerate(order):
                            g = gated[:, t, 40:80] if name == "q" else gated[:, t, 0:40]
                            g = g.rearrange("p (h e) -> p h e", e=E)
                            if n >= 5:
                                dve.wait_ge(r.ready, n // 5)
                            for e in range(E):
                                dve.wait_ge(r.part, n + 1)
                                dve.tensor_tensor(prod[e].rearrange("p (h d) -> p h d", h=H),
                                                  RING[n % 4][:, :].rearrange("p (h d) -> p h d", h=H),
                                                  g[:, :, e].unsqueeze(2).broadcast_to([P, H, DH]),
                                                  ALU.mult).then_inc(r.part_used, 1)
                                n += 1
                    ch.link(dve.tensor_copy(gsel.rearrange("p (t n) -> p t n", t=NT), sel))
                    dve.wait_ge(r.ready, 3 * NT)
                    att.dve(dve, r)
                    md = gsel.rearrange("p (t n) -> p t n", t=NT)[:, :, 40:80].rearrange("p t (h e) -> p t h e", e=E)
                    for qt in range(NT):
                        dve.wait_ge(r.xT, qt + 2)
                        o = tokens[:, qt, :].rearrange("p (h d) -> p h d", h=H)
                        if qt >= 1:
                            dve.wait_ge(r.hid_dve, qt)
                        if qt >= 2:
                            dve.wait_ge(r.hid, qt - 1)
                        tmp = [EX[:, e % 4, :].rearrange("p (h d) -> p h d", h=H) for e in range(E)]
                        for e in range(E):
                            ch.link(dve.tensor_tensor(tmp[e], o, md[:, qt, :, e].unsqueeze(2).broadcast_to([P, H, DH]),
                                                      ALU.mult))
                            ins = dve.tensor_reduce(NB[:, qt % 2, e * DH:(e + 1) * DH],
                                                    tmp[e].rearrange("p h d -> p d h"), AX.X, ALU.add)
                            if e == E - 1:
                                ins.then_inc(r.hid_dve, 1)
                            else:
                                ch.inc(ins)
                    tail(dve, r, ch, (r.outproj, NT), flatX)

        def step_L1_ssm():
            step = 4
            r = sets[step % 3]
            w = lambda n: W(step, n)
            tab = Table([([(w("win")[:, c * P:(c + 1) * P], XT[:, :])], P, SEQ, "AD"[c], "act" if c == 0 else "col",
                          QT[:, c, :], (ACT.Identity, C("L1a_bin", c), 1.0) if c == 0 else (C("L1a_bin", c),))
                         for c in range(2)])
            states = QT[0:16, 5, :]
            with nc.Block() as block:
                @block.sync
                def _(sp):
                    clear_previous(sp, step)
                    load_weights(sp, r, 5)
                    sp.wait_ge(r.loaded, 16)

                @block.gpsimd
                def _(pool):
                    pool_power(pool, r, 1)
                    pool_power(pool, r, 2)

                @block.tensor
                def _(pe):
                    pe.wait_ge(r.ready, 1)
                    pe_xT(pe, r, XN)
                    pe.wait_ge(r.xT, 1)
                    pe_table(pe, r, tab)
                    pe.wait_ge(r.evac_act, 1)
                    pe.wait_ge(r.evac_dve, 1)
                    for m in range(2):
                        for c in range(2):
                            ins = pe.matmul(S[m][0:16, :], w("ab")[:, 32 * c + 16 * m:32 * c + 16 * m + 16],
                                            QT[:, c, :], start=(c == 0), stop=(c == 1))
                    ins.then_inc(r.hid, 1)
                    pe.wait_ge(r.hid_dve, 1)
                    for c in range(2):
                        ins = pe.matmul(PP[c][:, :], w("c")[0:16, c * P:(c + 1) * P], states, start=True, stop=True)
                    ins.then_inc(r.part, 1)
                    pe.wait_ge(r.part_used, 2)
                    for t in range(NT):
                        for c in range(2):
                            ins = pe.matmul(OUT[:, t * P:(t + 1) * P], QT[:, 2 + c, t * P:(t + 1) * P],
                                            w("wout")[:, c * P:(c + 1) * P], start=(c == 0), stop=(c == 1))
                    ins.then_inc(r.out, 1)

                @block.scalar
                def _(act):
                    act_xT(act, r)
                    evacuate(act, r, tab, "A")
                    act.wait_ge(r.hid, 1)
                    act.activation(QT[0:16, 4, :], S[0][0:16, :], ACT.Sigmoid).then_inc(r.hid_sb, 1)
                    act.wait_ge(r.part, 1)
                    for c in range(2):
                        act.activation(QT[:, 2 + c, :], PP[c][:, :], ACT.Copy).then_inc(r.part_used, 1)

                @block.vector
                def _(dve):
                    ch = Chain(dve, r.dve_step)
                    dve_layer_norm(dve, r, ch, 1, X, XN, R_("L1a_nw"), R_("L1a_nb"))
                    dve.sem_inc(r.ready, 1)
                    evacuate(dve, r, tab, "D")
                    dve.wait_ge(r.hid_sb, 1)
                    dve.wait_ge(r.hid, 1)
                    dve.tensor_tensor_scan(states, QT[0:16, 4, :], S[1][0:16, :], 0.0, ALU.mult, ALU.add
                                           ).then_inc(r.hid_dve, 1)
                    ch.link(dve.scalar_tensor_tensor(Z[:, :, :], X[:, :, :], 2.0, row4(R_("L1a_bout")),
                                                     ALU.mult, ALU.add))
                    tail(dve, r, ch, (r.out, 1), flatZ, 2)
                    ch.link(dve.tensor_copy(flatXR, flatX))

        def step_L1_attention(l, cross):
            step = 6 if cross else 5
            r = sets[step % 3]
            w = lambda n: W(step, n)
            NK = CTX if cross else SEQ
            src = CT if cross else XT
            kc, nch = (CK, 2) if cross else (P, NT)
            rawq = wide[:, 2048:4096].rearrange("p (c t) -> p c t", c=4)
            rawk = (NB[:, :, :].rearrange("p a t -> p (a t)")[:, 0:4 * CTX] if cross else wide[:, 0:2048]
                    ).rearrange("p (c t) -> p c t", c=4)
            raw = lambda c: rawq[:, c, :] if c < 4 else rawk[:, c - 4, :]
            gain, bias = w("gain"), w("bias")
            added = None if cross else (lambda h, qt: maskb[:, :])
            att = Attention(8, 64, NK, added=added, keys=lambda c: KT[:, c, 0:NK])
            rowsA = [([(w("wq")[:, c * P:(c + 1) * P], XT[:, :])], P, SEQ, "A", "scale", raw(c), (0.125,))
                     for c in range(4)]
            rowsA += [([(w("wk")[:, c * P:(c + 1) * P], src[:, :])], P, NK, "A", "copy", raw(4 + c), None)
                      for c in range(4)]
            tab = Table(rowsA)
            tab2 = Table([([(K("rot"), raw(c))], P, SEQ if c < 4 else NK, "D", "row",
                           (QT[:, c, :] if c < 4 else KT[:, c - 4, 0:NK]),
                           (K("sin")[:, 0:(SEQ if c < 4 else NK)], ALU.mult)) for c in range(8)], tab)
            tab3 = Table([([(src[:, c * kc:(c + 1) * kc], w("wv"))], kc, SEQ, "A", "copy",
                           v_rows(kc, 8, 64, 64, c), None) for c in range(nch)], tab2)
            with nc.Block() as block:
                @block.sync
                def _(sp):
                    clear_previous(sp, step)
                    nxt = step + 1
                    sp.dma_start(arenas[nxt % 3][:, 0:WIDTH[nxt]],
                                 io[f"w{nxt}"][bass.ds(l, 1)].rearrange("o p n -> p (o n)")).then_inc(r.loaded, 16)
                    sp.wait_ge(r.loaded, 16)

                @block.gpsimd
                def _(pool):
                    pool_power(pool, r, 1, 44)
                    if cross:
                        pool_clear_context(pool, r, 1024)
                    for c in range(8):
                        n = SEQ if c < 4 else NK
                        pool.wait_ge(r.evac_act, c + 1)
                        pool.wait_ge(r.proj, 9 + c)
                        pool.tensor_tensor(raw(c), raw(c), K("cos")[:, 0:n], ALU.mult).then_inc(r.rot_mul, 1)
                    att.pool(pool, r, [(r.ready, 8)])

                @block.tensor
                def _(pe):
                    pe.wait_ge(r.early, 1)
                    pe_xT(pe, r, XN)
                    pe.wait_ge(r.xT, 1)
                    pe_table(pe, r, tab)
                    pe.wait_ge(r.evac_act, tab.a)
                    pe_table(pe, r, tab2)
                    pe_table(pe, r, tab3)
                    pe.wait_ge(r.ready, 8)
                    pe.wait_ge(r.evac_act, tab3.a)
                    att.pe(pe, r)
                    att.project(pe, r, w("wo"))

                @block.scalar
                def _(act):
                    act_xT(act, r)
                    evacuate(act, r, tab, "A")
                    if cross:
                        act.wait_ge(r.ones, 2)
                    evacuate(act, r, tab3, "A")
                    att.act(act, r)

                @block.vector
                def _(dve):
                    ch = Chain(dve, r.dve_step)
                    dve_rms_norm(dve, r, ch, 1, X, XN, gain)
                    dve.sem_inc(r.early, 1)
                    evacuate(dve, r, tab2, "D")
                    for c in range(8):
                        n = SEQ if c < 4 else NK
                        dst = QT[:, c, :] if c < 4 else KT[:, c - 4, 0:NK]
                        dve.wait_ge(r.evac_dve, c + 1)
                        dve.wait_ge(r.rot_mul, c + 1)
                        dve.tensor_tensor(dst, dst, raw(c), ALU.add).then_inc(r.ready, 1)
                    att.dve(dve, r)
                    ch.link(dve.tensor_tensor(X[:, :, :], X[:, :, :], row4(bias), ALU.add))
                    dve.wait_ge(r.out, 1)
                    ch.link(dve.tensor_tensor(flatX, OUT[:, :], flatX, ALU.add))

        def step_L1_mlp(l):
            step = 7
            r = sets[step % 3]
            w = lambda n: W(step, n)
            gain, bias = w("gain"), w("bias")
            with nc.Block() as block:
                @block.sync
                def _(sp):
                    clear_previous(sp, step)
                    sp.dma_start(arenas[2][:, 0:WIDTH[5]],
                                 io["w5next"][bass.ds(l, 1)].rearrange("o p n -> p (o n)")).then_inc(r.loaded, 16)
                    sp.wait_ge(r.loaded, 16)

                @block.gpsimd
                def _(pool):
                    pool_power(pool, r, 1, 44)

                @block.tensor
                def _(pe):
                    pe.wait_ge(r.early, 1)
                    pe_xT(pe, r, XN)
                    pe.wait_ge(r.xT, 1)
                    mlp_pe(pe, r, w, r.hid_sb)

                @block.scalar
                def _(act):
                    act_xT(act, r)
                    for c in range(4):
                        act.wait_ge(r.hid, c + 1)
                        act.activation(QT[:, c, :], RING[c][:, :], ACT.Gelu,
                                       bias=cols[:, bass.ds(cols_at["L1x_fb1"][0] + c + 4 * l, 1)]
                                       ).then_inc(r.hid_sb, 1)

                @block.vector
                def _(dve):
                    ch = Chain(dve, r.dve_step)
                    dve_rms_norm(dve, r, ch, 1, X, XN, gain)
                    dve.sem_inc(r.early, 1)
                    ch.link(dve.tensor_tensor(X[:, :, :], X[:, :, :], row4(bias), ALU.add))
                    dve.wait_ge(r.out, 1)
                    ch.link(dve.tensor_tensor(flatX, OUT[:, :], flatX, ALU.add))

        def step_L1_final():
            step = 8
            r = sets[step % 3]
            with nc.Block() as block:
                @block.sync
                def _(sp):
                    clear_previous(sp, step)
                    load_weights(sp, r, 9)
                    sp.wait_ge(r.loaded, 16)

                @block.gpsimd
                def _(pool):
                    pool_power(pool, r, 1, 44)
                    pool_power(pool, r, 2)

                @block.vector
                def _(dve):
                    ch = Chain(dve, r.dve_step)
                    dve_rms_norm(dve, r, ch, 1, X, XN, R_("L1x_gout"))
                    ch.link(dve.tensor_tensor(flatXN, flatXN, flatXR, ALU.add))
                    dve_layer_norm(dve, r, ch, 2, XN, X)

        def step_experts(step, E, swiglu):
            r = sets[step % 3]
            w = lambda n: W(step, n)
            gname = "gate" if swiglu else "wr"
            gates = small[:, 512:512 + NT * E]
            g3 = gates.rearrange("p (t e) -> p t e", e=E)
            acc = XN
            per = 8 if swiglu else 4
            hid = lambda e: QT[:, 4 * (e % 2):4 * (e % 2) + 4, :]
            with nc.Block() as block:
                @block.sync
                def _(sp):
                    clear_previous(sp, step)
                    if step == 9:
                        load_weights(sp, r, 10)
                        sp.wait_ge(r.loaded, 16)

                @block.gpsimd
                def _(pool):
                    pool_power(pool, r, 1)

                @block.tensor
                def _(pe):
                    pe_xT(pe, r, X)
                    pe.wait_ge(r.xT, 1)
                    for t in range(NT):
                        ins = pe.matmul(TB[:, t * E:(t + 1) * E], XT[:, t * P:(t + 1) * P], w(gname),
                                        start=True, stop=True)
                    ins.then_inc(r.gate, 1)
                    n = 0
                    for e in range(E + 1):
                        if e < E:
                            for c in range(4):
                                for m in range(2 if swiglu else 1):
                                    src = w("w3") if m else w("w1")
                                    if n >= 4:
                                        pe.wait_ge(r.part_used, n - 3)
                                    pe.matmul(RING[n % 4][:, :], src[:, e * 512 + c * P:e * 512 + (c + 1) * P],
                                              XT[:, :], start=True, stop=True).then_inc(r.part, 1)
                                    n += 1
                        if e >= 1:
                            f = e - 1
                            pe.wait_ge(r.hid_sb, 4 * e)
                            if f >= 2:
                                pe.wait_ge(r.hid_dve, f - 1)
                            for t in range(NT):
                                for c in range(4):
                                    ins = pe.matmul(S[f % 2][:, t * P:(t + 1) * P],
                                                    hid(f)[:, c, t * P:(t + 1) * P],
                                                    w("w2")[:, f * 512 + c * P:f * 512 + (c + 1) * P],
                                                    start=(c == 0), stop=(c == 3))
                            ins.then_inc(r.out, 1)

                if swiglu:
                    @block.scalar
                    def _(act):
                        act_xT(act, r)
                        act.wait_ge(r.gate, 2)
                        act.activation(small[:, 640:648], small[:, 600:608], ACT.Sigmoid).then_inc(r.act_step, 1)
                        for e in range(E):
                            for c in range(4):
                                n = 8 * e + 2 * c
                                act.wait_ge(r.part, n + 1)
                                if n >= 4:
                                    act.wait_ge(r.hid_sb, n // 2 - 1)
                                act.activation(NB[:, (n // 2) % 2, :], RING[n % 4][:, :], ACT.Silu
                                               ).then_inc(r.ready, 1)
                else:
                    @block.scalar
                    def _(act):
                        act_xT(act, r)
                        for e in range(E):
                            for c in range(4):
                                n = 4 * e + c
                                act.wait_ge(r.part, n + 1)
                                if e >= 2 and c == 0:
                                    act.wait_ge(r.out, e - 1)
                                act.activation(hid(e)[:, c, :], RING[n % 4][:, :], ACT.Relu,
                                               bias=C("L1f_be1", n)).then_inc(r.part_used, 1)
                                act.wait_ge(r.part_used, n + 1)
                                act.sem_inc(r.hid_sb, 1)

                @block.vector
                def _(dve):
                    ch = Chain(dve, r.dve_step)
                    lg, rank = small[:, 544:544 + NT * E], small[:, 608:608 + 32]
                    l3, r3 = lg.rearrange("p (t e) -> p t e", e=E), rank[:, 0:NT * E].rearrange("p (t e) -> p t e", e=E)
                    if swiglu:
                        lg = small[:, 704:704 + NT * E]
                        l3 = lg.rearrange("p (t e) -> p t e", e=E)
                        rank = small[:, 740:740 + NT * E]
                        r3 = rank.rearrange("p (t e) -> p t e", e=E)
                    t1, t2 = wide[:, 0:512], wide[:, 512:1024]
                    dve.wait_ge(r.gate, 1)
                    if swiglu:
                        ch.link(dve.tensor_copy(lg, TB[:, 0:NT * E]))
                    else:
                        ch.link(dve.tensor_tensor(l3, TB[:, 0:NT * E].rearrange("p (t e) -> p t e", e=E),
                                                  R_("L1f_br").unsqueeze(1).broadcast_to([P, NT, E]), ALU.add))
                    dve_ranks(dve, ch, l3, NT, E, R_("tri8" if swiglu else "tri4"), r3, t1, t2)
                    if swiglu:
                        first, second = small[:, 780:812], small[:, 820:852]
                        ch.inc(dve.tensor_scalar(first, rank, 0.0, None, ALU.is_equal))
                        ch.link(dve.tensor_scalar(second, rank, 1.0, None, ALU.is_equal))
                        fl, sl = wide[:, 1024:1056], wide[:, 1056:1088]
                        ch.inc(dve.tensor_tensor(fl, first, lg, ALU.mult))
                        ch.link(dve.tensor_tensor(sl, second, lg, ALU.mult))
                        v12 = wide[:, 1088:1096]
                        ch.inc(dve.tensor_reduce(v12[:, 0:4], fl.rearrange("p (t e) -> p t e", e=E), AX.X, ALU.add))
                        ch.link(dve.tensor_reduce(v12[:, 4:8], sl.rearrange("p (t e) -> p t e", e=E), AX.X, ALU.add))
                        ch.inc(dve.tensor_tensor(small[:, 600:604], v12[:, 0:4], v12[:, 4:8], ALU.subtract))
                        dve.tensor_tensor(small[:, 604:608], v12[:, 4:8], v12[:, 0:4], ALU.subtract).then_inc(r.gate, 1)
                        dve.wait_ge(r.act_step, 1)
                        ch.inc(dve.tensor_tensor(first.rearrange("p (t e) -> p t e", e=E),
                                                 first.rearrange("p (t e) -> p t e", e=E),
                                                 small[:, 640:644].unsqueeze(2).broadcast_to([P, NT, E]), ALU.mult))
                        ch.link(dve.tensor_tensor(second.rearrange("p (t e) -> p t e", e=E),
                                                  second.rearrange("p (t e) -> p t e", e=E),
                                                  small[:, 644:648].unsqueeze(2).broadcast_to([P, NT, E]), ALU.mult))
                        ch.link(dve.tensor_tensor(gates, first, second, ALU.add))
                    else:
                        ch.link(dve.tensor_scalar(gates, rank[:, 0:NT * E], 0.0, None, ALU.is_equal))
                    ch.link(dve.tensor_copy(flatZ, flatX))
                    for e in range(E + 1):
                        if swiglu and e < E:
                            for c in range(4):
                                n = 8 * e + 2 * c
                                if e >= 2 and c == 0:
                                    dve.wait_ge(r.out, e - 1)
                                dve.wait_ge(r.ready, n // 2 + 1)
                                dve.wait_ge(r.part, n + 2)
                                dve.tensor_tensor(hid(e)[:, c, :], RING[(n + 1) % 4][:, :], NB[:, (n // 2) % 2, :],
                                                  ALU.mult).then_inc(r.hid_sb, 1)
                                dve.wait_ge(r.hid_sb, n // 2 + 1)
                                dve.sem_inc(r.part_used, 2)
                        if e < 1:
                            continue
                        f = e - 1
                        dve.wait_ge(r.out, e)
                        src = S[f % 2]
                        if not swiglu:
                            tmp = wide[:, 2048:2560]
                            ch.link(dve.tensor_tensor(tiles(tmp), tiles(src[:, :]),
                                                      row4(R_("L1f_be2")[:, f * P:(f + 1) * P]), ALU.add))
                            src = tmp
                        for t in range(NT):
                            ins = dve.scalar_tensor_tensor(Z[:, t, :], src[:, t * P:(t + 1) * P],
                                                           g3[:, t, f:f + 1], Z[:, t, :], ALU.mult, ALU.add)
                            ch.inc(ins)
                        ch.join()
                        dve.sem_inc(r.hid_dve, 1)
                    dve_layer_norm(dve, r, ch, 1, Z, X)

        def step_L2_attention():
            step = 10
            r = sets[step % 3]
            w = lambda n: W(step, n)
            att = Attention(1, P, SEQ, keys=lambda c: KT[:, 0, :])
            tab = Table([([(w("wq"), XT[:, :])], P, SEQ, "A", "act", QT[:, 1, :], (ACT.Identity, C("L2a_bq"), 1.0)),
                         ([(w("wk"), XT[:, :])], P, SEQ, "D", "col", KT[:, 1, :], (C("L2a_bk"),))]
                        + [([(XT[:, t * P:(t + 1) * P], w("wv"))], P, P, "D", "row", V[:, t * P:(t + 1) * P],
                            (R_("L2a_bv"), ALU.add)) for t in range(NT)])
            tab2 = Table([([(K("pair"), QT[:, 1, :])], P, SEQ, "D", "row", QT[:, 2, :], (w("sincos"), ALU.mult)),
                          ([(K("pair"), KT[:, 1, :])], P, SEQ, "D", "row", KT[:, 0, :], (w("sincos"), ALU.mult))], tab)
            with nc.Block() as block:
                @block.sync
                def _(sp):
                    clear_previous(sp, step)
                    load_weights(sp, r, 11)
                    sp.wait_ge(r.loaded, 16)

                @block.gpsimd
                def _(pool):
                    pool.wait_ge(r.evac_dve, tab2.d)
                    pool.tensor_scalar(QT[:, 0, :], QT[:, 2, :], 0.125, None, ALU.mult).then_inc(r.ready, 1)
                    pool_power(pool, r, 1)

                @block.tensor
                def _(pe):
                    pe_xT(pe, r, X)
                    pe.wait_ge(r.xT, 1)
                    pe_table(pe, r, tab)
                    pe.wait_ge(r.evac_act, tab.a)
                    pe.wait_ge(r.evac_dve, tab.d)
                    pe_table(pe, r, tab2)
                    pe.wait_ge(r.evac_dve, tab2.d)
                    pe.wait_ge(r.ready, 1)
                    att.pe(pe, r)
                    pe.wait_ge(r.av_sb, 1)
                    for t in range(NT):
                        ins = pe.transpose(OUT[:, t * P:(t + 1) * P], QT[:, 0, t * P:(t + 1) * P], ident)
                    ins.then_inc(r.out, 1)

                @block.scalar
                def _(act):
                    act_xT(act, r)
                    evacuate(act, r, tab, "A")
                    att.act(act, r)

                @block.vector
                def _(dve):
                    ch = Chain(dve, r.dve_step)
                    evacuate(dve, r, tab, "D")
                    evacuate(dve, r, tab2, "D")
                    att.dve(dve, r)
                    tail(dve, r, ch, (r.out, 1), flatX)

        def step_L2_sigmoid_attention():
            step = 11
            r = sets[step % 3]
            w = lambda n: W(step, n)
            tab = Table([([(w("wq"), XT[:, :])], 32, SEQ, "A", "act", QT[0:32, 0, :],
                          (ACT.Identity, C("L2x_bq", parts=32), 1.0)),
                         ([(w("wk"), CT[:, :])], 32, CTX, "D", "col", KT[0:32, 0, 0:CTX], (C("L2x_bk", parts=32),))]
                        + [([(CT[:, c * CK:(c + 1) * CK], w("wv"))], CK, P, "D", "row", V[0:CK, c * P:(c + 1) * P],
                            (R_("L2x_bv", CK), ALU.add)) for c in range(2)])
            with nc.Block() as block:
                @block.sync
                def _(sp):
                    clear_previous(sp, step)
                    load_weights(sp, r, 12)
                    sp.wait_ge(r.loaded, 16)

                @block.gpsimd
                def _(pool):
                    pool_power(pool, r, 1)

                @block.tensor
                def _(pe):
                    pe_xT(pe, r, X)
                    pe.wait_ge(r.xT, 1)
                    pe_table(pe, r, tab)
                    pe.wait_ge(r.evac_act, tab.a)
                    pe.wait_ge(r.evac_dve, tab.d)
                    for c in range(2):
                        ins = pe.matmul(S[c][0:CK, :], KT[0:32, 0, c * CK:(c + 1) * CK], QT[0:32, 0, :],
                                        start=True, stop=True)
                        ins.then_inc(r.scores, 1)
                    pe.wait_ge(r.exped, 2)
                    for t in range(NT):
                        for c in range(2):
                            ins = pe.matmul(OUT[:, t * P:(t + 1) * P], EX[0:CK, c, t * P:(t + 1) * P],
                                            V[0:CK, c * P:(c + 1) * P], start=(c == 0), stop=(c == 1))
                    ins.then_inc(r.out, 1)

                @block.scalar
                def _(act):
                    act_xT(act, r)
                    evacuate(act, r, tab, "A")
                    for c in range(2):
                        act.wait_ge(r.scores, c + 1)
                        act.activation(EX[0:CK, c, :], S[c][0:CK, :], ACT.Sigmoid, scale=32.0 ** -0.5).then_inc(r.exped, 1)

                @block.vector
                def _(dve):
                    ch = Chain(dve, r.dve_step)
                    evacuate(dve, r, tab, "D")
                    tail(dve, r, ch, (r.out, 1), flatX)

        def step_L2_lora_experts():
            step = 12
            r = sets[step % 3]
            w = lambda n: W(step, n)
            E = 8
            hsum = wide[:, 0:2048].rearrange("p (t f) -> p t f", t=NT)
            part = [wide[:, 2048 + 512 * i:2560 + 512 * i] for i in range(2)]
            gates = small[:, 512:544]
            g3 = gates.rearrange("p (t e) -> p t e", e=E)
            tab = Table([([(w("loraA")[:, c * P:(c + 1) * P], XT[:, :])], P, SEQ, "D", "col", QT[:, c, :],
                          (C("L2f_one"),)) for c in range(2)])
            with nc.Block() as block:
                @block.sync
                def _(sp):
                    clear_previous(sp, step)
                    load_weights(sp, r, 13)
                    sp.wait_ge(r.loaded, 16)

                @block.gpsimd
                def _(pool):
                    for n in range(NT * E):
                        t, e = n % NT, n // NT
                        pool.wait_ge(r.hid_sb, n + 1)
                        if e == 0:
                            pool.tensor_copy(hsum[:, t, :], part[n % 2]).then_inc(r.ready, 1)
                        else:
                            pool.wait_ge(r.ready, n - NT + 1)
                            pool.tensor_tensor(hsum[:, t, :], hsum[:, t, :], part[n % 2], ALU.add).then_inc(r.ready, 1)
                    pool_power(pool, r, 1)

                @block.tensor
                def _(pe):
                    pe_xT(pe, r, X)
                    pe.wait_ge(r.xT, 1)
                    for t in range(NT):
                        ins = pe.matmul(TB[:, t * E:(t + 1) * E], XT[:, t * P:(t + 1) * P], w("gate"),
                                        start=True, stop=True)
                    ins.then_inc(r.gate, 1)
                    pe_table(pe, r, tab)
                    pe.wait_ge(r.evac_dve, tab.d)
                    for n in range(NT * E):
                        t, e = n % NT, n // NT
                        if n >= 4:
                            pe.wait_ge(r.hid_sb, n - 3)
                        c = e // 4
                        pe.matmul(RING[n % 4][:, :], XT[:, t * P:(t + 1) * P], w("wi"), start=True, stop=False)
                        pe.matmul(RING[n % 4][:, :], QT[:, c, t * P:(t + 1) * P],
                                  w("loraB")[:, e * 512:(e + 1) * 512], start=False, stop=True).then_inc(r.hid, 1)
                    pe.wait_ge(r.gate, 3)
                    for t in range(NT):
                        pe.wait_ge(r.ready, NT * (E - 1) + t + 1)
                        if t >= 2:
                            pe.wait_ge(r.attnT_sb, t - 1)
                        for c in range(4):
                            ins = pe.transpose(S[t % 2][:, c * P:(c + 1) * P], hsum[:, t, c * P:(c + 1) * P], ident)
                        ins.then_inc(r.attnT, 1)
                        pe.wait_ge(r.attnT_sb, t + 1)
                        for c in range(4):
                            ins = pe.matmul(OUT[:, t * P:(t + 1) * P], KT[:, t, c * P:(c + 1) * P],
                                            w("wo")[:, c * P:(c + 1) * P], start=(c == 0), stop=(c == 3))
                    ins.then_inc(r.out, 1)

                @block.scalar
                def _(act):
                    act_xT(act, r)
                    act.wait_ge(r.gate, 2)
                    act.activation(small[:, 576:608], small[:, 544:576], ACT.Exp).then_inc(r.act_step, 1)
                    act.wait_ge(r.gate, 3)
                    for n in range(NT * E):
                        t, e = n % NT, n // NT
                        act.wait_ge(r.hid, n + 1)
                        if n >= 2:
                            act.wait_ge(r.ready, n - 1)
                        act.activation(part[n % 2], RING[n % 4][:, :], ACT.Relu, scale=g3[:, t, e:e + 1]
                                       ).then_inc(r.hid_sb, 1)
                    for t in range(NT):
                        act.wait_ge(r.attnT, t + 1)
                        act.activation(KT[:, t, :], S[t % 2][:, :], ACT.Copy).then_inc(r.attnT_sb, 1)

                @block.vector
                def _(dve):
                    ch = Chain(dve, r.dve_step)
                    lg = small[:, 544:576]
                    l3 = lg.rearrange("p (t e) -> p t e", e=E)
                    mx, ex, rank, sel = small[:, 608:612], small[:, 576:608], small[:, 640:672], small[:, 672:704]
                    e3, r3 = (z.rearrange("p (t e) -> p t e", e=E) for z in (ex, rank))
                    s3 = sel.rearrange("p (t e) -> p t e", e=E)
                    dve.wait_ge(r.gate, 1)
                    ch.link(dve.tensor_tensor(l3, TB[:, 0:32].rearrange("p (t e) -> p t e", e=E),
                                              R_("L2f_gb").unsqueeze(1).broadcast_to([P, NT, E]), ALU.add))
                    ch.link(dve.tensor_reduce(mx, l3, AX.X, ALU.max))
                    dve.tensor_tensor(l3, l3, mx.unsqueeze(2).broadcast_to([P, NT, E]), ALU.subtract).then_inc(r.gate, 1)
                    evacuate(dve, r, tab, "D")
                    dve.wait_ge(r.act_step, 1)
                    ch.link(dve.tensor_reduce(small[:, 612:616], e3, AX.X, ALU.add))
                    ch.link(dve.reciprocal(small[:, 616:620], small[:, 612:616]))
                    ch.link(dve.tensor_tensor(e3, e3, small[:, 616:620].unsqueeze(2).broadcast_to([P, NT, E]), ALU.mult))
                    dve_ranks(dve, ch, e3, NT, E, R_("tri8"), r3, NB[:, 0, :], NB[:, 1, :])
                    ch.link(dve.tensor_scalar(sel, rank, 1.5, None, ALU.is_lt))
                    ch.link(dve.tensor_tensor(ex, ex, sel, ALU.mult))
                    ch.link(dve.tensor_reduce(small[:, 620:624], e3, AX.X, ALU.add))
                    dve.tensor_tensor(g3, s3, small[:, 620:624].unsqueeze(2).broadcast_to([P, NT, E]), ALU.mult
                                      ).then_inc(r.gate, 1)
                    dve.wait_ge(r.gate, 3)
                    ch.link(dve.tensor_reduce(small[:, 624:628], g3, AX.X, ALU.add))
                    for t in range(NT):
                        ch.inc(dve.scalar_tensor_tensor(Z[:, t, :], R_("L2f_bo"), small[:, 624 + t:625 + t],
                                                        X[:, t, :], ALU.mult, ALU.add))
                    ch.join()
                    tail(dve, r, ch, (r.out, 1), flatZ)

        def step_L3_attention():
            step = 13
            r = sets[step % 3]
            w = lambda n: W(step, n)
            att = Attention(16, 8, SEQ, causal=True, keys=lambda c: KT[:, c, :],
                            added=lambda h, qt: relbias[:, h, SEQ - P * (qt + 1):SEQ])
            rowsA = [([(w("wq")[:, c * P:(c + 1) * P], XT[:, :])], P, SEQ, "A", "act", QT[:, c, :],
                      (ACT.Identity, scaled[:, 4 + c:5 + c], RSQRT8)) for c in range(4)]
            rowsA += [([(w("wk")[:, c * P:(c + 1) * P], XT[:, :])], P, SEQ, "D", "col", KT[:, c, :],
                       (C("L3a_bk", c),)) for c in range(4)]
            vrow = R_("L3a_bv").rearrange("p (h d) -> p h d", h=16)
            rowsA += [([(XT[:, t * P:(t + 1) * P], w("wv"))], P, P, "D", "row", v_rows(P, 16, 32, 8, t),
                       (vrow, ALU.add)) for t in range(NT)]
            tab = Table(rowsA)
            with nc.Block() as block:
                @block.sync
                def _(sp):
                    clear_previous(sp, step)
                    load_weights(sp, r, 14)
                    sp.wait_ge(r.loaded, 16)

                @block.gpsimd
                def _(pool):
                    pool.memset(V[:, 0:2048], 0.0).then_inc(r.ones, 1)
                    att.pool(pool, r, [(r.evac_dve, tab.d)])
                    pool_power(pool, r, 1)

                @block.tensor
                def _(pe):
                    pe_xT(pe, r, X)
                    pe.wait_ge(r.xT, 1)
                    pe_table(pe, r, tab)
                    pe.wait_ge(r.evac_act, tab.a)
                    pe.wait_ge(r.evac_dve, tab.d)
                    att.pe(pe, r)
                    att.project(pe, r, w("wo"))

                @block.scalar
                def _(act):
                    act_xT(act, r)
                    evacuate(act, r, tab, "A")
                    att.act(act, r)

                @block.vector
                def _(dve):
                    ch = Chain(dve, r.dve_step)
                    dve.wait_ge(r.ones, 1)
                    evacuate(dve, r, tab, "D")
                    att.dve(dve, r)
                    ch.link(dve.tensor_tensor(Z[:, :, :], X[:, :, :], row4(R_("L3a_bo")), ALU.add))
                    tail(dve, r, ch, (r.out, 1), flatZ)

        def step_L3_cross():
            step = 14
            r = sets[step % 3]
            w = lambda n: W(step, n)
            keys = KT[:, :, :].rearrange("p c t -> p (c t)")[:, 0:8 * CTX].rearrange("p (c t) -> p c t", c=8)
            att = Attention(16, 64, CTX, keys=lambda c: keys[:, c, :],
                            added=lambda h, qt: padb[:, min(qt, 2), :])
            rowsA = [([(w("wq")[:, c * P:(c + 1) * P], XT[:, :])], P, SEQ, "A", "act", QT[:, c, :],
                      (ACT.Identity, scaled[:, 8 + c:9 + c], 0.125)) for c in range(8)]
            rowsA += [([(w("wk")[:, c * P:(c + 1) * P], CT[:, :])], P, CTX, "D", "col", keys[:, c, :],
                       (C("L3x_bk", c),)) for c in range(8)]
            for c in range(2):
                for m in range(2):
                    rowsA.append(([(CT[:, c * CK:(c + 1) * CK], w("wv")[:, m * 512:(m + 1) * 512])], CK, SEQ, "D", "row",
                                  v_rows(CK, 16, 64, 64, c)[:, 8 * m:8 * m + 8, :],
                                  (KZ[0:CK, 2 + m, :].rearrange("p (h d) -> p h d", h=8),
                                   ALU.add)))
            tab = Table(rowsA)
            with nc.Block() as block:
                @block.sync
                def _(sp):
                    clear_previous(sp, step)
                    sp.dma_start(KZ[:, 2:4, :].rearrange("p a t -> p (a t)"),
                                 io["L3x_bv"][0:1, :].broadcast_to([P, 1024])).then_inc(r.early, 16)
                    load_weights(sp, r, 15)
                    sp.wait_ge(r.loaded, 16)

                @block.gpsimd
                def _(pool):
                    pool_clear_context(pool, r, 2048)
                    att.pool(pool, r, [(r.evac_dve, tab.d)])
                    pool_power(pool, r, 1)

                @block.tensor
                def _(pe):
                    pe_xT(pe, r, X)
                    pe.wait_ge(r.xT, 1)
                    pe_table(pe, r, tab)
                    pe.wait_ge(r.evac_act, tab.a)
                    pe.wait_ge(r.evac_dve, tab.d)
                    att.pe(pe, r)
                    att.project(pe, r, w("wo"))

                @block.scalar
                def _(act):
                    act_xT(act, r)
                    evacuate(act, r, tab, "A")
                    att.act(act, r)

                @block.vector
                def _(dve):
                    ch = Chain(dve, r.dve_step)
                    dve.wait_ge(r.ones, 2)
                    dve.wait_ge(r.early, 16)
                    evacuate(dve, r, tab, "D")
                    att.dve(dve, r)
                    ch.link(dve.tensor_tensor(Z[:, :, :], X[:, :, :], row4(R_("L3x_bo")), ALU.add))
                    tail(dve, r, ch, (r.out, 1), flatZ)

        def step_store(b):
            step = 16
            r = sets[step % 3]
            with nc.Block() as block:
                @block.sync
                def _(sp):
                    clear_previous(sp, step)
                    sp.dma_start(io["out"][bass.ds(b, 1)].rearrange("o (t p) d -> p (o t) d", p=P), X[:, :, :]
                                 ).then_inc(r.loaded, 16)
                    load_weights(sp, r, 0)
                    sp.wait_ge(r.loaded, 32)

        with nc.Fori(0, NBATCH) as b:
            step_load(b)
            step_L0_linear_attention()
            step_L0_mlp()
            step_L0_cross()
            step_L0_moe_attention()
            step_L1_ssm()
            with nc.Fori(0, LAYERS) as l:
                step_L1_attention(l, False)
                step_L1_attention(l, True)
                step_L1_mlp(l)
            step_L1_final()
            step_experts(9, 4, False)
            step_L2_attention()
            step_L2_sigmoid_attention()
            step_L2_lora_experts()
            step_L3_attention()
            step_L3_cross()
            step_experts(15, 8, True)
            step_store(b)



def pack(np, parts, widths):
    out = np.zeros((P, sum(widths)), np.float32)
    at = 0
    for a, n in zip(parts, widths):
        assert a.shape[1] == n, (a.shape, n)
        out[:a.shape[0], at:at + n] = a
        at += n
    return out


def chunked(np, a):
    n = -(-a.shape[0] // P)
    full = np.zeros((n * P, a.shape[1]), a.dtype)
    full[:a.shape[0]] = a
    return full.reshape(n, P, -1).transpose(1, 0, 2).reshape(P, -1)


def pad_heads(np, a, real, padded):
    lead = a.shape[:-1]
    out = np.zeros(lead + (a.shape[-1] // real, padded), a.dtype)
    out[..., :real] = a.reshape(lead + (-1, real))
    return out.reshape(lead + (-1,))


def columns(np, v):
    return chunked(np, v.reshape(-1, 1))


def layout(np, i):
    out = {"x": i["x"], "ctxT": i["ctx_1024"].transpose(0, 2, 1), "mask1": i["mask_BxS_bf1"],
           "mask2": i["mask_BxS2_if1"]}
    proj = np.zeros((P, 512), np.float32)
    for h in range(16):
        proj[8 * h:8 * h + 8, 32 * h:32 * h + 32] = i["L0_attn_proj"][h]
    lb = np.zeros((P, 4096), np.float32)
    for e in range(8):
        at = 32 * (e % 4)
        lb[at:at + 16, 512 * e:512 * e + 512] = i["L2_ffn_lora_B"][e].T
        lb[at + 16, 512 * e:512 * e + 512] = i["L2_ffn_bi"]
    kv = i["L0_ffn_Wkv"]
    experts = lambda a: a.transpose(1, 0, 2).reshape(P, -1)
    second = lambda a: np.concatenate([chunked(np, m) for m in a], 1)
    pos = np.arange(SEQ, dtype=np.float32)
    inv2 = (10000.0 ** (np.arange(0, 64, 2, dtype=np.float32) / np.float32(64))).astype(np.float32)
    rad = pos[None, :] / inv2[:, None]
    sc = np.stack([np.sin(rad), np.cos(rad)], 1).reshape(64, SEQ)
    w = {
        0: [i["L0_attn_w_qkv"].T, proj, i["L0_attn_w_out"].T],
        1: [i["L0_attn_w1"].T, chunked(np, i["L0_attn_w2"].T)],
        2: [pad_heads(np, i["L0_xattn_Wq"], 8, 32), pad_heads(np, i["L0_xattn_Wk"], 8, 32), i["L0_xattn_Wv"],
            chunked(np, pad_heads(np, i["L0_xattn_Wo"].T, 8, 32).T)],
        3: [i["L0_ffn_Wq"], kv[:, :2560], kv[:, 2560:], np.concatenate([i["L0_ffn_Ws"], i["L0_ffn_Wd"]], 1),
            chunked(np, i["L0_ffn_Wo"].reshape(64, 5, P).transpose(1, 0, 2).reshape(320, P))],
        4: [i["L1_attn_W_in"].T, chunked(np, np.concatenate([i["L1_attn_A"], i["L1_attn_B_ssm"]], 1)),
            i["L1_attn_C_ssm"].T, chunked(np, i["L1_attn_W_out"].T)],
        9: [i["L1_ffn_Wr"], experts(i["L1_ffn_We1"]), second(i["L1_ffn_We2"])],
        10: [i["L2_attn_Wq"].T, i["L2_attn_Wk"].T, i["L2_attn_Wv"].T, np.repeat(sc, 2, 0)],
        11: [i["L2_xattn_Wq"].T, i["L2_xattn_Wk"].T, i["L2_xattn_Wv"].T],
        12: [i["L2_ffn_gate_w"].T, i["L2_ffn_wi"].T,
             pad_heads(np, i["L2_ffn_lora_A"].reshape(P, P).T, 16, 32), lb, chunked(np, i["L2_ffn_wo"].T)],
        13: [pad_heads(np, i["L3_attn_WQ"].T, 8, 32), pad_heads(np, i["L3_attn_WK"].T, 8, 32), i["L3_attn_WV"].T,
             chunked(np, pad_heads(np, i["L3_attn_WO"], 8, 32).T)],
        14: [i["L3_xattn_Wq"], i["L3_xattn_Wk"], i["L3_xattn_Wv"], chunked(np, i["L3_xattn_Wo"])],
        15: [i["L3_ffn_gate_w"].T, experts(i["L3_ffn_w1"].transpose(0, 2, 1)),
             experts(i["L3_ffn_w3"].transpose(0, 2, 1)), second(i["L3_ffn_w2"].transpose(0, 2, 1))],
    }
    for k, parts in w.items():
        out[f"w{k}"] = pack(np, parts, [n for _, n in WEIGHTS[k]])
    for k, c in ((5, "s"), (6, "c")):
        spread = lambda v: np.broadcast_to(v, (P, P))
        layers = [pack(np, [i[f"L1_xattn_{c}Wq"][l], i[f"L1_xattn_{c}Wk"][l], i[f"L1_xattn_{c}Wv"][l],
                            chunked(np, i[f"L1_xattn_{c}Wo"][l]),
                            spread(i[f"L1_xattn_{c}g"][l]), spread(i[f"L1_xattn_{c}bo"][l])], [n for _, n in WEIGHTS[k]]) for l in range(LAYERS)]
        out[f"w{k}"] = np.stack(layers)
    out["w7"] = np.stack([pack(np, [i["L1_xattn_fW1"][l], chunked(np, i["L1_xattn_fW2"][l]),
                                    spread(i["L1_xattn_fg"][l]), spread(i["L1_xattn_fb2"][l])], [512, 512, 128, 128])
                          for l in range(LAYERS)])
    out["w5next"] = out["w5"][[1, 2, 3, 0]]
    out["w5"] = out["w5"][0]
    one = np.zeros((P, 1), np.float32)
    one[16::32] = 1
    block4 = np.zeros((P, 4), np.float32)
    for h in range(4):
        block4[32 * h:32 * h + 32, h] = 1
    padcols = lambda v: columns(np, pad_heads(np, v, 8, 32))
    c = {"L0a_b1": columns(np, i["L0_attn_b1"]), "L0x_bq": padcols(i["L0_xattn_bq"]),
         "L0x_bk": padcols(i["L0_xattn_bk"]), "L1a_bin": columns(np, i["L1_attn_b_in"]),
         "L1x_fb1": columns(np, i["L1_xattn_fb1"].reshape(-1)), "L1f_be1": columns(np, i["L1_ffn_be1"].reshape(-1)),
         "L2a_bq": columns(np, i["L2_attn_bq"]), "L2a_bk": columns(np, i["L2_attn_bk"]),
         "L2x_bq": columns(np, i["L2_xattn_bq"]), "L2x_bk": columns(np, i["L2_xattn_bk"]), "L2f_one": one,
         "L3a_bq": padcols(i["L3_attn_bQ"]), "L3a_bk": padcols(i["L3_attn_bK"]),
         "L3x_bq": columns(np, i["L3_xattn_bq"]), "L3x_bk": columns(np, i["L3_xattn_bk"]), "block4": block4}
    out["cols"] = pack(np, [c[n] for n, _ in COLS], [m for _, m in COLS])
    tri = lambda n: np.tril(np.ones((n, n), np.float32), -1)
    rw = {"L0a_bout": i["L0_attn_b_out"], "L0a_gamma": i["L0_attn_gamma"], "L0a_beta": i["L0_attn_beta"],
          "L0a_b2": i["L0_attn_b2"], "L0x_bv": i["L0_xattn_bv"], "L0x_bo": i["L0_xattn_bo"],
          "L1a_nw": i["L1_attn_norm_w"], "L1a_nb": i["L1_attn_norm_b"], "L1a_bout": i["L1_attn_b_out"],
          "L1x_gout": i["L1_xattn_g_out"], "L1f_be2": i["L1_ffn_be2"], "L1f_br": i["L1_ffn_br"],
          "L2a_bv": i["L2_attn_bv"], "L2x_bv": i["L2_xattn_bv"], "L2f_bo": i["L2_ffn_bo"],
          "L2f_gb": i["L2_ffn_gate_b"], "L3a_bv": i["L3_attn_bV"], "L3a_bo": i["L3_attn_bO"],
          "L3x_bo": i["L3_xattn_bo"], "tri5": tri(5), "tri4": tri(4), "tri8": tri(8)}
    out["L3x_bv"] = i["L3_xattn_bv"].reshape(1, -1)
    out["rows"] = np.concatenate([rw[n].reshape(1, -1) for n, _ in ROWS], 1)
    ident = np.eye(P, dtype=np.float32)
    rot = np.zeros((P, P), np.float32)
    for h in (0, 64):
        for m in range(16):
            rot[h + m + 16, h + m] = -1
            rot[h + m, h + m + 16] = 1
    pair = np.eye(P, dtype=np.float32)
    for m in range(0, P, 2):
        pair[m + 1, m] = -1
        pair[m, m + 1] = 1
    inv = (1.0 / 10000.0 ** (np.arange(0, 32, 2, dtype=np.float32) / np.float32(32))).astype(np.float32)
    fr = np.concatenate([inv, inv])[:, None] * pos[None, :]
    cos, sin = np.ones((P, SEQ), np.float32), np.zeros((P, SEQ), np.float32)
    for h in (0, 64):
        cos[h:h + 32], sin[h:h + 32] = np.cos(fr), np.sin(fr)
    out["consts"] = pack(np, [ident, rot, pair, cos, sin], [m for _, m in CONSTS])
    table = i["L3_attn_rel_pos_table"]
    at = np.arange(P)[:, None] - np.arange(SEQ)[None, :] + (SEQ - P) + len(table) // 2
    out["reltab"] = table[np.clip(at, 0, len(table) - 1)].transpose(0, 2, 1).reshape(P, -1)
    return {k: np.ascontiguousarray(v) for k, v in out.items()}


def kernel(**inputs):
    import numpy as np
    import concourse.bacc as bacc
    from concourse.bass_utils import run_bass_kernel_spmd

    nc = bacc.Bacc("TRN2", target_bir_lowering=False, num_devices=1)
    arrays, io = {}, {}
    for name, a in layout(np, {k: np.asarray(v) for k, v in inputs.items()}).items():
        arrays[f"in_{name}_dram"] = a
        io[name] = nc.dram_tensor(f"in_{name}_dram", a.shape, mybir.dt.from_np(a.dtype), kind="ExternalInput").ap()
    io["out"] = nc.dram_tensor("out_0_dram", (NBATCH, SEQ, P), F32, kind="ExternalOutput").ap()
    build(nc, io)
    r = run_bass_kernel_spmd(nc, [arrays], core_ids=[0])
    return r.results[0]["out_0_dram"]
```

```python
from contextlib import ExitStack

import concourse.bass as bass
from concourse import mybir

F32 = mybir.dt.float32
I32 = mybir.dt.int32
U8 = mybir.dt.uint8
ALU = mybir.AluOpType
ACT = mybir.ActivationFunctionType
AX = mybir.AxisListType

P = 128
NBATCH, SEQ, CTX = 4, 512, 154
NT = SEQ // P
CK = CTX // 2
LAYERS = 4
HUGE = 3.0e38
MASKED = 1.0e30
EPS = 1e-5
RSQRT8 = 8.0 ** -0.5

WEIGHTS = {
    0: [("wqkv", 384), ("proj", 512), ("wout", 128)],
    1: [("w1", 512), ("w2", 512)],
    2: [("wq", 512), ("wk", 512), ("wv", 128), ("wo", 512)],
    3: [("wq", 2560), ("wk", 2560), ("wv", 2560), ("wsd", 80), ("wo", 640)],
    4: [("win", 256), ("ab", 64), ("c", 256), ("wout", 256)],
    5: [("wq", 512), ("wk", 512), ("swapq", 512), ("swapk", 512), ("wv", 512), ("wo", 512), ("gain", 128), ("bias", 128)],
    6: [("wq", 512), ("wk", 512), ("swapq", 512), ("swapk", 512), ("wv", 512), ("wo", 512), ("gain", 128), ("bias", 128)],
    7: [("w1", 512), ("w2", 512), ("gain", 128), ("bias", 128)],
    9: [("wr", 4), ("w1", 2048), ("w2", 2048)],
    10: [("wq", 128), ("wk", 128), ("wv", 128), ("sincos", 512)],
    11: [("wq", 32), ("wk", 32), ("wv", 128)],
    12: [("gate", 8), ("wi", 512), ("loraA", 256), ("loraB", 4096), ("wo", 512)],
    13: [("wq", 512), ("wk", 512), ("wv", 128), ("wo", 512)],
    14: [("wq", 1024), ("wk", 1024), ("wv", 1024), ("wo", 1024)],
    15: [("gate", 8), ("w1", 4096), ("w3", 4096), ("w2", 4096)],
}
COLS = [("L0a_b1", 4), ("L0x_bq", 4), ("L0x_bk", 4), ("L1a_bin", 2), ("L1x_fb1", 16), ("L1f_be1", 16),
        ("L2a_bq", 1), ("L2a_bk", 1), ("L2x_bq", 1), ("L2x_bk", 1), ("L2f_one", 1),
        ("L3a_bq", 4), ("L3a_bk", 4), ("L3x_bq", 8), ("L3x_bk", 8), ("block4", 4)]
ROWS = [("L0a_bout", 128), ("L0a_gamma", 128), ("L0a_beta", 128), ("L0a_b2", 128), ("L0x_bv", 128),
        ("L0x_bo", 128), ("L1a_nw", 128), ("L1a_nb", 128), ("L1a_bout", 128),
        ("L1x_gout", 128), ("L1f_be2", 512), ("L1f_br", 4), ("L2a_bv", 128), ("L2x_bv", 128),
        ("L2f_bo", 128), ("L2f_gb", 8), ("L3a_bv", 128), ("L3a_bo", 128), ("L3x_bo", 128),
        ("index5", 5), ("tri4", 16), ("tri8", 64)]
CONSTS = [("ident", 128), ("pair", 128), ("cos", 512), ("sin", 512)]


def spans(spec):
    at, out = 0, {}
    for name, n in spec:
        out[name] = (at, n)
        at += n
    return out, at


WIDTH = {k: spans(v)[1] for k, v in WEIGHTS.items()}
class Roles:
    def __init__(self, sem):
        self.loaded = sem("loaded")
        self.xT_ps = sem("xT_ps")
        self.xT = sem("xT")
        self.proj = sem("proj")
        self.evac_act = sem("evac_act")
        self.evac_dve = sem("evac_dve")
        self.rotated = sem("rotated")
        self.recip = sem("recip")
        self.probs = sem("probs")
        self.headkeys = sem("headkeys")
        self.av_sb = sem("av_sb")
        self.ones = sem("ones")
        self.scores = sem("scores")
        self.negmax = sem("negmax")
        self.exped = sem("exped")
        self.probsT = sem("probsT")
        self.probsT_sb = sem("probsT_sb")
        self.unit_av = sem("unit_av")
        self.av = sem("av")
        self.normed = sem("normed")
        self.mixed = sem("mixed")
        self.attnT = sem("attnT")
        self.attnT_sb = sem("attnT_sb")
        self.outproj = sem("outproj")
        self.out = sem("out")
        self.var = sem("var")
        self.rstd = sem("rstd")
        self.hid = sem("hid")
        self.hid_sb = sem("hid_sb")
        self.hid_dve = sem("hid_dve")
        self.part = sem("part")
        self.part_used = sem("part_used")
        self.gate = sem("gate")
        self.ready = sem("ready")
        self.squares = sem("squares")
        self.early = sem("early")
        self.dve_step = sem("dve_step")
        self.act_step = sem("act_step")
        self.sum_step = sem("sum_step")
        self.pool_step = sem("pool_step")


class Chain:

    def __init__(self, eng, sem):
        self.eng, self.sem, self.n = eng, sem, 0

    def inc(self, ins):
        ins.then_inc(self.sem, 1)
        self.n += 1
        return ins

    def join(self):
        if self.n:
            self.eng.wait_ge(self.sem, self.n)

    def link(self, ins):
        self.inc(ins)
        self.join()


class Table:

    def __init__(self, rows, before=None):
        self.rows, self.before = rows, before
        self.j0 = before.j1 if before else 0
        a, d = (before.a, before.d) if before else (0, 0)
        self.count = list(before.count) if before else []
        for r in rows:
            if r[3] == "A":
                a += 1
            else:
                d += 1
            self.count.append((r[3], a if r[3] == "A" else d))
        self.a, self.d, self.j1 = a, d, self.j0 + len(rows)


def build(nc, io):
    ctx = ExitStack()
    with ctx:
        def sb(name, shape, dt=F32):
            return ctx.enter_context(nc.sbuf_tensor(name, shape, dt))

        cols_at, ncols = spans(COLS)
        rows_at, nrows = spans(ROWS)
        consts_at, nconsts = spans(CONSTS)
        arena_w = [max(w for k, w in WIDTH.items() if k % 3 == a) for a in range(3)]
        arenas = [sb(f"weights{a}", [P, arena_w[a]]) for a in range(3)]
        cols = sb("cols", [P, ncols])
        scaled = sb("scaled", [P, 16])
        rows = sb("rows", [P, nrows])
        consts = sb("consts", [P, nconsts])
        relbias = sb("relbias", [P, 16, SEQ])
        X = sb("X", [P, NT, P])
        XN = sb("XN", [P, NT, P])
        XR = sb("XR", [P, NT, P])
        Z = sb("Z", [P, NT, P])
        XT = sb("XT", [P, SEQ])
        CT = sb("CT", [P, CTX])
        QT = sb("QT", [P, 8, SEQ])
        KT = sb("KT", [P, 4, SEQ])
        V = sb("V", [P, 2080])
        wide = sb("wide", [P, 4096])
        KZ = sb("KZ", [P, 4, SEQ])
        EX = sb("EX", [P, 4, SEQ])
        NB = sb("NB", [P, 2, SEQ])
        maskb = sb("maskb", [P, SEQ])
        mask_u8 = sb("mask_u8", [P, SEQ], U8)
        padm = sb("padm", [P, CTX], I32)
        padb = sb("padb", [P, 3, CTX])
        neg, sums, recips = sb("neg", [P, 8]), sb("sums", [P, 8]), sb("recips", [P, 8])
        small = sb("small", [P, 880])
        ps = {n: ctx.enter_context(nc.psum_tensor("ps_" + n, [P, SEQ], F32))
              for n in ("S0", "S1", "P0", "P1", "O0", "O1", "T", "OUT")}
        S = [ps["S0"], ps["S1"]]
        PP = [ps["P0"], ps["P1"]]
        O = [ps["O0"], ps["O1"]]
        TB, OUT = ps["T"], ps["OUT"]
        RING = [ps["P0"], ps["P1"], ps["O0"], ps["O1"]]

        sets = []
        for n in range(3):
            nums = []

            def sem(name):
                s = ctx.enter_context(nc.semaphore(f"{name}_{n}"))
                nums.append(s.num)
                return s

            r = Roles(sem)
            r.nums = range(min(nums), max(nums) + 1)
            assert len(r.nums) == len(nums)
            sets.append(r)
        s_boot = ctx.enter_context(nc.semaphore("boot"))
        s_boot3 = ctx.enter_context(nc.semaphore("boot_gpsimd"))
        s_boot2 = ctx.enter_context(nc.semaphore("boot_steps"))

        def C(name, c=0, n=1, parts=P):
            a = cols_at[name][0] + c
            return cols[0:parts, a:a + n]

        def R_(name, parts=P):
            a, n = rows_at[name]
            return rows[0:parts, a:a + n]

        def K(name):
            a, n = consts_at[name]
            return consts[:, a:a + n]

        ident = K("ident")

        def W(step, name):
            at, n = spans(WEIGHTS[step])[0][name]
            return arenas[step % 3][:, at:at + n]

        def tiles(ap, n=NT):
            return ap.rearrange("p (t d) -> p t d", t=n)

        flatX, flatZ, flatXN, flatXR = (t[:, :, :].rearrange("p t d -> p (t d)") for t in (X, Z, XN, XR))

        def row4(ap):
            return ap.unsqueeze(1).broadcast_to([P, NT, P])


        def load_weights(sp, r, step):
            sp.dma_start(arenas[step % 3][:, 0:WIDTH[step]], io[f"w{step}"][:, :]).then_inc(r.loaded, 16)

        def clear_previous(eng, step):
            eng.sem_clear(sets[(step - 1) % 3].nums)

        def pe_xT(pe, r, src, n=1):
            for t in range(NT):
                ins = pe.transpose(TB[:, t * P:(t + 1) * P], src[:, t, :], ident)
            ins.then_inc(r.xT_ps, 1)

        def act_xT(act, r, n=1):
            act.wait_ge(r.xT_ps, n)
            act.activation(XT[:, :], TB[:, :], ACT.Copy).then_inc(r.xT, 1)

        def pe_table(pe, r, tab):
            for j, row in enumerate(tab.rows):
                g = tab.j0 + j
                if g >= len(RING):
                    e, n = tab.count[g - len(RING)]
                    pe.wait_ge(r.evac_act if e == "A" else r.evac_dve, n)
                bank = RING[g % len(RING)]
                mms = row[0]
                for i, (lhsT, rhs) in enumerate(mms):
                    ins = pe.matmul(bank[0:row[1], 0:row[2]], lhsT, rhs, start=(i == 0), stop=(i == len(mms) - 1))
                ins.then_inc(r.proj, 1)

        def evacuate(eng, r, tab, who):
            for j, row in enumerate(tab.rows):
                if row[3] != who:
                    continue
                g = tab.j0 + j
                kind, dst, args = row[4], row[5], row[6]
                src = RING[g % len(RING)][0:row[1], 0:row[2]]
                if len(dst.shape) == 3:
                    src = src.rearrange("p (a b) -> p a b", a=dst.shape[1])
                eng.wait_ge(r.proj, g + 1)
                if len(row) > 7 and row[7]:
                    eng.wait_ge(*row[7])
                done = r.evac_act if who == "A" else r.evac_dve
                if kind == "act":
                    eng.activation(dst, src, args[0], bias=args[1], scale=args[2]).then_inc(done, 1)
                elif kind == "copy":
                    if who == "A":
                        eng.activation(dst, src, ACT.Copy).then_inc(done, 1)
                    else:
                        eng.tensor_copy(dst, src).then_inc(done, 1)
                elif kind == "scale":
                    eng.activation(dst, src, ACT.Copy, scale=args[0]).then_inc(done, 1)
                elif kind == "col":
                    eng.tensor_scalar(dst, src, args[0], None, ALU.add).then_inc(done, 1)
                elif kind == "times":
                    eng.scalar_tensor_tensor(dst, src, args[0], args[1], ALU.mult, ALU.mult).then_inc(done, 1)
                elif kind == "row":
                    eng.tensor_tensor(dst, src, args[0], args[1]).then_inc(done, 1)

        def dve_layer_norm(dve, r, ch, n, src, dst, gain=None, shift=None):
            st, mv, ve = small[:, 0:24], small[:, 24:32], small[:, 32:36]
            for t in range(NT):
                ch.inc(dve.bn_stats(st[:, 6 * t:6 * t + 6], src[:, t, :]))
            ch.join()
            for t in range(NT):
                ch.inc(dve.bn_aggr(mv[:, 2 * t:2 * t + 2], st[:, 6 * t:6 * t + 6]))
            ch.join()
            dve.tensor_scalar(ve, mv.rearrange("p (t k) -> p t k", k=2)[:, :, 1], EPS, None,
                              ALU.add).then_inc(r.var, 1)
            dve.wait_ge(r.rstd, n)
            for t in range(NT):
                ch.inc(dve.tensor_scalar(dst[:, t, :], src[:, t, :], mv[:, 2 * t:2 * t + 1],
                                         small[:, 36 + t:37 + t], ALU.subtract, ALU.mult))
            ch.join()
            if gain is not None:
                ch.link(dve.tensor_tensor(dst[:, :, :], dst[:, :, :], row4(gain), ALU.mult))
                ch.link(dve.tensor_tensor(dst[:, :, :], dst[:, :, :], row4(shift), ALU.add))

        def pool_power(pool, r, n, half=40):
            pool.wait_ge(r.var, n)
            pool.tensor_tensor(small[:, 36:40], small[:, 32:36], small[:, half:half + 4], ALU.pow).then_inc(r.rstd, 1)

        def dve_rms_norm(dve, r, ch, n, src, dst, gain):
            for t in range(2):
                ch.inc(dve.tensor_tensor_reduce(Z[:, t, :], src[:, t, :], src[:, t, :], 1.0, 0.0, ALU.mult, ALU.add,
                                                small[:, 48 + t:49 + t]))
            ch.join()
            dve.wait_ge(r.squares, 2)
            dve.tensor_scalar(small[:, 32:36], small[:, 48:52], 1.0 / P, None, ALU.mult).then_inc(r.var, 1)
            dve.wait_ge(r.rstd, n)
            ch.link(dve.tensor_scalar(small[:, 52:56], small[:, 36:40], 1e-8, None, ALU.max))
            ch.link(dve.reciprocal(small[:, 56:60], small[:, 52:56]))
            for t in range(NT):
                ch.inc(dve.scalar_tensor_tensor(dst[:, t, :], src[:, t, :], small[:, 56 + t:57 + t], gain,
                                                ALU.mult, ALU.mult))
            ch.join()

        def act_squares(act, r, src):
            for t in range(2, NT):
                act.activation(Z[:, t, :], src[:, t, :], ACT.Square, accum_out=small[:, 48 + t:49 + t]
                               ).then_inc(r.squares, 1)

        def dve_ranks(dve, ch, s, G, E, tri, rank, t1, t2):
            mine = s.unsqueeze(3).broadcast_to([P, G, E, E])
            other = s.unsqueeze(2).broadcast_to([P, G, E, E])
            lower = tri.rearrange("p (a b) -> p a b", a=E).unsqueeze(1).broadcast_to([P, G, E, E])
            a = t1[:, 0:G * E * E].rearrange("p (g e f) -> p g e f", g=G, e=E)
            b = t2[:, 0:G * E * E].rearrange("p (g e f) -> p g e f", g=G, e=E)
            ch.inc(dve.tensor_tensor(a, other, mine, ALU.is_gt))
            ch.link(dve.tensor_tensor(b, other, mine, ALU.is_equal))
            ch.link(dve.tensor_tensor(b, b, lower, ALU.mult))
            ch.link(dve.tensor_tensor(a, a, b, ALU.add))
            ch.link(dve.tensor_reduce(rank, a, AX.X, ALU.add))


        class Attention:
            LAG = 3

            def __init__(self, heads, dh, nkeys, added=None, causal=False, keys=None, queries=None):
                self.heads, self.dh, self.nkeys, self.added, self.causal = heads, dh, nkeys, added, causal
                self.keys = keys
                self.queries = queries
                self.ctx = nkeys == CTX
                self.kc = CK if self.ctx else P
                self.nch = nkeys // self.kc
                self.U = self.nch
                self.slot = {8: 32, 64: 64, P: P}[dh]
                self.hpc = P // self.slot
                self.chunks = heads // self.hpc
                self.units = [(h, [2 * u, 2 * u + 1] if self.ctx else [u],
                               P * (u + 1) if causal else nkeys) for h in range(heads) for u in range(self.U)]
                self.steps = len(self.units) + self.LAG + self.U + 1

            def probs(self, h):
                n = self.nch * SEQ
                return wide[:, (h % 2) * n:(h % 2 + 1) * n].rearrange("p (c q) -> p c q", c=self.nch)

            def value(self, h, c):
                w = self.heads * self.slot
                return V[:, c * w + h * self.slot:c * w + (h + 1) * self.slot]

            def out_chunk(self, c):
                return QT[:, c, :]

            def av_at(self, i):
                k = i - self.LAG - self.U
                return (k // self.U, k % self.U) if 0 <= k < self.heads * self.U else None

            def pool_clear(self, pool, r):
                if self.hpc > 1:
                    for c in range(self.hpc):
                        pool.memset(KZ[:, c, 0:self.nkeys], 0.0).then_inc(r.pool_step, 1)

            def pool(self, pool, r, waits, of=None, clear=True):
                if self.hpc == 1:
                    return
                if clear:
                    pool.wait_ge(r.pool_step, self.hpc)
                for sem, n in waits:
                    pool.wait_ge(sem, n)
                for h in of or range(self.heads):
                    j = h % self.hpc
                    if h >= self.hpc:
                        pool.wait_ge(r.scores, self.U * (h - self.hpc + 1))
                    rows_of = slice(self.slot * j, self.slot * (j + 1))
                    pool.tensor_copy(KZ[rows_of, j, 0:self.nkeys], self.keys(h // self.hpc)[rows_of, :]
                                     ).then_inc(r.headkeys, 1)

            def pe(self, pe, r, banks=(), beside=None):
                n = len(self.units)
                for i in range(self.steps):
                    if i < n:
                        h, qts, N = self.units[i]
                        c = h // self.hpc
                        if i % self.U == 0 and self.hpc > 1:
                            pe.wait_ge(r.headkeys, h + 1)
                        if i % (self.U * self.hpc) == 0 and self.queries:
                            pe.wait_ge(*self.queries(c))
                        if i >= 2:
                            pe.wait_ge(r.negmax if self.added else r.exped, i - 1)
                        k = KZ[:, h % self.hpc, 0:N] if self.hpc > 1 else self.keys(c)[:, 0:N]
                        for a, qt in enumerate(qts):
                            ins = pe.matmul(S[i % 2][:, a * N:(a + 1) * N], QT[:, c, qt * P:(qt + 1) * P], k,
                                            start=True, stop=True)
                        ins.then_inc(r.scores, 1)
                    u = i - self.LAG
                    if 0 <= u < n:
                        h, qts, N = self.units[u]
                        pe.wait_ge(r.probs, u + 1)
                        for sem, count in banks if u == 0 else ():
                            pe.wait_ge(sem, count)
                        if u >= 2:
                            pe.wait_ge(r.probsT_sb, u - 1)
                        for c in range(N // self.kc):
                            for a, qt in enumerate(qts):
                                b = c * len(qts) + a
                                ins = pe.transpose(PP[u % 2][0:self.kc, b * P:(b + 1) * P],
                                                   EX[:, u % 4, a * N + c * self.kc:a * N + (c + 1) * self.kc],
                                                   ident)
                        ins.then_inc(r.probsT, 1)
                    hc = self.av_at(i)
                    if hc:
                        h, c = hc
                        m = h // self.hpc
                        if c == 0:
                            pe.wait_ge(r.probsT_sb, self.U * (h + 1))
                            if h % self.hpc == 0 and m >= 2:
                                pe.wait_ge(r.av_sb, m - 1)
                        q0 = c * P if self.causal else 0
                        j = h % self.hpc
                        ins = pe.matmul(O[m % 2][self.slot * j:self.slot * (j + 1), q0:SEQ], self.value(h, c),
                                        self.probs(h)[:, c, q0:SEQ], start=(c == 0), stop=(c == self.nch - 1),
                                        skip_group_check=self.causal)
                        if c == self.nch - 1:
                            ins.then_inc(r.av, 1)
                    if beside:
                        beside(i)

            def act(self, act, r):
                n = len(self.units)
                for i in range(self.steps):
                    if i < n:
                        h, qts, N = self.units[i]
                        act.wait_ge(r.negmax, i + 1)
                        if i >= 4:
                            act.wait_ge(r.probsT, i - 3)
                        for a in range(len(qts)):
                            src = NB[:, i % 2, a * N:(a + 1) * N] if self.added else S[i % 2][:, a * N:(a + 1) * N]
                            at = 2 * (i % 4) + a
                            ins = act.activation(EX[:, i % 4, a * N:(a + 1) * N], src, ACT.Exp,
                                                 bias=neg[:, at:at + 1], scale=-1.0 if self.added else 1.0,
                                                 accum_out=sums[:, at:at + 1])
                        ins.then_inc(r.exped, 1)
                    u = i - 1
                    if 0 <= u < n and not self.ctx:
                        h, qts, N = self.units[u]
                        act.wait_ge(r.recip, u + 1)
                        at = 2 * (u % 4)
                        act.activation(EX[:, u % 4, 0:N], EX[:, u % 4, 0:N], ACT.Copy, scale=recips[:, at:at + 1]
                                       ).then_inc(r.probs, 1)
                    hc = self.av_at(i)
                    if hc and hc[1] == self.nch - 1 and hc[0] % self.hpc == self.hpc - 1:
                        h = hc[0]
                        act.wait_ge(r.av, h + 1)
                        act.activation(self.out_chunk(h // self.hpc), O[(h // self.hpc) % 2][:, :], ACT.Copy
                                       ).then_inc(r.av_sb, 1)

            def dve(self, dve, r, free=None, beside=None):
                n = len(self.units)
                for i in range(self.steps):
                    if i < n:
                        h, qts, N = self.units[i]
                        dve.wait_ge(r.scores, i + 1)
                        if self.added and i >= 2:
                            dve.wait_ge(r.exped, i - 1)
                        elif i >= 4:
                            dve.wait_ge(r.exped, i - 3)
                        at = 2 * (i % 4)
                        if self.added:
                            for a, qt in enumerate(qts):
                                ins = dve.tensor_tensor_reduce(
                                    NB[:, i % 2, a * N:(a + 1) * N], S[i % 2][:, a * N:(a + 1) * N],
                                    self.added(h, qt), -1.0, HUGE, ALU.add, ALU.min, neg[:, at + a:at + a + 1])
                        else:
                            w = len(qts)
                            ins = dve.tensor_reduce(neg[:, at:at + w],
                                                    S[i % 2][:, 0:w * N].rearrange("p (a k) -> p a k", k=N),
                                                    AX.X, ALU.max, negate=True)
                        ins.then_inc(r.negmax, 1)
                    u = i - 1
                    if 0 <= u < n:
                        h, qts, N = self.units[u]
                        at, w = 2 * (u % 4), len(qts)
                        dve.wait_ge(r.exped, u + 1)
                        if u >= 4 and not self.ctx:
                            dve.wait_ge(r.probs, u - 3)
                        dve.reciprocal(recips[:, at:at + w], sums[:, at:at + w]).then_inc(r.recip, 1)
                        if self.ctx:
                            e = EX[:, u % 4, 0:w * N].rearrange("p (a k) -> p a k", k=N)
                            dve.wait_ge(r.recip, u + 1)
                            dve.tensor_tensor(e, e, recips[:, at:at + w].unsqueeze(2).broadcast_to([P, w, N]),
                                              ALU.mult).then_inc(r.probs, 1)
                    u = i - self.LAG
                    if 0 <= u < n:
                        h, qts, N = self.units[u]
                        dve.wait_ge(r.probsT, u + 1)
                        if u % self.U == 0 and h >= 2:
                            dve.wait_ge(r.av, h - 1)
                        if free and u % self.U == 0 and h in free:
                            dve.wait_ge(*free[h])
                        nc_ = N // self.kc
                        w = len(qts) * P
                        dve.tensor_copy(self.probs(h)[0:self.kc, 0:nc_, qts[0] * P:qts[0] * P + w],
                                        PP[u % 2][0:self.kc, 0:nc_ * w].rearrange("p (c q) -> p c q", c=nc_)
                                        ).then_inc(r.probsT_sb, 1)
                    if beside:
                        beside(i)

            def project(self, pe, r, wo):
                pe.wait_ge(r.av_sb, self.chunks)
                for t in range(NT):
                    for c in range(self.chunks):
                        ins = pe.matmul(OUT[:, t * P:(t + 1) * P], self.out_chunk(c)[:, t * P:(t + 1) * P],
                                        wo[:, c * P:(c + 1) * P], start=(c == 0), stop=(c == self.chunks - 1))
                ins.then_inc(r.out, 1)

        def pool_clear_context(pool, r, n):
            pool.memset(V[:, 0:n], 0.0).then_inc(r.ones, 1)
            pool.memset(wide[:, 0:4 * SEQ], 0.0).then_inc(r.ones, 1)

        def v_rows(kc, heads, slot, dh, c):
            w = heads * slot
            return V[0:kc, c * w:(c + 1) * w].rearrange("p (h d) -> p h d", h=heads)[:, :, 0:dh]

        with nc.Block() as block:
            @block.sync
            def _(sp):
                sp.dma_start(cols[:, :], io["cols"][:, :]).then_inc(s_boot, 16)
                sp.dma_start(rows[:, :], bass.AP(io["rows"].tensor, 0, [[0, P], [1, nrows]])).then_inc(s_boot, 16)
                sp.dma_start(consts[:, :], io["consts"][:, :]).then_inc(s_boot, 16)
                sp.dma_start(relbias[:, :, :].rearrange("p h k -> p (h k)"), io["reltab"][:, :]).then_inc(s_boot, 16)
                sp.dma_start(arenas[0][:, 0:WIDTH[0]], io["w0"][:, :]).then_inc(s_boot, 16)
                sp.wait_ge(s_boot, 80)

            @block.gpsimd
            def _(pool):
                pool.wait_ge(s_boot, 80)
                pool.affine_select(relbias[:, :, :], relbias[:, :, :], [[0, 16], [-1, SEQ]], ALU.is_ge, -HUGE,
                                   base=SEQ - P, channel_multiplier=1).then_inc(s_boot3, 1)
                pool.memset(small[:, 40:44], -0.5).then_inc(s_boot3, 1)
                pool.memset(small[:, 44:48], 0.5).then_inc(s_boot3, 1)
                pool.wait_ge(s_boot3, 3)

            @block.vector
            def _(dve):
                dve.wait_ge(s_boot, 80)
                a = cols_at["L0x_bq"][0]
                dve.tensor_scalar(scaled[:, 0:4], cols[:, a:a + 4], RSQRT8, None, ALU.mult).then_inc(s_boot2, 1)
                a = cols_at["L3a_bq"][0]
                dve.tensor_scalar(scaled[:, 4:8], cols[:, a:a + 4], RSQRT8, None, ALU.mult).then_inc(s_boot2, 1)
                a = cols_at["L3x_bq"][0]
                dve.tensor_scalar(scaled[:, 8:16], cols[:, a:a + 8], 0.125, None, ALU.mult).then_inc(s_boot2, 1)
                dve.wait_ge(s_boot2, 3)


        def step_load(b):
            step = 17
            r = sets[step % 3]
            with nc.Block() as block:
                @block.sync
                def _(sp):
                    clear_previous(sp, step)
                    sp.dma_start(X[:, :, :], io["x"][bass.ds(b, 1)].rearrange("o (t p) d -> p (o t) d", p=P)
                                 ).then_inc(r.loaded, 16)
                    sp.dma_start(CT[:, :], io["ctxT"][bass.ds(b, 1)].rearrange("o p k -> p (o k)")
                                 ).then_inc(r.loaded, 16)
                    sp.dma_start(mask_u8[:, :], io["mask1"][bass.ds(b, 1), :].broadcast_to([P, SEQ])
                                 ).then_inc(r.loaded, 16)
                    sp.dma_start(padm[:, :], io["mask2"][bass.ds(b, 1), :].broadcast_to([P, CTX])
                                 ).then_inc(r.loaded, 16)
                    sp.wait_ge(r.loaded, 64)

                @block.vector
                def _(dve):
                    ch = Chain(dve, r.dve_step)
                    dve.wait_ge(r.loaded, 64)
                    ch.inc(dve.tensor_scalar(maskb[:, :], mask_u8[:, :], MASKED, -MASKED, ALU.mult, ALU.add))
                    for m in range(3):
                        ins = dve.tensor_scalar(padb[:, m, :], padm[:, :], 0.0, -HUGE, ALU.is_equal, ALU.mult)
                        ins.then_inc(r.ready, 1)
                    dve.wait_ge(r.early, 2)

                @block.gpsimd
                def _(pool):
                    pool.wait_ge(r.ready, 3)
                    for m in range(2):
                        pool.affine_select(padb[:, m, :], padb[:, m, :], [[-1, CTX]], ALU.is_ge, -HUGE,
                                           base=P * m, channel_multiplier=1).then_inc(r.early, 1)
                    pool.wait_ge(r.early, 2)

        def tail(dve, r, ch, out_wait, base, n=1):
            dve.wait_ge(*out_wait)
            ch.link(dve.tensor_tensor(flatZ, OUT[:, :], base, ALU.add))
            dve_layer_norm(dve, r, ch, n, Z, X)

        def step_L0_linear_attention():
            step = 0
            r = sets[step % 3]
            w = lambda n: W(step, n)
            qT, kT = KT[:, 0, :], KT[:, 1, :]
            qf = QT[:, 0:4, :]
            kf = QT[:, 4:8, :]
            pos = wide[:, 0:4096].rearrange("p (c t) -> p c t", c=8)
            vv = V[:, 0:NT * 144].rearrange("p (t h d) -> p t h d", t=NT, h=16)
            kvb = small[:, 128:272].rearrange("p (c h d) -> p c h d", c=4, h=4)
            rowsA = [([(w("wqkv")[:, 0:128], XT[:, :])], P, SEQ, "A", "copy", qT, None),
                     ([(w("wqkv")[:, 128:256], XT[:, :])], P, SEQ, "D", "copy", kT, None)]
            rowsA += [([(XT[:, t * P:(t + 1) * P], w("wqkv")[:, 256:384])], P, P, "AD"[t % 2], "copy",
                       vv[:, t, :, 0:8], None) for t in range(NT)]
            tab = Table(rowsA)
            with nc.Block() as block:
                @block.sync
                def _(sp):
                    clear_previous(sp, step)
                    load_weights(sp, r, 1)
                    sp.wait_ge(r.loaded, 16)

                @block.gpsimd
                def _(pool):
                    pool.memset(V[:, 0:NT * 144].rearrange("p (t d) -> p t d", d=9)[:, :, 8:9], 1.0).then_inc(r.ones, 1)
                    for c in range(8):
                        pool.wait_ge(r.hid_sb, c + 1)
                        pool.wait_ge(r.hid_dve, 2 * c + 2)
                        f = qf[:, c, :] if c < 4 else kf[:, c - 4, :]
                        pool.tensor_tensor(f, f, pos[:, c, :], ALU.add).then_inc(r.ready, 1)
                    pool_power(pool, r, 1)

                @block.tensor
                def _(pe):
                    pe_xT(pe, r, X)
                    pe.wait_ge(r.xT, 1)
                    pe_table(pe, r, tab)
                    pe.wait_ge(r.evac_act, tab.a)
                    pe.wait_ge(r.evac_dve, tab.d)
                    for c in range(8):
                        if c >= 4:
                            pe.wait_ge(r.hid_dve, 2 * (c - 4) + 2)
                        if c < 4:
                            ins = pe.matmul(RING[c % 4][:, :], w("proj")[:, c * P:(c + 1) * P], qT, start=True, stop=True)
                        else:
                            t = c - 4
                            ins = pe.matmul(RING[c % 4][:, :], kT[:, t * P:(t + 1) * P], w("proj"), start=True, stop=True)
                        ins.then_inc(r.hid, 1)
                    pe.wait_ge(r.ready, 8)
                    pe.wait_ge(r.ones, 1)
                    for c in range(4):
                        for t in range(NT):
                            ins = pe.matmul(TB[:, c * 36:(c + 1) * 36], kf[:, t, c * P:(c + 1) * P],
                                            vv[:, t, 4 * c:4 * c + 4, :], start=(t == 0), stop=(t == NT - 1))
                    ins.then_inc(r.part, 1)
                    pe.wait_ge(r.part_used, 1)
                    for t in range(NT):
                        for c in range(4):
                            ins = pe.matmul(S[t % 2][:, (t // 2) * 144 + c * 36:(t // 2) * 144 + (c + 1) * 36],
                                            qf[:, c, t * P:(t + 1) * P], kvb[:, c, :, :], start=True, stop=True)
                    ins.then_inc(r.av, 1)
                    pe.wait_ge(r.normed, 4)
                    for t in range(NT):
                        ins = pe.transpose(TB[:, t * P:(t + 1) * P], XN[:, t, :], ident)
                    ins.then_inc(r.attnT, 1)
                    pe.wait_ge(r.attnT_sb, 1)
                    for t in range(NT):
                        ins = pe.matmul(OUT[:, t * P:(t + 1) * P], XT[:, t * P:(t + 1) * P], w("wout"),
                                        start=True, stop=True)
                    ins.then_inc(r.out, 1)

                @block.scalar
                def _(act):
                    act_xT(act, r)
                    evacuate(act, r, tab, "A")
                    for c in range(8):
                        act.wait_ge(r.hid_dve, 2 * c + 2)
                        f = qf[:, c, :] if c < 4 else kf[:, c - 4, :]
                        act.activation(f, f, ACT.Exp).then_inc(r.hid_sb, 1)
                    act.wait_ge(r.attnT, 1)
                    act.activation(XT[:, :], TB[:, :], ACT.Copy).then_inc(r.attnT_sb, 1)

                @block.vector
                def _(dve):
                    ch = Chain(dve, r.dve_step)
                    evacuate(dve, r, tab, "D")
                    for c in range(8):
                        dve.wait_ge(r.hid, c + 1)
                        f = qf[:, c, :] if c < 4 else kf[:, c - 4, :]
                        dve.tensor_scalar(f, RING[c % 4][:, :], 0.0, None, ALU.min).then_inc(r.hid_dve, 1)
                        dve.tensor_scalar(pos[:, c, :], RING[c % 4][:, :], 0.0, None, ALU.max).then_inc(r.hid_dve, 1)
                    dve.wait_ge(r.part, 1)
                    dve.tensor_tensor(kvb, TB[:, 0:144].rearrange("p (c h d) -> p c h d", c=4, h=4),
                                      C("block4", 0, 4).unsqueeze(1).unsqueeze(3).broadcast_to([P, 4, 4, 9]),
                                      ALU.mult).then_inc(r.part_used, 1)
                    dve.wait_ge(r.av, 1)
                    for t in range(NT):
                        o = S[t % 2][:, (t // 2) * 144:(t // 2) * 144 + 144].rearrange("p (h d) -> p h d", h=16)
                        den = small[:, 272 + 16 * t:288 + 16 * t]
                        ch.link(dve.tensor_scalar(den, o[:, :, 8], 1e-8, None, ALU.add))
                        ch.link(dve.reciprocal(den, den))
                        dve.tensor_tensor(XN[:, t, :].rearrange("p (h d) -> p h d", h=16), o[:, :, 0:8],
                                          den.unsqueeze(2).broadcast_to([P, 16, 8]), ALU.mult).then_inc(r.normed, 1)
                    ch.link(dve.tensor_tensor(Z[:, :, :], X[:, :, :], row4(R_("L0a_bout")), ALU.add))
                    dve.wait_ge(r.out, 1)
                    ch.link(dve.tensor_tensor(flatZ, OUT[:, :], flatZ, ALU.add))
                    dve_layer_norm(dve, r, ch, 1, Z, XR, R_("L0a_gamma"), R_("L0a_beta"))

        def mlp_pe(pe, r, w, act_done):
            for c in range(4):
                ins = pe.matmul(RING[c][:, :], w("w1")[:, c * P:(c + 1) * P], XT[:, :], start=True, stop=True)
                ins.then_inc(r.hid, 1)
            pe.wait_ge(act_done, 4)
            for t in range(NT):
                for c in range(4):
                    ins = pe.matmul(OUT[:, t * P:(t + 1) * P], QT[:, c, t * P:(t + 1) * P],
                                    w("w2")[:, c * P:(c + 1) * P], start=(c == 0), stop=(c == 3))
            ins.then_inc(r.out, 1)

        def step_L0_mlp():
            step = 1
            r = sets[step % 3]
            w = lambda n: W(step, n)
            with nc.Block() as block:
                @block.sync
                def _(sp):
                    clear_previous(sp, step)
                    load_weights(sp, r, 2)
                    sp.wait_ge(r.loaded, 16)

                @block.gpsimd
                def _(pool):
                    pool_power(pool, r, 1)
                    pool_power(pool, r, 2)

                @block.tensor
                def _(pe):
                    pe_xT(pe, r, XR)
                    pe.wait_ge(r.xT, 1)
                    mlp_pe(pe, r, w, r.hid_sb)

                @block.scalar
                def _(act):
                    act_xT(act, r)
                    for c in range(4):
                        act.wait_ge(r.hid, c + 1)
                        act.activation(QT[:, c, :], RING[c][:, :], ACT.Gelu, bias=C("L0a_b1", c)).then_inc(r.hid_sb, 1)

                @block.vector
                def _(dve):
                    ch = Chain(dve, r.dve_step)
                    ch.link(dve.tensor_tensor(Z[:, :, :], XR[:, :, :], row4(R_("L0a_b2")), ALU.add))
                    dve.wait_ge(r.out, 1)
                    ch.link(dve.tensor_tensor(flatZ, OUT[:, :], flatZ, ALU.add))
                    dve_layer_norm(dve, r, ch, 1, Z, XN, R_("L0a_gamma"), R_("L0a_beta"))
                    ch.link(dve.tensor_tensor(flatZ, flatX, flatXN, ALU.add))
                    dve_layer_norm(dve, r, ch, 2, Z, X)

        def step_L0_cross():
            step = 2
            r = sets[step % 3]
            w = lambda n: W(step, n)
            att = Attention(16, 8, CTX, keys=lambda c: KT[:, c, 0:CTX])
            rowsA = [([(w("wq")[:, c * P:(c + 1) * P], XT[:, :])], P, SEQ, "A", "act", QT[:, c, :],
                      (ACT.Relu, scaled[:, c:c + 1], RSQRT8)) for c in range(4)]
            rowsA += [([(w("wk")[:, c * P:(c + 1) * P], CT[:, :])], P, CTX, "A", "act", KT[:, c, 0:CTX],
                       (ACT.Relu, C("L0x_bk", c), 1.0)) for c in range(4)]
            vrow = R_("L0x_bv", CK).rearrange("p (h d) -> p h d", h=16)
            rowsA += [([(CT[:, c * CK:(c + 1) * CK], w("wv"))], CK, P, "D", "row", v_rows(CK, 16, 32, 8, c),
                       (vrow, ALU.add)) for c in range(2)]
            tab = Table(rowsA)
            with nc.Block() as block:
                @block.sync
                def _(sp):
                    clear_previous(sp, step)
                    load_weights(sp, r, 3)
                    sp.wait_ge(r.loaded, 16)

                @block.gpsimd
                def _(pool):
                    pool_clear_context(pool, r, 1024)
                    att.pool_clear(pool, r)
                    att.pool(pool, r, [(r.evac_act, tab.a)])
                    pool_power(pool, r, 1)

                @block.tensor
                def _(pe):
                    pe_xT(pe, r, X)
                    pe.wait_ge(r.xT, 1)
                    pe_table(pe, r, tab)
                    pe.wait_ge(r.evac_act, tab.a)
                    pe.wait_ge(r.ready, 1)
                    att.pe(pe, r)
                    att.project(pe, r, w("wo"))

                @block.scalar
                def _(act):
                    act_xT(act, r)
                    evacuate(act, r, tab, "A")
                    att.act(act, r)

                @block.vector
                def _(dve):
                    ch = Chain(dve, r.dve_step)
                    dve.wait_ge(r.ones, 2)
                    evacuate(dve, r, tab, "D")
                    dve.wait_ge(r.evac_dve, tab.d)
                    dve.tensor_scalar(V[0:CK, 0:1024], V[0:CK, 0:1024], 0.0, None, ALU.max).then_inc(r.ready, 1)
                    att.dve(dve, r)
                    dve.wait_ge(r.out, 1)
                    ch.link(dve.tensor_tensor(Z[:, :, :], tiles(OUT[:, :]), row4(R_("L0x_bo")), ALU.add))
                    ch.link(dve.scalar_tensor_tensor(flatZ, flatZ, 0.0, flatX, ALU.max, ALU.add))
                    dve_layer_norm(dve, r, ch, 1, Z, X)

        def step_L0_moe_attention():
            step = 3
            r = sets[step % 3]
            w = lambda n: W(step, n)
            H, E, DH = 8, 5, 64
            order = ["q", "k", "v"]
            G = NT * 3
            sig = wide[:, 0:320].rearrange("p (t n) -> p t n", t=NT)
            rank = wide[:, 320:640]
            sel = wide[:, 640:960].rearrange("p (t n) -> p t n", t=NT)
            gated = wide[:, 960:1280].rearrange("p (t n) -> p t n", t=NT)
            prods = [[wide[:, 1280 + 512 * e:1792 + 512 * e] for e in range(E)],
                     [EX[:, e, :] for e in range(4)] + [KZ[:, 3, :]]]
            sums = NB
            att = Attention(H, DH, SEQ, keys=lambda c: KT[:, c, :])
            gsel = small[:, 128:448]
            md = gsel.rearrange("p (t n) -> p t n", t=NT)[:, :, 40:80].rearrange("p t (h e) -> p t h e", e=E)
            wsrc = {"q": w("wq"), "k": w("wk"), "v": w("wv")}
            EW = E * P
            mixed = w("wq").rearrange("p (t n) -> p t n", t=NT)
            picked = w("wk").rearrange("p (t n) -> p t n", t=NT)
            mixedT = w("wv").rearrange("p (t n) -> p t n", t=NT)
            with nc.Block() as block:
                @block.sync
                def _(sp):
                    clear_previous(sp, step)
                    load_weights(sp, r, 4)
                    sp.wait_ge(r.loaded, 16)

                @block.gpsimd
                def _(pool):
                    for g in range(G):
                        p = prods[g % 2]
                        for e in range(1, 4):
                            pool.wait_ge(r.part_used, 5 * g + e + 1)
                            if e >= 2:
                                pool.wait_ge(r.sum_step, 3 * g + e - 1)
                            pool.tensor_tensor(p[0], p[0], p[e], ALU.add).then_inc(r.sum_step, 1)
                    pool.wait_ge(r.sum_step, 3 * G)
                    att.pool_clear(pool, r)
                    att.pool(pool, r, [(r.attnT_sb, 2 * NT)])
                    for c in range(1, 4):
                        for t in range(NT if c < 3 else 2):
                            pool.wait_ge(r.hid_dve, NT * c + t + 1)
                            if c >= 2:
                                pool.wait_ge(r.normed, NT * (c - 2) + t + 1)
                            elif t == 0:
                                pool.wait_ge(r.headkeys, H)
                            pool.tensor_tensor(mixed[:, t, :], mixed[:, t, :], picked[:, t, :], ALU.add
                                               ).then_inc(r.normed, 1)
                    pool_power(pool, r, 1)

                def _turn(pe, g):
                    t, m = g // 3, g % 3
                    k_ = 2 * t + m
                    pe.wait_ge(r.ready, g + 1)
                    if k_ >= 1:
                        pe.wait_ge(r.attnT_sb, k_)
                    for c in range(4):
                        ins = pe.transpose(TB[:, c * P:(c + 1) * P], sums[:, m, c * P:(c + 1) * P], ident)
                    ins.then_inc(r.attnT, 1)

                def mix_product(pe, t):
                    pe.wait_ge(r.hid_sb, 2 * t + 2)
                    for e in range(E):
                        ins = pe.matmul(OUT[:, t * P:(t + 1) * P], mixedT[:, t, e * P:(e + 1) * P],
                                        w("wo")[:, e * P:(e + 1) * P], start=(e == 0), stop=(e == E - 1))
                    ins.then_inc(r.out, 1)

                @block.tensor
                def _(pe):
                    pe_xT(pe, r, X)
                    pe.wait_ge(r.xT, 1)
                    for t in range(NT):
                        ins = pe.matmul(OUT[:, t * 80:(t + 1) * 80], XT[:, t * P:(t + 1) * P], w("wsd"),
                                        start=True, stop=True)
                    ins.then_inc(r.gate, 1)
                    n = 0
                    for g in range(G):
                        t, name = g // 3, order[g % 3]
                        ws = wsrc[name].rearrange("p (h e d) -> p h e d", h=H, e=E)
                        for e in range(E):
                            if n >= 4:
                                pe.wait_ge(r.part_used, n - 3)
                            pe.matmul(RING[n % 4][:, :], XT[:, t * P:(t + 1) * P], ws[:, :, e, :],
                                      start=True, stop=True).then_inc(r.part, 1)
                            n += 1
                            if e == 2 and g >= 2 and (g - 2) % 3 < 2:
                                _turn(pe, g - 2)
                    _turn(pe, G - 2)
                    pe.wait_ge(r.attnT_sb, 2 * NT)

                    def turn_back(i):
                        c, at = divmod(i - 2 * att.U - att.LAG - att.U, 2 * att.U)
                        if at != 0 or not 0 <= c < 4:
                            return
                        pe.wait_ge(r.av_sb, c + 1)
                        if c >= 1:
                            pe.wait_ge(r.hid_dve, NT * c)
                        for t in range(NT):
                            ins = pe.transpose(TB[:, t * P:(t + 1) * P], QT[:, c, t * P:(t + 1) * P], ident)
                        ins.then_inc(r.hid, 1)

                    att.pe(pe, r, [(r.ready, G), (r.part_used, 5 * G)], turn_back)
                    turned = [S, PP]
                    for t in range(NT):
                        if t < 2:
                            pe.wait_ge(r.normed, 2 * NT + t + 1)
                        else:
                            pe.wait_ge(r.mixed, t - 2 + 1)
                            pe.wait_ge(r.hid_sb, 2 * (t - 2) + 2)
                        for e in range(E):
                            ins = pe.transpose(turned[e // 4][t % 2][:, e % 4 * P:(e % 4 + 1) * P],
                                               mixed[:, t, e * P:(e + 1) * P], ident)
                        ins.then_inc(r.outproj, 1)
                        if t >= 1:
                            mix_product(pe, t - 1)
                    mix_product(pe, NT - 1)

                @block.scalar
                def _(act):
                    act_xT(act, r)
                    act.wait_ge(r.gate, 1)
                    act.activation(sig, OUT[:, 0:320].rearrange("p (t n) -> p t n", t=NT), ACT.Sigmoid
                                   ).then_inc(r.early, 1)
                    for t in range(NT):
                        for m in range(2):
                            act.wait_ge(r.attnT, 2 * t + m + 1)
                            if t == 0 and m == 0:
                                act.wait_ge(r.gate, 2)
                            dst = (QT if m == 0 else KT)[:, 0:4, t * P:(t + 1) * P]
                            act.activation(dst, TB[:, :].rearrange("p (c d) -> p c d", c=4), ACT.Copy
                                           ).then_inc(r.attnT_sb, 1)
                    att.act(act, r)
                    for t in range(NT):
                        act.wait_ge(r.outproj, t + 1)
                        act.activation(mixedT[:, t, 0:4 * P], S[t % 2][:, :], ACT.Copy).then_inc(r.hid_sb, 1)
                        act.activation(mixedT[:, t, 4 * P:EW], PP[t % 2][:, 0:P], ACT.Copy).then_inc(r.hid_sb, 1)

                @block.vector
                def _(dve):
                    ch = Chain(dve, r.dve_step)
                    dve.wait_ge(r.early, 1)
                    s3 = sig.rearrange("p t (g e) -> p (t g) e", e=E)
                    r3 = rank.rearrange("p (g e) -> p g e", e=E)
                    later = [QT[:, d, 0:64 * (E - d)].rearrange("p (g e) -> p g e", g=64) for d in range(E)]
                    ch.inc(dve.tensor_copy(r3, R_("index5").unsqueeze(1).broadcast_to([P, 64, E])))
                    for d in range(1, E):
                        ch.inc(dve.tensor_tensor(later[d], s3[:, :, d:E], s3[:, :, 0:E - d], ALU.is_gt))
                    ch.join()
                    for d in range(1, E):
                        ch.link(dve.tensor_tensor(r3[:, :, 0:E - d], r3[:, :, 0:E - d], later[d], ALU.add))
                        ch.link(dve.tensor_tensor(r3[:, :, d:E], r3[:, :, d:E], later[d], ALU.subtract))
                    ch.link(dve.tensor_scalar(sel.rearrange("p t n -> p (t n)"), rank, 2.5, None, ALU.is_lt))
                    ch.link(dve.tensor_tensor(gated, sig, sel, ALU.mult))
                    dve.tensor_scalar(gated[:, :, 40:80], gated[:, :, 40:80], DH ** -0.5, None, ALU.mult
                                      ).then_inc(r.gate, 1)
                    ch.link(dve.tensor_copy(gsel.rearrange("p (t n) -> p t n", t=NT), sel))
                    dve.wait_ge(r.gate, 2)

                    def finish(g):
                        t, m = g // 3, g % 3
                        dst = v_rows(P, H, DH, DH, t) if m == 2 else sums[:, m, :].rearrange("p (h d) -> p h d", h=H)
                        if t >= 1 and m < 2:
                            dve.wait_ge(r.attnT, 2 * (t - 1) + m + 1)
                        dve.wait_ge(r.sum_step, 3 * (g + 1))
                        a, b = (prods[g % 2][e].rearrange("p (h d) -> p h d", h=H) for e in (0, 4))
                        dve.tensor_tensor(dst, a, b, ALU.add).then_inc(r.ready, 1)

                    n = 0
                    for g in range(G):
                        t, name = g // 3, order[g % 3]
                        gate = gated[:, t, 40:80] if name == "q" else gated[:, t, 0:40]
                        gate = gate.rearrange("p (h e) -> p h e", e=E)
                        if g >= 2:
                            dve.wait_ge(r.ready, g - 1)
                        for e in range(E):
                            dve.wait_ge(r.part, n + 1)
                            dve.tensor_tensor(prods[g % 2][e].rearrange("p (h d) -> p h d", h=H),
                                              RING[n % 4][:, :].rearrange("p (h d) -> p h d", h=H),
                                              gate[:, :, e].unsqueeze(2).broadcast_to([P, H, DH]),
                                              ALU.mult).then_inc(r.part_used, 1)
                            n += 1
                        if g >= 1:
                            dve.wait_ge(r.part_used, 5 * g)
                            finish(g - 1)
                    dve.wait_ge(r.part_used, 5 * G)
                    finish(G - 1)

                    def pick(c, t):
                        dve.wait_ge(r.hid, c + 1)
                        if c >= 2:
                            dve.wait_ge(r.normed, NT * (c - 2) + t + 1)
                        dst = (mixed if c == 0 else picked)[:, t, :]
                        dve.tensor_tensor(dst.rearrange("p (e j d) -> p e j d", e=E, j=2),
                                          TB[:, t * P:(t + 1) * P].rearrange("p (j d) -> p j d", j=2)
                                          .unsqueeze(1).broadcast_to([P, E, 2, DH]),
                                          md[:, t, 2 * c:2 * c + 2, :].rearrange("p j e -> p e j")
                                          .unsqueeze(3).broadcast_to([P, E, 2, DH]), ALU.mult).then_inc(r.hid_dve, 1)

                    def pick_beside(i):
                        c, at = divmod(i - 3 * att.U - att.LAG - 1, 2 * att.U)
                        if 0 <= c < 3 and at < NT:
                            pick(c, at)

                    att.dve(dve, r, {0: (r.ready, G), 1: (r.ready, G)}, pick_beside)
                    for t in (0, 1, 2, 3):
                        pick(3, t)
                    for t in (2, 3):
                        dve.wait_ge(r.hid_dve, 3 * NT + t + 1)
                        dve.wait_ge(r.normed, NT + t + 1)
                        dve.tensor_tensor(mixed[:, t, :], mixed[:, t, :], picked[:, t, :], ALU.add
                                          ).then_inc(r.mixed, 1)
                    tail(dve, r, ch, (r.out, NT), flatX)

        def step_L1_ssm():
            step = 4
            r = sets[step % 3]
            w = lambda n: W(step, n)
            tab = Table([([(w("win")[:, c * P:(c + 1) * P], XT[:, :])], P, SEQ, "AD"[c], "act" if c == 0 else "col",
                          QT[:, c, :], (ACT.Identity, C("L1a_bin", c), 1.0) if c == 0 else (C("L1a_bin", c),))
                         for c in range(2)])
            states = QT[0:16, 5, :]
            with nc.Block() as block:
                @block.sync
                def _(sp):
                    clear_previous(sp, step)
                    load_weights(sp, r, 5)
                    sp.wait_ge(r.loaded, 16)

                @block.gpsimd
                def _(pool):
                    pool_power(pool, r, 1)
                    pool_power(pool, r, 2)

                @block.tensor
                def _(pe):
                    pe.wait_ge(r.ready, 1)
                    pe_xT(pe, r, XN)
                    pe.wait_ge(r.xT, 1)
                    pe_table(pe, r, tab)
                    pe.wait_ge(r.evac_act, 1)
                    pe.wait_ge(r.evac_dve, 1)
                    for m in range(2):
                        for c in range(2):
                            ins = pe.matmul(S[m][0:16, :], w("ab")[:, 32 * c + 16 * m:32 * c + 16 * m + 16],
                                            QT[:, c, :], start=(c == 0), stop=(c == 1))
                    ins.then_inc(r.hid, 1)
                    pe.wait_ge(r.hid_dve, 1)
                    for c in range(2):
                        ins = pe.matmul(PP[c][:, :], w("c")[0:16, c * P:(c + 1) * P], states, start=True, stop=True)
                    ins.then_inc(r.part, 1)
                    pe.wait_ge(r.part_used, 2)
                    for t in range(NT):
                        for c in range(2):
                            ins = pe.matmul(OUT[:, t * P:(t + 1) * P], QT[:, 2 + c, t * P:(t + 1) * P],
                                            w("wout")[:, c * P:(c + 1) * P], start=(c == 0), stop=(c == 1))
                    ins.then_inc(r.out, 1)

                @block.scalar
                def _(act):
                    act_xT(act, r)
                    evacuate(act, r, tab, "A")
                    act.wait_ge(r.hid, 1)
                    act.activation(QT[0:16, 4, :], S[0][0:16, :], ACT.Sigmoid).then_inc(r.hid_sb, 1)
                    act.wait_ge(r.part, 1)
                    for c in range(2):
                        act.activation(QT[:, 2 + c, :], PP[c][:, :], ACT.Copy).then_inc(r.part_used, 1)

                @block.vector
                def _(dve):
                    ch = Chain(dve, r.dve_step)
                    dve_layer_norm(dve, r, ch, 1, X, XN, R_("L1a_nw"), R_("L1a_nb"))
                    dve.sem_inc(r.ready, 1)
                    evacuate(dve, r, tab, "D")
                    dve.wait_ge(r.hid_sb, 1)
                    dve.wait_ge(r.hid, 1)
                    dve.tensor_tensor_scan(states, QT[0:16, 4, :], S[1][0:16, :], 0.0, ALU.mult, ALU.add
                                           ).then_inc(r.hid_dve, 1)
                    ch.link(dve.scalar_tensor_tensor(Z[:, :, :], X[:, :, :], 2.0, row4(R_("L1a_bout")),
                                                     ALU.mult, ALU.add))
                    tail(dve, r, ch, (r.out, 1), flatZ, 2)
                    ch.link(dve.tensor_copy(flatXR, flatX))

        def step_L1_attention(l, cross):
            step = 6 if cross else 5
            r = sets[step % 3]
            w = lambda n: W(step, n)
            NK = CTX if cross else SEQ
            src = CT if cross else XT
            kc, nch = (CK, 2) if cross else (P, NT)
            gain, bias = w("gain"), w("bias")
            added = None if cross else (lambda h, qt: maskb[:, :])
            order = [("k", c) for c in range(4)] + [("q", c) for c in range(4)]
            att = Attention(8, 64, NK, added=added, keys=lambda c: KT[:, c, 0:NK],
                            queries=lambda c: (r.rotated, 4 + c + 1))
            part = [wide[:, 2048 + SEQ * j:2048 + SEQ * (j + 1)] for j in range(4)]
            dest = lambda m, c: QT[:, c, :] if m == "q" else KT[:, c, 0:NK]

            def rotary(j):
                m, c = order[j]
                n = SEQ if m == "q" else NK
                x = XT[:, :] if m == "q" else src[:, :]
                by = (lambda t: ("times", (0.125, t))) if m == "q" else (lambda t: ("row", (t, ALU.mult)))
                (kind, cos), (_, sin) = by(K("cos")[:, 0:n]), by(K("sin")[:, 0:n])
                return [([(w("w" + m)[:, c * P:(c + 1) * P], x)], P, n, "D", kind, dest(m, c), cos),
                        ([(w("swap" + m)[:, c * P:(c + 1) * P], x)], P, n, "D", kind, part[j % 4][:, 0:n], sin,
                         (r.rotated, j - 3) if j >= 4 else None)]

            values = [([(src[:, c * kc:(c + 1) * kc], w("wv"))], kc, SEQ, "A", "copy",
                       v_rows(kc, 8, 64, 64, c), None) for c in range(nch)]
            keys = [row for j in range(4) for row in rotary(j)]
            queries = [row for j in range(4, 8) for row in rotary(j)]
            if cross:
                tab = Table(keys + values)
                tab2 = Table(queries, tab)
            else:
                tab = Table(keys[0:4])
                tab2 = Table(keys[4:8] + queries + values, tab)

            def rotate(pool, js):
                for j in js:
                    m, c = order[j]
                    d = dest(m, c)
                    pool.wait_ge(r.evac_dve, 2 * j + 2)
                    pool.tensor_tensor(d, d, part[j % 4][:, 0:SEQ if m == "q" else NK], ALU.add
                                       ).then_inc(r.rotated, 1)

            with nc.Block() as block:
                @block.sync
                def _(sp):
                    clear_previous(sp, step)
                    nxt = step + 1
                    sp.dma_start(arenas[nxt % 3][:, 0:WIDTH[nxt]],
                                 io[f"w{nxt}"][bass.ds(l, 1)].rearrange("o p n -> p (o n)")).then_inc(r.loaded, 16)
                    sp.wait_ge(r.loaded, 16)

                @block.gpsimd
                def _(pool):
                    if cross:
                        pool.memset(V[:, 0:1024], 0.0).then_inc(r.ones, 1)
                        pool_power(pool, r, 1, 44)
                        pool.memset(wide[:, 0:4 * SEQ], 0.0).then_inc(r.ones, 1)
                    else:
                        att.pool_clear(pool, r)
                        pool_power(pool, r, 1, 44)
                    rotate(pool, range(4))
                    att.pool(pool, r, [(r.rotated, 4)], range(2), not cross)
                    pool.wait_ge(r.headkeys, 2)
                    rotate(pool, range(4, 8))
                    att.pool(pool, r, [(r.rotated, 8)], range(2, 8), False)

                @block.tensor
                def _(pe):
                    if cross:
                        pe_table(pe, r, tab)
                    pe.wait_ge(r.early, 1)
                    pe_xT(pe, r, XN)
                    pe.wait_ge(r.xT, 1)
                    if not cross:
                        pe_table(pe, r, tab)
                    pe_table(pe, r, tab2)
                    att.pe(pe, r, [(r.evac_act, tab2.a), (r.evac_dve, tab2.d)])
                    att.project(pe, r, w("wo"))

                @block.scalar
                def _(act):
                    act_squares(act, r, X)
                    if cross:
                        act.wait_ge(r.ones, 1)
                        evacuate(act, r, tab, "A")
                    act_xT(act, r)
                    if not cross:
                        evacuate(act, r, tab2, "A")
                    att.act(act, r)

                @block.vector
                def _(dve):
                    ch = Chain(dve, r.dve_step)
                    dve_rms_norm(dve, r, ch, 1, X, XN, gain)
                    dve.sem_inc(r.early, 1)
                    evacuate(dve, r, tab, "D")
                    evacuate(dve, r, tab2, "D")
                    att.dve(dve, r, {0: (r.ones, 2)} if cross else {1: (r.rotated, 8)})
                    ch.link(dve.tensor_tensor(X[:, :, :], X[:, :, :], row4(bias), ALU.add))
                    dve.wait_ge(r.out, 1)
                    ch.link(dve.tensor_tensor(flatX, OUT[:, :], flatX, ALU.add))

        def step_L1_mlp(l):
            step = 7
            r = sets[step % 3]
            w = lambda n: W(step, n)
            gain, bias = w("gain"), w("bias")
            with nc.Block() as block:
                @block.sync
                def _(sp):
                    clear_previous(sp, step)
                    sp.dma_start(arenas[2][:, 0:WIDTH[5]],
                                 io["w5next"][bass.ds(l, 1)].rearrange("o p n -> p (o n)")).then_inc(r.loaded, 16)
                    sp.wait_ge(r.loaded, 16)

                @block.gpsimd
                def _(pool):
                    pool_power(pool, r, 1, 44)

                @block.tensor
                def _(pe):
                    pe.wait_ge(r.early, 1)
                    pe_xT(pe, r, XN)
                    pe.wait_ge(r.xT, 1)
                    mlp_pe(pe, r, w, r.hid_sb)

                @block.scalar
                def _(act):
                    act_squares(act, r, X)
                    act_xT(act, r)
                    for c in range(4):
                        act.wait_ge(r.hid, c + 1)
                        act.activation(QT[:, c, :], RING[c][:, :], ACT.Gelu,
                                       bias=cols[:, bass.ds(cols_at["L1x_fb1"][0] + c + 4 * l, 1)]
                                       ).then_inc(r.hid_sb, 1)

                @block.vector
                def _(dve):
                    ch = Chain(dve, r.dve_step)
                    dve_rms_norm(dve, r, ch, 1, X, XN, gain)
                    dve.sem_inc(r.early, 1)
                    ch.link(dve.tensor_tensor(X[:, :, :], X[:, :, :], row4(bias), ALU.add))
                    dve.wait_ge(r.out, 1)
                    ch.link(dve.tensor_tensor(flatX, OUT[:, :], flatX, ALU.add))

        def step_L1_final():
            step = 8
            r = sets[step % 3]
            with nc.Block() as block:
                @block.sync
                def _(sp):
                    clear_previous(sp, step)
                    load_weights(sp, r, 9)
                    sp.wait_ge(r.loaded, 16)

                @block.gpsimd
                def _(pool):
                    pool_power(pool, r, 1, 44)
                    pool_power(pool, r, 2)

                @block.scalar
                def _(act):
                    act_squares(act, r, X)

                @block.vector
                def _(dve):
                    ch = Chain(dve, r.dve_step)
                    dve_rms_norm(dve, r, ch, 1, X, XN, R_("L1x_gout"))
                    ch.link(dve.tensor_tensor(flatXN, flatXN, flatXR, ALU.add))
                    dve_layer_norm(dve, r, ch, 2, XN, X)

        def step_experts(step, E, swiglu):
            r = sets[step % 3]
            w = lambda n: W(step, n)
            gname = "gate" if swiglu else "wr"
            gates = small[:, 512:512 + NT * E]
            g3 = gates.rearrange("p (t e) -> p t e", e=E)
            acc = XN
            per = 8 if swiglu else 4
            hid = lambda e: QT[:, 4 * (e % 2):4 * (e % 2) + 4, :]
            with nc.Block() as block:
                @block.sync
                def _(sp):
                    clear_previous(sp, step)
                    if step == 9:
                        load_weights(sp, r, 10)
                        sp.wait_ge(r.loaded, 16)

                @block.gpsimd
                def _(pool):
                    pool_power(pool, r, 1)

                @block.tensor
                def _(pe):
                    pe_xT(pe, r, X)
                    pe.wait_ge(r.xT, 1)
                    for t in range(NT):
                        ins = pe.matmul(TB[:, t * E:(t + 1) * E], XT[:, t * P:(t + 1) * P], w(gname),
                                        start=True, stop=True)
                    ins.then_inc(r.gate, 1)
                    n = 0
                    for e in range(E + 1):
                        if e < E:
                            for c in range(4):
                                for m in range(2 if swiglu else 1):
                                    src = w("w3") if m else w("w1")
                                    if n >= 4:
                                        pe.wait_ge(r.part_used, n - 3)
                                    pe.matmul(RING[n % 4][:, :], src[:, e * 512 + c * P:e * 512 + (c + 1) * P],
                                              XT[:, :], start=True, stop=True).then_inc(r.part, 1)
                                    n += 1
                        if e >= 1:
                            f = e - 1
                            pe.wait_ge(r.hid_sb, 4 * e)
                            if f >= 2:
                                pe.wait_ge(r.hid_dve, f - 1)
                            for t in range(NT):
                                for c in range(4):
                                    ins = pe.matmul(S[f % 2][:, t * P:(t + 1) * P],
                                                    hid(f)[:, c, t * P:(t + 1) * P],
                                                    w("w2")[:, f * 512 + c * P:f * 512 + (c + 1) * P],
                                                    start=(c == 0), stop=(c == 3))
                            ins.then_inc(r.out, 1)

                if swiglu:
                    @block.scalar
                    def _(act):
                        act_xT(act, r)
                        act.wait_ge(r.gate, 2)
                        act.activation(small[:, 640:648], small[:, 600:608], ACT.Sigmoid).then_inc(r.act_step, 1)
                        for e in range(E):
                            for c in range(4):
                                n = 8 * e + 2 * c
                                act.wait_ge(r.part, n + 1)
                                if n >= 4:
                                    act.wait_ge(r.hid_sb, n // 2 - 1)
                                act.activation(NB[:, (n // 2) % 2, :], RING[n % 4][:, :], ACT.Silu
                                               ).then_inc(r.ready, 1)
                else:
                    @block.scalar
                    def _(act):
                        act_xT(act, r)
                        for e in range(E):
                            for c in range(4):
                                n = 4 * e + c
                                act.wait_ge(r.part, n + 1)
                                if e >= 2 and c == 0:
                                    act.wait_ge(r.out, e - 1)
                                act.activation(hid(e)[:, c, :], RING[n % 4][:, :], ACT.Relu,
                                               bias=C("L1f_be1", n)).then_inc(r.part_used, 1)
                                act.wait_ge(r.part_used, n + 1)
                                act.sem_inc(r.hid_sb, 1)

                @block.vector
                def _(dve):
                    ch = Chain(dve, r.dve_step)
                    lg, rank = small[:, 544:544 + NT * E], small[:, 608:608 + 32]
                    l3, r3 = lg.rearrange("p (t e) -> p t e", e=E), rank[:, 0:NT * E].rearrange("p (t e) -> p t e", e=E)
                    if swiglu:
                        lg = small[:, 704:704 + NT * E]
                        l3 = lg.rearrange("p (t e) -> p t e", e=E)
                        rank = small[:, 740:740 + NT * E]
                        r3 = rank.rearrange("p (t e) -> p t e", e=E)
                    t1, t2 = wide[:, 0:512], wide[:, 512:1024]
                    dve.wait_ge(r.gate, 1)
                    if swiglu:
                        ch.link(dve.tensor_copy(lg, TB[:, 0:NT * E]))
                    else:
                        ch.link(dve.tensor_tensor(l3, TB[:, 0:NT * E].rearrange("p (t e) -> p t e", e=E),
                                                  R_("L1f_br").unsqueeze(1).broadcast_to([P, NT, E]), ALU.add))
                    dve_ranks(dve, ch, l3, NT, E, R_("tri8" if swiglu else "tri4"), r3, t1, t2)
                    if swiglu:
                        first, second = small[:, 780:812], small[:, 820:852]
                        ch.inc(dve.tensor_scalar(first, rank, 0.0, None, ALU.is_equal))
                        ch.link(dve.tensor_scalar(second, rank, 1.0, None, ALU.is_equal))
                        fl, sl = wide[:, 1024:1056], wide[:, 1056:1088]
                        ch.inc(dve.tensor_tensor(fl, first, lg, ALU.mult))
                        ch.link(dve.tensor_tensor(sl, second, lg, ALU.mult))
                        v12 = wide[:, 1088:1096]
                        ch.inc(dve.tensor_reduce(v12[:, 0:4], fl.rearrange("p (t e) -> p t e", e=E), AX.X, ALU.add))
                        ch.link(dve.tensor_reduce(v12[:, 4:8], sl.rearrange("p (t e) -> p t e", e=E), AX.X, ALU.add))
                        ch.inc(dve.tensor_tensor(small[:, 600:604], v12[:, 0:4], v12[:, 4:8], ALU.subtract))
                        dve.tensor_tensor(small[:, 604:608], v12[:, 4:8], v12[:, 0:4], ALU.subtract).then_inc(r.gate, 1)
                        dve.wait_ge(r.act_step, 1)
                        ch.inc(dve.tensor_tensor(first.rearrange("p (t e) -> p t e", e=E),
                                                 first.rearrange("p (t e) -> p t e", e=E),
                                                 small[:, 640:644].unsqueeze(2).broadcast_to([P, NT, E]), ALU.mult))
                        ch.link(dve.tensor_tensor(second.rearrange("p (t e) -> p t e", e=E),
                                                  second.rearrange("p (t e) -> p t e", e=E),
                                                  small[:, 644:648].unsqueeze(2).broadcast_to([P, NT, E]), ALU.mult))
                        ch.link(dve.tensor_tensor(gates, first, second, ALU.add))
                    else:
                        ch.link(dve.tensor_scalar(gates, rank[:, 0:NT * E], 0.0, None, ALU.is_equal))
                    ch.link(dve.tensor_copy(flatZ, flatX))
                    for e in range(E + 1):
                        if swiglu and e < E:
                            for c in range(4):
                                n = 8 * e + 2 * c
                                if e >= 2 and c == 0:
                                    dve.wait_ge(r.out, e - 1)
                                dve.wait_ge(r.ready, n // 2 + 1)
                                dve.wait_ge(r.part, n + 2)
                                dve.tensor_tensor(hid(e)[:, c, :], RING[(n + 1) % 4][:, :], NB[:, (n // 2) % 2, :],
                                                  ALU.mult).then_inc(r.hid_sb, 1)
                                dve.wait_ge(r.hid_sb, n // 2 + 1)
                                dve.sem_inc(r.part_used, 2)
                        if e < 1:
                            continue
                        f = e - 1
                        dve.wait_ge(r.out, e)
                        src = S[f % 2]
                        if not swiglu:
                            tmp = wide[:, 2048:2560]
                            ch.link(dve.tensor_tensor(tiles(tmp), tiles(src[:, :]),
                                                      row4(R_("L1f_be2")[:, f * P:(f + 1) * P]), ALU.add))
                            src = tmp
                        for t in range(NT):
                            ins = dve.scalar_tensor_tensor(Z[:, t, :], src[:, t * P:(t + 1) * P],
                                                           g3[:, t, f:f + 1], Z[:, t, :], ALU.mult, ALU.add)
                            ch.inc(ins)
                        ch.join()
                        dve.sem_inc(r.hid_dve, 1)
                    dve_layer_norm(dve, r, ch, 1, Z, X)

        def step_L2_attention():
            step = 10
            r = sets[step % 3]
            w = lambda n: W(step, n)
            att = Attention(1, P, SEQ, keys=lambda c: KT[:, 0, :])
            tab = Table([([(w("wq"), XT[:, :])], P, SEQ, "A", "act", QT[:, 1, :], (ACT.Identity, C("L2a_bq"), 1.0)),
                         ([(w("wk"), XT[:, :])], P, SEQ, "D", "col", KT[:, 1, :], (C("L2a_bk"),))]
                        + [([(XT[:, t * P:(t + 1) * P], w("wv"))], P, P, "D", "row", V[:, t * P:(t + 1) * P],
                            (R_("L2a_bv"), ALU.add)) for t in range(NT)])
            tab2 = Table([([(K("pair"), QT[:, 1, :])], P, SEQ, "D", "row", QT[:, 2, :], (w("sincos"), ALU.mult)),
                          ([(K("pair"), KT[:, 1, :])], P, SEQ, "D", "row", KT[:, 0, :], (w("sincos"), ALU.mult))], tab)
            with nc.Block() as block:
                @block.sync
                def _(sp):
                    clear_previous(sp, step)
                    load_weights(sp, r, 11)
                    sp.wait_ge(r.loaded, 16)

                @block.gpsimd
                def _(pool):
                    pool.wait_ge(r.evac_dve, tab2.d)
                    pool.tensor_scalar(QT[:, 0, :], QT[:, 2, :], 0.125, None, ALU.mult).then_inc(r.ready, 1)
                    pool_power(pool, r, 1)

                @block.tensor
                def _(pe):
                    pe_xT(pe, r, X)
                    pe.wait_ge(r.xT, 1)
                    pe_table(pe, r, tab)
                    pe.wait_ge(r.evac_act, tab.a)
                    pe.wait_ge(r.evac_dve, tab.d)
                    pe_table(pe, r, tab2)
                    pe.wait_ge(r.evac_dve, tab2.d)
                    pe.wait_ge(r.ready, 1)
                    att.pe(pe, r)
                    pe.wait_ge(r.av_sb, 1)
                    for t in range(NT):
                        ins = pe.transpose(OUT[:, t * P:(t + 1) * P], QT[:, 0, t * P:(t + 1) * P], ident)
                    ins.then_inc(r.out, 1)

                @block.scalar
                def _(act):
                    act_xT(act, r)
                    evacuate(act, r, tab, "A")
                    att.act(act, r)

                @block.vector
                def _(dve):
                    ch = Chain(dve, r.dve_step)
                    evacuate(dve, r, tab, "D")
                    evacuate(dve, r, tab2, "D")
                    att.dve(dve, r)
                    tail(dve, r, ch, (r.out, 1), flatX)

        def step_L2_sigmoid_attention():
            step = 11
            r = sets[step % 3]
            w = lambda n: W(step, n)
            tab = Table([([(w("wq"), XT[:, :])], 32, SEQ, "A", "act", QT[0:32, 0, :],
                          (ACT.Identity, C("L2x_bq", parts=32), 1.0)),
                         ([(w("wk"), CT[:, :])], 32, CTX, "D", "col", KT[0:32, 0, 0:CTX], (C("L2x_bk", parts=32),))]
                        + [([(CT[:, c * CK:(c + 1) * CK], w("wv"))], CK, P, "D", "row", V[0:CK, c * P:(c + 1) * P],
                            (R_("L2x_bv", CK), ALU.add)) for c in range(2)])
            with nc.Block() as block:
                @block.sync
                def _(sp):
                    clear_previous(sp, step)
                    load_weights(sp, r, 12)
                    sp.wait_ge(r.loaded, 16)

                @block.gpsimd
                def _(pool):
                    pool_power(pool, r, 1)

                @block.tensor
                def _(pe):
                    pe_xT(pe, r, X)
                    pe.wait_ge(r.xT, 1)
                    pe_table(pe, r, tab)
                    pe.wait_ge(r.evac_act, tab.a)
                    pe.wait_ge(r.evac_dve, tab.d)
                    for c in range(2):
                        ins = pe.matmul(S[c][0:CK, :], KT[0:32, 0, c * CK:(c + 1) * CK], QT[0:32, 0, :],
                                        start=True, stop=True)
                        ins.then_inc(r.scores, 1)
                    pe.wait_ge(r.exped, 2)
                    for t in range(NT):
                        for c in range(2):
                            ins = pe.matmul(OUT[:, t * P:(t + 1) * P], EX[0:CK, c, t * P:(t + 1) * P],
                                            V[0:CK, c * P:(c + 1) * P], start=(c == 0), stop=(c == 1))
                    ins.then_inc(r.out, 1)

                @block.scalar
                def _(act):
                    act_xT(act, r)
                    evacuate(act, r, tab, "A")
                    for c in range(2):
                        act.wait_ge(r.scores, c + 1)
                        act.activation(EX[0:CK, c, :], S[c][0:CK, :], ACT.Sigmoid, scale=32.0 ** -0.5).then_inc(r.exped, 1)

                @block.vector
                def _(dve):
                    ch = Chain(dve, r.dve_step)
                    evacuate(dve, r, tab, "D")
                    tail(dve, r, ch, (r.out, 1), flatX)

        def step_L2_lora_experts():
            step = 12
            r = sets[step % 3]
            w = lambda n: W(step, n)
            E = 8
            hsum = wide[:, 0:2048].rearrange("p (t f) -> p t f", t=NT)
            part = [wide[:, 2048 + 512 * i:2560 + 512 * i] for i in range(2)]
            gates = small[:, 512:544]
            g3 = gates.rearrange("p (t e) -> p t e", e=E)
            tab = Table([([(w("loraA")[:, c * P:(c + 1) * P], XT[:, :])], P, SEQ, "D", "col", QT[:, c, :],
                          (C("L2f_one"),)) for c in range(2)])
            with nc.Block() as block:
                @block.sync
                def _(sp):
                    clear_previous(sp, step)
                    load_weights(sp, r, 13)
                    sp.wait_ge(r.loaded, 16)

                @block.gpsimd
                def _(pool):
                    for n in range(NT * E):
                        t, e = n % NT, n // NT
                        pool.wait_ge(r.hid_sb, n + 1)
                        if e == 0:
                            pool.tensor_copy(hsum[:, t, :], part[n % 2]).then_inc(r.ready, 1)
                        else:
                            pool.wait_ge(r.ready, n - NT + 1)
                            pool.tensor_tensor(hsum[:, t, :], hsum[:, t, :], part[n % 2], ALU.add).then_inc(r.ready, 1)
                    pool_power(pool, r, 1)

                @block.tensor
                def _(pe):
                    pe_xT(pe, r, X)
                    pe.wait_ge(r.xT, 1)
                    for t in range(NT):
                        ins = pe.matmul(TB[:, t * E:(t + 1) * E], XT[:, t * P:(t + 1) * P], w("gate"),
                                        start=True, stop=True)
                    ins.then_inc(r.gate, 1)
                    pe_table(pe, r, tab)
                    pe.wait_ge(r.evac_dve, tab.d)
                    for n in range(NT * E):
                        t, e = n % NT, n // NT
                        if n >= 4:
                            pe.wait_ge(r.hid_sb, n - 3)
                        c = e // 4
                        pe.matmul(RING[n % 4][:, :], XT[:, t * P:(t + 1) * P], w("wi"), start=True, stop=False)
                        pe.matmul(RING[n % 4][:, :], QT[:, c, t * P:(t + 1) * P],
                                  w("loraB")[:, e * 512:(e + 1) * 512], start=False, stop=True).then_inc(r.hid, 1)
                    pe.wait_ge(r.gate, 3)
                    for t in range(NT):
                        pe.wait_ge(r.ready, NT * (E - 1) + t + 1)
                        if t >= 2:
                            pe.wait_ge(r.attnT_sb, t - 1)
                        for c in range(4):
                            ins = pe.transpose(S[t % 2][:, c * P:(c + 1) * P], hsum[:, t, c * P:(c + 1) * P], ident)
                        ins.then_inc(r.attnT, 1)
                        pe.wait_ge(r.attnT_sb, t + 1)
                        for c in range(4):
                            ins = pe.matmul(OUT[:, t * P:(t + 1) * P], KT[:, t, c * P:(c + 1) * P],
                                            w("wo")[:, c * P:(c + 1) * P], start=(c == 0), stop=(c == 3))
                    ins.then_inc(r.out, 1)

                @block.scalar
                def _(act):
                    act_xT(act, r)
                    act.wait_ge(r.gate, 2)
                    act.activation(small[:, 576:608], small[:, 544:576], ACT.Exp).then_inc(r.act_step, 1)
                    act.wait_ge(r.gate, 3)
                    for n in range(NT * E):
                        t, e = n % NT, n // NT
                        act.wait_ge(r.hid, n + 1)
                        if n >= 2:
                            act.wait_ge(r.ready, n - 1)
                        act.activation(part[n % 2], RING[n % 4][:, :], ACT.Relu, scale=g3[:, t, e:e + 1]
                                       ).then_inc(r.hid_sb, 1)
                    for t in range(NT):
                        act.wait_ge(r.attnT, t + 1)
                        act.activation(KT[:, t, :], S[t % 2][:, :], ACT.Copy).then_inc(r.attnT_sb, 1)

                @block.vector
                def _(dve):
                    ch = Chain(dve, r.dve_step)
                    lg = small[:, 544:576]
                    l3 = lg.rearrange("p (t e) -> p t e", e=E)
                    mx, ex, rank, sel = small[:, 608:612], small[:, 576:608], small[:, 640:672], small[:, 672:704]
                    e3, r3 = (z.rearrange("p (t e) -> p t e", e=E) for z in (ex, rank))
                    s3 = sel.rearrange("p (t e) -> p t e", e=E)
                    dve.wait_ge(r.gate, 1)
                    ch.link(dve.tensor_tensor(l3, TB[:, 0:32].rearrange("p (t e) -> p t e", e=E),
                                              R_("L2f_gb").unsqueeze(1).broadcast_to([P, NT, E]), ALU.add))
                    ch.link(dve.tensor_reduce(mx, l3, AX.X, ALU.max))
                    dve.tensor_tensor(l3, l3, mx.unsqueeze(2).broadcast_to([P, NT, E]), ALU.subtract).then_inc(r.gate, 1)
                    evacuate(dve, r, tab, "D")
                    dve.wait_ge(r.act_step, 1)
                    ch.link(dve.tensor_reduce(small[:, 612:616], e3, AX.X, ALU.add))
                    ch.link(dve.reciprocal(small[:, 616:620], small[:, 612:616]))
                    ch.link(dve.tensor_tensor(e3, e3, small[:, 616:620].unsqueeze(2).broadcast_to([P, NT, E]), ALU.mult))
                    dve_ranks(dve, ch, e3, NT, E, R_("tri8"), r3, NB[:, 0, :], NB[:, 1, :])
                    ch.link(dve.tensor_scalar(sel, rank, 1.5, None, ALU.is_lt))
                    ch.link(dve.tensor_tensor(ex, ex, sel, ALU.mult))
                    ch.link(dve.tensor_reduce(small[:, 620:624], e3, AX.X, ALU.add))
                    dve.tensor_tensor(g3, s3, small[:, 620:624].unsqueeze(2).broadcast_to([P, NT, E]), ALU.mult
                                      ).then_inc(r.gate, 1)
                    dve.wait_ge(r.gate, 3)
                    ch.link(dve.tensor_reduce(small[:, 624:628], g3, AX.X, ALU.add))
                    for t in range(NT):
                        ch.inc(dve.scalar_tensor_tensor(Z[:, t, :], R_("L2f_bo"), small[:, 624 + t:625 + t],
                                                        X[:, t, :], ALU.mult, ALU.add))
                    ch.join()
                    tail(dve, r, ch, (r.out, 1), flatZ)

        def step_L3_attention():
            step = 13
            r = sets[step % 3]
            w = lambda n: W(step, n)
            att = Attention(16, 8, SEQ, causal=True, keys=lambda c: KT[:, c, :],
                            added=lambda h, qt: relbias[:, h, SEQ - P * (qt + 1):SEQ])
            rowsA = [([(w("wq")[:, c * P:(c + 1) * P], XT[:, :])], P, SEQ, "A", "act", QT[:, c, :],
                      (ACT.Identity, scaled[:, 4 + c:5 + c], RSQRT8)) for c in range(4)]
            rowsA += [([(w("wk")[:, c * P:(c + 1) * P], XT[:, :])], P, SEQ, "D", "col", KT[:, c, :],
                       (C("L3a_bk", c),)) for c in range(4)]
            vrow = R_("L3a_bv").rearrange("p (h d) -> p h d", h=16)
            rowsA += [([(XT[:, t * P:(t + 1) * P], w("wv"))], P, P, "D", "row", v_rows(P, 16, 32, 8, t),
                       (vrow, ALU.add)) for t in range(NT)]
            tab = Table(rowsA)
            with nc.Block() as block:
                @block.sync
                def _(sp):
                    clear_previous(sp, step)
                    load_weights(sp, r, 14)
                    sp.wait_ge(r.loaded, 16)

                @block.gpsimd
                def _(pool):
                    pool.memset(V[:, 0:2048], 0.0).then_inc(r.ones, 1)
                    att.pool_clear(pool, r)
                    att.pool(pool, r, [(r.evac_dve, tab.d)])
                    pool_power(pool, r, 1)

                @block.tensor
                def _(pe):
                    pe_xT(pe, r, X)
                    pe.wait_ge(r.xT, 1)
                    pe_table(pe, r, tab)
                    pe.wait_ge(r.evac_act, tab.a)
                    pe.wait_ge(r.evac_dve, tab.d)
                    att.pe(pe, r)
                    att.project(pe, r, w("wo"))

                @block.scalar
                def _(act):
                    act_xT(act, r)
                    evacuate(act, r, tab, "A")
                    att.act(act, r)

                @block.vector
                def _(dve):
                    ch = Chain(dve, r.dve_step)
                    dve.wait_ge(r.ones, 1)
                    evacuate(dve, r, tab, "D")
                    att.dve(dve, r)
                    ch.link(dve.tensor_tensor(Z[:, :, :], X[:, :, :], row4(R_("L3a_bo")), ALU.add))
                    tail(dve, r, ch, (r.out, 1), flatZ)

        def step_L3_cross():
            step = 14
            r = sets[step % 3]
            w = lambda n: W(step, n)
            keys = KT[:, :, :].rearrange("p c t -> p (c t)")[:, 0:8 * CTX].rearrange("p (c t) -> p c t", c=8)
            att = Attention(16, 64, CTX, keys=lambda c: keys[:, c, :],
                            added=lambda h, qt: padb[:, min(qt, 2), :])
            rowsA = [([(w("wq")[:, c * P:(c + 1) * P], XT[:, :])], P, SEQ, "A", "act", QT[:, c, :],
                      (ACT.Identity, scaled[:, 8 + c:9 + c], 0.125)) for c in range(8)]
            rowsA += [([(w("wk")[:, c * P:(c + 1) * P], CT[:, :])], P, CTX, "D", "col", keys[:, c, :],
                       (C("L3x_bk", c),)) for c in range(8)]
            for c in range(2):
                for m in range(2):
                    rowsA.append(([(CT[:, c * CK:(c + 1) * CK], w("wv")[:, m * 512:(m + 1) * 512])], CK, SEQ, "D", "row",
                                  v_rows(CK, 16, 64, 64, c)[:, 8 * m:8 * m + 8, :],
                                  (KZ[0:CK, 2 + m, :].rearrange("p (h d) -> p h d", h=8),
                                   ALU.add)))
            tab = Table(rowsA)
            with nc.Block() as block:
                @block.sync
                def _(sp):
                    clear_previous(sp, step)
                    sp.dma_start(KZ[:, 2:4, :].rearrange("p a t -> p (a t)"),
                                 io["L3x_bv"][0:1, :].broadcast_to([P, 1024])).then_inc(r.early, 16)
                    load_weights(sp, r, 15)
                    sp.wait_ge(r.loaded, 16)

                @block.gpsimd
                def _(pool):
                    pool_clear_context(pool, r, 2048)
                    att.pool_clear(pool, r)
                    att.pool(pool, r, [(r.evac_dve, tab.d)])
                    pool_power(pool, r, 1)

                @block.tensor
                def _(pe):
                    pe_xT(pe, r, X)
                    pe.wait_ge(r.xT, 1)
                    pe_table(pe, r, tab)
                    pe.wait_ge(r.evac_act, tab.a)
                    pe.wait_ge(r.evac_dve, tab.d)
                    att.pe(pe, r)
                    att.project(pe, r, w("wo"))

                @block.scalar
                def _(act):
                    act_xT(act, r)
                    evacuate(act, r, tab, "A")
                    att.act(act, r)

                @block.vector
                def _(dve):
                    ch = Chain(dve, r.dve_step)
                    dve.wait_ge(r.ones, 2)
                    dve.wait_ge(r.early, 16)
                    evacuate(dve, r, tab, "D")
                    att.dve(dve, r)
                    ch.link(dve.tensor_tensor(Z[:, :, :], X[:, :, :], row4(R_("L3x_bo")), ALU.add))
                    tail(dve, r, ch, (r.out, 1), flatZ)

        def step_store(b):
            step = 16
            r = sets[step % 3]
            with nc.Block() as block:
                @block.sync
                def _(sp):
                    clear_previous(sp, step)
                    sp.dma_start(io["out"][bass.ds(b, 1)].rearrange("o (t p) d -> p (o t) d", p=P), X[:, :, :]
                                 ).then_inc(r.loaded, 16)
                    load_weights(sp, r, 0)
                    sp.wait_ge(r.loaded, 32)

        with nc.Fori(0, NBATCH) as b:
            step_load(b)
            step_L0_linear_attention()
            step_L0_mlp()
            step_L0_cross()
            step_L0_moe_attention()
            step_L1_ssm()
            with nc.Fori(0, LAYERS) as l:
                step_L1_attention(l, False)
                step_L1_attention(l, True)
                step_L1_mlp(l)
            step_L1_final()
            step_experts(9, 4, False)
            step_L2_attention()
            step_L2_sigmoid_attention()
            step_L2_lora_experts()
            step_L3_attention()
            step_L3_cross()
            step_experts(15, 8, True)
            step_store(b)



def pack(np, parts, widths):
    out = np.zeros((P, sum(widths)), np.float32)
    at = 0
    for a, n in zip(parts, widths):
        assert a.shape[1] == n, (a.shape, n)
        out[:a.shape[0], at:at + n] = a
        at += n
    return out


def chunked(np, a):
    n = -(-a.shape[0] // P)
    full = np.zeros((n * P, a.shape[1]), a.dtype)
    full[:a.shape[0]] = a
    return full.reshape(n, P, -1).transpose(1, 0, 2).reshape(P, -1)


def pad_heads(np, a, real, padded):
    lead = a.shape[:-1]
    out = np.zeros(lead + (a.shape[-1] // real, padded), a.dtype)
    out[..., :real] = a.reshape(lead + (-1, real))
    return out.reshape(lead + (-1,))


def swapped(np, a):
    a = a.reshape(P, 8, 64)
    return np.concatenate([a[:, :, 16:32], a[:, :, 0:16], a[:, :, 32:]], 2).reshape(P, 512)


def columns(np, v):
    return chunked(np, v.reshape(-1, 1))


def layout(np, i):
    out = {"x": i["x"], "ctxT": i["ctx_1024"].transpose(0, 2, 1), "mask1": i["mask_BxS_bf1"],
           "mask2": i["mask_BxS2_if1"]}
    proj = np.zeros((P, 512), np.float32)
    for h in range(16):
        proj[8 * h:8 * h + 8, 32 * h:32 * h + 32] = i["L0_attn_proj"][h]
    lb = np.zeros((P, 4096), np.float32)
    for e in range(8):
        at = 32 * (e % 4)
        lb[at:at + 16, 512 * e:512 * e + 512] = i["L2_ffn_lora_B"][e].T
        lb[at + 16, 512 * e:512 * e + 512] = i["L2_ffn_bi"]
    kv = i["L0_ffn_Wkv"]
    experts = lambda a: a.transpose(1, 0, 2).reshape(P, -1)
    second = lambda a: np.concatenate([chunked(np, m) for m in a], 1)
    pos = np.arange(SEQ, dtype=np.float32)
    inv2 = (10000.0 ** (np.arange(0, 64, 2, dtype=np.float32) / np.float32(64))).astype(np.float32)
    rad = pos[None, :] / inv2[:, None]
    sc = np.stack([np.sin(rad), np.cos(rad)], 1).reshape(64, SEQ)
    w = {
        0: [i["L0_attn_w_qkv"].T, proj, i["L0_attn_w_out"].T],
        1: [i["L0_attn_w1"].T, chunked(np, i["L0_attn_w2"].T)],
        2: [pad_heads(np, i["L0_xattn_Wq"], 8, 32), pad_heads(np, i["L0_xattn_Wk"], 8, 32), i["L0_xattn_Wv"],
            chunked(np, pad_heads(np, i["L0_xattn_Wo"].T, 8, 32).T)],
        3: [i["L0_ffn_Wq"], kv[:, :2560], kv[:, 2560:], np.concatenate([i["L0_ffn_Ws"], i["L0_ffn_Wd"]], 1),
            np.concatenate([i["L0_ffn_Wo"], i["L0_ffn_Wo"]], 0)],
        4: [i["L1_attn_W_in"].T, chunked(np, np.concatenate([i["L1_attn_A"], i["L1_attn_B_ssm"]], 1)),
            i["L1_attn_C_ssm"].T, chunked(np, i["L1_attn_W_out"].T)],
        9: [i["L1_ffn_Wr"], experts(i["L1_ffn_We1"]), second(i["L1_ffn_We2"])],
        10: [i["L2_attn_Wq"].T, i["L2_attn_Wk"].T, i["L2_attn_Wv"].T, np.repeat(sc, 2, 0)],
        11: [i["L2_xattn_Wq"].T, i["L2_xattn_Wk"].T, i["L2_xattn_Wv"].T],
        12: [i["L2_ffn_gate_w"].T, i["L2_ffn_wi"].T,
             pad_heads(np, i["L2_ffn_lora_A"].reshape(P, P).T, 16, 32), lb, chunked(np, i["L2_ffn_wo"].T)],
        13: [pad_heads(np, i["L3_attn_WQ"].T, 8, 32), pad_heads(np, i["L3_attn_WK"].T, 8, 32), i["L3_attn_WV"].T,
             chunked(np, pad_heads(np, i["L3_attn_WO"], 8, 32).T)],
        14: [i["L3_xattn_Wq"], i["L3_xattn_Wk"], i["L3_xattn_Wv"], chunked(np, i["L3_xattn_Wo"])],
        15: [i["L3_ffn_gate_w"].T, experts(i["L3_ffn_w1"].transpose(0, 2, 1)),
             experts(i["L3_ffn_w3"].transpose(0, 2, 1)), second(i["L3_ffn_w2"].transpose(0, 2, 1))],
    }
    for k, parts in w.items():
        out[f"w{k}"] = pack(np, parts, [n for _, n in WEIGHTS[k]])
    for k, c in ((5, "s"), (6, "c")):
        spread = lambda v: np.broadcast_to(v, (P, P))
        layers = [pack(np, [i[f"L1_xattn_{c}Wq"][l], i[f"L1_xattn_{c}Wk"][l],
                            swapped(np, i[f"L1_xattn_{c}Wq"][l]), swapped(np, i[f"L1_xattn_{c}Wk"][l]),
                            i[f"L1_xattn_{c}Wv"][l],
                            chunked(np, i[f"L1_xattn_{c}Wo"][l]),
                            spread(i[f"L1_xattn_{c}g"][l]), spread(i[f"L1_xattn_{c}bo"][l])], [n for _, n in WEIGHTS[k]]) for l in range(LAYERS)]
        out[f"w{k}"] = np.stack(layers)
    out["w7"] = np.stack([pack(np, [i["L1_xattn_fW1"][l], chunked(np, i["L1_xattn_fW2"][l]),
                                    spread(i["L1_xattn_fg"][l]), spread(i["L1_xattn_fb2"][l])], [512, 512, 128, 128])
                          for l in range(LAYERS)])
    out["w5next"] = out["w5"][[1, 2, 3, 0]]
    out["w5"] = out["w5"][0]
    one = np.zeros((P, 1), np.float32)
    one[16::32] = 1
    block4 = np.zeros((P, 4), np.float32)
    for h in range(4):
        block4[32 * h:32 * h + 32, h] = 1
    padcols = lambda v: columns(np, pad_heads(np, v, 8, 32))
    c = {"L0a_b1": columns(np, i["L0_attn_b1"]), "L0x_bq": padcols(i["L0_xattn_bq"]),
         "L0x_bk": padcols(i["L0_xattn_bk"]), "L1a_bin": columns(np, i["L1_attn_b_in"]),
         "L1x_fb1": columns(np, i["L1_xattn_fb1"].reshape(-1)), "L1f_be1": columns(np, i["L1_ffn_be1"].reshape(-1)),
         "L2a_bq": columns(np, i["L2_attn_bq"]), "L2a_bk": columns(np, i["L2_attn_bk"]),
         "L2x_bq": columns(np, i["L2_xattn_bq"]), "L2x_bk": columns(np, i["L2_xattn_bk"]), "L2f_one": one,
         "L3a_bq": padcols(i["L3_attn_bQ"]), "L3a_bk": padcols(i["L3_attn_bK"]),
         "L3x_bq": columns(np, i["L3_xattn_bq"]), "L3x_bk": columns(np, i["L3_xattn_bk"]), "block4": block4}
    out["cols"] = pack(np, [c[n] for n, _ in COLS], [m for _, m in COLS])
    tri = lambda n: np.tril(np.ones((n, n), np.float32), -1)
    rw = {"L0a_bout": i["L0_attn_b_out"], "L0a_gamma": i["L0_attn_gamma"], "L0a_beta": i["L0_attn_beta"],
          "L0a_b2": i["L0_attn_b2"], "L0x_bv": i["L0_xattn_bv"], "L0x_bo": i["L0_xattn_bo"],
          "L1a_nw": i["L1_attn_norm_w"], "L1a_nb": i["L1_attn_norm_b"], "L1a_bout": i["L1_attn_b_out"],
          "L1x_gout": i["L1_xattn_g_out"], "L1f_be2": i["L1_ffn_be2"], "L1f_br": i["L1_ffn_br"],
          "L2a_bv": i["L2_attn_bv"], "L2x_bv": i["L2_xattn_bv"], "L2f_bo": i["L2_ffn_bo"],
          "L2f_gb": i["L2_ffn_gate_b"], "L3a_bv": i["L3_attn_bV"], "L3a_bo": i["L3_attn_bO"],
          "L3x_bo": i["L3_xattn_bo"], "index5": np.arange(5, dtype=np.float32), "tri4": tri(4), "tri8": tri(8)}
    out["L3x_bv"] = i["L3_xattn_bv"].reshape(1, -1)
    out["rows"] = np.concatenate([rw[n].reshape(1, -1) for n, _ in ROWS], 1)
    ident = np.eye(P, dtype=np.float32)
    pair = np.eye(P, dtype=np.float32)
    for m in range(0, P, 2):
        pair[m + 1, m] = -1
        pair[m, m + 1] = 1
    inv = (1.0 / 10000.0 ** (np.arange(0, 32, 2, dtype=np.float32) / np.float32(32))).astype(np.float32)
    fr = np.concatenate([inv, inv])[:, None] * pos[None, :]
    cos, sin = np.ones((P, SEQ), np.float32), np.zeros((P, SEQ), np.float32)
    for h in (0, 64):
        cos[h:h + 32], sin[h:h + 32] = np.cos(fr), np.sin(fr)
        sin[h:h + 16] *= -1
    out["consts"] = pack(np, [ident, pair, cos, sin], [m for _, m in CONSTS])
    table = i["L3_attn_rel_pos_table"]
    at = np.arange(P)[:, None] - np.arange(SEQ)[None, :] + (SEQ - P) + len(table) // 2
    out["reltab"] = table[np.clip(at, 0, len(table) - 1)].transpose(0, 2, 1).reshape(P, -1)
    return {k: np.ascontiguousarray(v) for k, v in out.items()}


def kernel(**inputs):
    import numpy as np
    import concourse.bacc as bacc
    from concourse.bass_utils import run_bass_kernel_spmd

    nc = bacc.Bacc("TRN2", target_bir_lowering=False, num_devices=1)
    arrays, io = {}, {}
    for name, a in layout(np, {k: np.asarray(v) for k, v in inputs.items()}).items():
        arrays[f"in_{name}_dram"] = a
        io[name] = nc.dram_tensor(f"in_{name}_dram", a.shape, mybir.dt.from_np(a.dtype), kind="ExternalInput").ap()
    io["out"] = nc.dram_tensor("out_0_dram", (NBATCH, SEQ, P), F32, kind="ExternalOutput").ap()
    build(nc, io)
    r = run_bass_kernel_spmd(nc, [arrays], core_ids=[0])
    return r.results[0]["out_0_dram"]
```
